# Optimizing a Trainium2 kernel written in Bass

```python
import numpy as np
import jax
import jax.numpy as jnp

def _softmax(x, axis=-1):
    return jax.nn.softmax(x, axis=axis)

def _gelu(x):
    return jax.nn.gelu(x, approximate=True)

def _silu(x):
    return jax.nn.silu(x)

def _sigmoid(x):
    return jax.nn.sigmoid(x)

def _layernorm(x, axis=-1, eps=1e-05):
    m = jnp.mean(x, axis=axis, keepdims=True)
    v = jnp.var(x, axis=axis, keepdims=True)
    return (x - m) / jnp.sqrt(v + eps)

def _scatter_add(tgt, idx, src, axis=0):
    return tgt.at[idx].add(src)

def _segment_sum(src, seg, n):
    return jax.ops.segment_sum(src, seg, n)
kernel_name = 'mk_lm_tower_d2_tok_ids4096_r4_d88e54'

def setup_inputs(seed: int=0):
    np.random.seed(seed)
    _w = jnp.asarray

    def _rec_inputs():
        import jax
        import jax.numpy as jnp
        _rk = jax.random.key(seed)
        x = jax.random.randint(jax.random.fold_in(_rk, 1), (2, 1024), 0, 1024, jnp.int32)
        return x
    x = _rec_inputs()

    def _L0_tok_setup():
        import jax, jax.numpy as jnp
        import numpy as np
        V = 1024
        M = 4
        B = 8
        L = 512

        def _contexts(idx, vocab, order):
            Bb, Ll = idx.shape
            cols = []
            for k in range(order):
                s = order - 1 - k
                if s == 0:
                    cols.append(idx)
                else:
                    pad = jnp.full((Bb, s), vocab, dtype=idx.dtype)
                    cols.append(jnp.concatenate([pad, idx[:, :Ll - s]], axis=1))
            return jnp.stack(cols, axis=-1)
        key = jax.random.key(seed)
        k1, k2 = jax.random.split(key, 2)
        idx = jax.random.randint(k1, (B, L), 0, V, dtype=jnp.int64 if jax.config.jax_enable_x64 else jnp.int32)
        fan_in = M * (V + 1)
        bound = 1.0 / np.sqrt(fan_in)
        W = jax.random.uniform(k2, (V, fan_in), minval=-bound, maxval=bound, dtype=jnp.float32)
        b = jax.random.uniform(jax.random.fold_in(k2, 1), (V,), minval=-bound, maxval=bound, dtype=jnp.float32)
        return {'idx': idx, 'W': W, 'b': b}
    _L0_tok_all = _L0_tok_setup()
    _L0_tok_in = {k: v for k, v in _L0_tok_all.items() if k in ('W', 'b')}
    del _L0_tok_all

    def _L0_attn_setup():
        import jax, jax.numpy as jnp
        import numpy as np
        HID = 1024
        DM = 128
        DIN = 2 * DM
        DST = 16
        HD = 64
        NH = DIN // HD
        DCONV = 7
        CONV_DIM = DIN + 2 * DST
        DIN_PROJ = 2 * DIN + 2 * DST + 2 * NH
        SEQ, BATCH = (512, 4)

        def _causal_conv(x, w, b):
            y = jax.lax.conv_general_dilated(jnp.transpose(x, (0, 2, 1)), w, (1,), [(DCONV - 1, 0)], feature_group_count=CONV_DIM, dimension_numbers=('NCH', 'OIH', 'NCH'))
            return jnp.transpose(y, (0, 2, 1)) + b

        def _ssm_scan(x, dt, A, B, C):
            dA = jnp.exp(dt * A)
            dBx = dt[..., None] * x

            def step(h, t):
                dA_t, dBx_t, B_t, C_t = t
                h = dA_t[:, :, None, None] * h + dBx_t[..., None] * B_t[:, None, None, :]
                y = jnp.einsum('bhpn,bn->bhp', h, C_t)
                return (h, y)
            h0 = jnp.zeros((x.shape[0], NH, HD, DST), x.dtype)
            _, ys = jax.lax.scan(step, h0, (jnp.moveaxis(dA, 1, 0), jnp.moveaxis(dBx, 1, 0), jnp.moveaxis(B, 1, 0), jnp.moveaxis(C, 1, 0)))
            return jnp.moveaxis(ys, 0, 1)

        def _hydra(u, in_w, conv_w, conv_b, dt_bias, A_log, D, fcD_w, norm_w, out_w):
            b, l, _ = u.shape
            zxbcdt = u @ in_w.T
            z = zxbcdt[..., :DIN]
            xBC = zxbcdt[..., DIN:DIN + CONV_DIM]
            dt2 = zxbcdt[..., DIN + CONV_DIM:]
            dt_fw = jax.nn.softplus(dt2[..., :NH] + dt_bias)
            dt_bw = jax.nn.softplus(jnp.flip(dt2[..., NH:], 1) + dt_bias)
            xBC = jax.nn.silu(_causal_conv(xBC, conv_w, conv_b))
            xs = xBC[..., :DIN]
            Bm = xBC[..., DIN:DIN + DST]
            Cm = xBC[..., DIN + DST:]
            A = -jnp.exp(A_log)
            x4 = xs.reshape(b, l, NH, HD)
            y_fw = _ssm_scan(x4, dt_fw, A, Bm, Cm).reshape(b, l, DIN)
            y_bw = jnp.flip(_ssm_scan(jnp.flip(x4, 1), dt_bw, A, jnp.flip(Bm, 1), jnp.flip(Cm, 1)).reshape(b, l, DIN), 1)
            zero = jnp.zeros((b, 1, DIN), u.dtype)
            y = jnp.concatenate([zero, y_fw[:, :-1]], 1) + jnp.concatenate([y_bw[:, 1:], zero], 1)
            y = y + xs * jnp.repeat(xs @ fcD_w.T + D, HD, axis=-1)
            yz = y * jax.nn.silu(z)
            y = yz * jax.lax.rsqrt(jnp.mean(jnp.square(yz), -1, keepdims=True) + 1e-05) * norm_w
            return y @ out_w.T
        key = jax.random.key(seed)
        ks = jax.random.split(key, 12)
        rn = lambda k, shape, s=0.02: jax.random.normal(k, shape, jnp.float32) * s
        dt = jnp.exp(jax.random.uniform(ks[5], (NH,), jnp.float32, np.log(0.001), np.log(0.1)))
        return dict(x=jax.random.normal(ks[0], (SEQ, BATCH, HID), jnp.float32), w_down=rn(ks[1], (DM, HID)), b_down=jnp.zeros((DM,), jnp.float32), w_up=rn(ks[2], (HID, DM)), b_up=jnp.zeros((HID,), jnp.float32), gate1=jnp.asarray(0.6, jnp.float32), hy_in_w=rn(ks[3], (DIN_PROJ, DM)), hy_conv_w=rn(ks[4], (CONV_DIM, 1, DCONV), 0.2), hy_conv_b=jnp.zeros((CONV_DIM,), jnp.float32), hy_dt_bias=jnp.log(jnp.expm1(dt)), hy_A_log=jnp.log(jax.random.uniform(ks[6], (NH,), jnp.float32, 1.0, 16.0)), hy_D=jnp.ones((NH,), jnp.float32), hy_fcD_w=rn(ks[7], (NH, DIN)), hy_norm_w=jnp.ones((DIN,), jnp.float32), hy_out_w=rn(ks[8], (DM, DIN)))
    _L0_attn_all = _L0_attn_setup()
    _L0_attn_in = {k: v for k, v in _L0_attn_all.items() if k in ('w_down', 'b_down', 'w_up', 'b_up', 'gate1', 'hy_in_w', 'hy_conv_w', 'hy_conv_b', 'hy_dt_bias', 'hy_A_log', 'hy_D', 'hy_fcD_w', 'hy_norm_w', 'hy_out_w')}
    del _L0_attn_all

    def _L0_ffn_setup():
        import jax, jax.numpy as jnp
        import numpy as np
        R = 16
        ALPHA = 32
        SCALING = ALPHA / R
        E = 8
        TOP_K = 2
        key = jax.random.key(seed)
        ks = jax.random.split(key, 5)
        B, S, D = (4, 512, 1024)
        x = jax.random.normal(ks[0], (B, S, D), dtype=jnp.float32)
        base_W = jax.random.normal(ks[1], (D, D), dtype=jnp.float32) * 0.02
        router_W = jax.random.normal(ks[2], (E, D), dtype=jnp.float32) * 0.02
        lora_A = jax.random.normal(ks[3], (E, D, R), dtype=jnp.float32) * 0.02
        lora_B = jax.random.normal(ks[4], (E, R, D), dtype=jnp.float32) * 0.02
        return {'x': x, 'base_W': base_W, 'router_W': router_W, 'lora_A': lora_A, 'lora_B': lora_B}
    _L0_ffn_all = _L0_ffn_setup()
    _L0_ffn_in = {k: v for k, v in _L0_ffn_all.items() if k in ('base_W', 'router_W', 'lora_A', 'lora_B')}
    del _L0_ffn_all

    def _L1_attn_setup():
        import jax, jax.numpy as jnp
        import numpy as np
        H = 1024
        D = 2048
        N = 16
        K = 4
        R = 64
        BATCH = 1
        L = 512
        EPS = 1e-06

        def _rmsnorm(x, w):
            return x * jax.lax.rsqrt(jnp.mean(x * x, axis=-1, keepdims=True) + EPS) * w
        key = jax.random.key(seed)
        ks = jax.random.split(key, 10)
        s = 0.02
        return {'hidden_states': jax.random.normal(ks[0], (BATCH, L, H), jnp.float32), 'W_in': jax.random.normal(ks[1], (2 * D, H), jnp.float32) * s, 'conv_w': jax.random.normal(ks[2], (D, K), jnp.float32) * s, 'conv_b': jax.random.normal(ks[3], (D,), jnp.float32) * s, 'Wx': jax.random.normal(ks[4], (R + 2 * N, D), jnp.float32) * s, 'dt_ln_w': jnp.ones((R,), jnp.float32), 'b_ln_w': jnp.ones((N,), jnp.float32), 'c_ln_w': jnp.ones((N,), jnp.float32), 'Wdt': jax.random.normal(ks[5], (D, R), jnp.float32) * s, 'dt_bias': jax.random.normal(ks[6], (D,), jnp.float32) * s, 'A': -jnp.exp(jax.random.normal(ks[7], (D, N), jnp.float32) * 0.5), 'D_param': jnp.ones((D,), jnp.float32), 'W_out': jax.random.normal(ks[8], (H, D), jnp.float32) * s}
    _L1_attn_all = _L1_attn_setup()
    _L1_attn_in = {k: v for k, v in _L1_attn_all.items() if k in ('W_in', 'conv_w', 'conv_b', 'Wx', 'dt_ln_w', 'b_ln_w', 'c_ln_w', 'Wdt', 'dt_bias', 'A', 'D_param', 'W_out')}
    del _L1_attn_all

    def _L1_ffn_setup():
        import jax, jax.numpy as jnp
        import numpy as np
        IN_F = 1024
        OUT_F = 1024
        GROUP = 128
        key = jax.random.key(seed)
        k1, k2, k3 = jax.random.split(key, 3)
        x = jax.random.normal(k1, (4, 512, IN_F), dtype=jnp.float32)
        ternary = (jax.random.randint(k2, (OUT_F, IN_F), 0, 3) - 1).astype(jnp.int8)
        n_groups = OUT_F * IN_F // GROUP
        scales = jax.random.uniform(k3, (n_groups,), dtype=jnp.float32, minval=0.01, maxval=0.1)
        return {'x': x, 'ternary': ternary, 'scales': scales}
    _L1_ffn_all = _L1_ffn_setup()
    _L1_ffn_in = {k: v for k, v in _L1_ffn_all.items() if k in ('ternary', 'scales')}
    del _L1_ffn_all
    return {'x': x, 'L0_tok_W': _L0_tok_in['W'], 'L0_tok_b': _L0_tok_in['b'], 'L0_attn_w_down': _L0_attn_in['w_down'], 'L0_attn_b_down': _L0_attn_in['b_down'], 'L0_attn_w_up': _L0_attn_in['w_up'], 'L0_attn_b_up': _L0_attn_in['b_up'], 'L0_attn_gate1': _L0_attn_in['gate1'], 'L0_attn_hy_in_w': _L0_attn_in['hy_in_w'], 'L0_attn_hy_conv_w': _L0_attn_in['hy_conv_w'], 'L0_attn_hy_conv_b': _L0_attn_in['hy_conv_b'], 'L0_attn_hy_dt_bias': _L0_attn_in['hy_dt_bias'], 'L0_attn_hy_A_log': _L0_attn_in['hy_A_log'], 'L0_attn_hy_D': _L0_attn_in['hy_D'], 'L0_attn_hy_fcD_w': _L0_attn_in['hy_fcD_w'], 'L0_attn_hy_norm_w': _L0_attn_in['hy_norm_w'], 'L0_attn_hy_out_w': _L0_attn_in['hy_out_w'], 'L0_ffn_base_W': _L0_ffn_in['base_W'], 'L0_ffn_router_W': _L0_ffn_in['router_W'], 'L0_ffn_lora_A': _L0_ffn_in['lora_A'], 'L0_ffn_lora_B': _L0_ffn_in['lora_B'], 'L1_attn_W_in': _L1_attn_in['W_in'], 'L1_attn_conv_w': _L1_attn_in['conv_w'], 'L1_attn_conv_b': _L1_attn_in['conv_b'], 'L1_attn_Wx': _L1_attn_in['Wx'], 'L1_attn_dt_ln_w': _L1_attn_in['dt_ln_w'], 'L1_attn_b_ln_w': _L1_attn_in['b_ln_w'], 'L1_attn_c_ln_w': _L1_attn_in['c_ln_w'], 'L1_attn_Wdt': _L1_attn_in['Wdt'], 'L1_attn_dt_bias': _L1_attn_in['dt_bias'], 'L1_attn_A': _L1_attn_in['A'], 'L1_attn_D_param': _L1_attn_in['D_param'], 'L1_attn_W_out': _L1_attn_in['W_out'], 'L1_ffn_ternary': _L1_ffn_in['ternary'], 'L1_ffn_scales': _L1_ffn_in['scales']}

def reference(x, L0_tok_W, L0_tok_b, L0_attn_w_down, L0_attn_b_down, L0_attn_w_up, L0_attn_b_up, L0_attn_gate1, L0_attn_hy_in_w, L0_attn_hy_conv_w, L0_attn_hy_conv_b, L0_attn_hy_dt_bias, L0_attn_hy_A_log, L0_attn_hy_D, L0_attn_hy_fcD_w, L0_attn_hy_norm_w, L0_attn_hy_out_w, L0_ffn_base_W, L0_ffn_router_W, L0_ffn_lora_A, L0_ffn_lora_B, L1_attn_W_in, L1_attn_conv_w, L1_attn_conv_b, L1_attn_Wx, L1_attn_dt_ln_w, L1_attn_b_ln_w, L1_attn_c_ln_w, L1_attn_Wdt, L1_attn_dt_bias, L1_attn_A, L1_attn_D_param, L1_attn_W_out, L1_ffn_ternary, L1_ffn_scales):
    import jax
    import jax.numpy as jnp

    def _L0_tok_ref(idx, W, b):
        import jax, jax.numpy as jnp
        import numpy as np
        V = 1024
        M = 4
        B = 8
        L = 512

        def _contexts(idx, vocab, order):
            Bb, Ll = idx.shape
            cols = []
            for k in range(order):
                s = order - 1 - k
                if s == 0:
                    cols.append(idx)
                else:
                    pad = jnp.full((Bb, s), vocab, dtype=idx.dtype)
                    cols.append(jnp.concatenate([pad, idx[:, :Ll - s]], axis=1))
            return jnp.stack(cols, axis=-1)
        vocab = W.shape[0]
        order = W.shape[1] // (vocab + 1)
        x = _contexts(idx, vocab, order)
        Wt = W.T.reshape(order, vocab + 1, vocab)
        logits = b
        for k in range(order):
            logits = logits + Wt[k][x[..., k]]
        return logits

    def _L0_attn_ref(x, w_down, b_down, w_up, b_up, gate1, hy_in_w, hy_conv_w, hy_conv_b, hy_dt_bias, hy_A_log, hy_D, hy_fcD_w, hy_norm_w, hy_out_w):
        import jax, jax.numpy as jnp
        import numpy as np
        HID = 1024
        DM = 128
        DIN = 2 * DM
        DST = 16
        HD = 64
        NH = DIN // HD
        DCONV = 7
        CONV_DIM = DIN + 2 * DST
        DIN_PROJ = 2 * DIN + 2 * DST + 2 * NH
        SEQ, BATCH = (512, 4)

        def _causal_conv(x, w, b):
            y = jax.lax.conv_general_dilated(jnp.transpose(x, (0, 2, 1)), w, (1,), [(DCONV - 1, 0)], feature_group_count=CONV_DIM, dimension_numbers=('NCH', 'OIH', 'NCH'))
            return jnp.transpose(y, (0, 2, 1)) + b

        def _ssm_scan(x, dt, A, B, C):
            dA = jnp.exp(dt * A)
            dBx = dt[..., None] * x

            def step(h, t):
                dA_t, dBx_t, B_t, C_t = t
                h = dA_t[:, :, None, None] * h + dBx_t[..., None] * B_t[:, None, None, :]
                y = jnp.einsum('bhpn,bn->bhp', h, C_t)
                return (h, y)
            h0 = jnp.zeros((x.shape[0], NH, HD, DST), x.dtype)
            _, ys = jax.lax.scan(step, h0, (jnp.moveaxis(dA, 1, 0), jnp.moveaxis(dBx, 1, 0), jnp.moveaxis(B, 1, 0), jnp.moveaxis(C, 1, 0)))
            return jnp.moveaxis(ys, 0, 1)

        def _hydra(u, in_w, conv_w, conv_b, dt_bias, A_log, D, fcD_w, norm_w, out_w):
            b, l, _ = u.shape
            zxbcdt = u @ in_w.T
            z = zxbcdt[..., :DIN]
            xBC = zxbcdt[..., DIN:DIN + CONV_DIM]
            dt2 = zxbcdt[..., DIN + CONV_DIM:]
            dt_fw = jax.nn.softplus(dt2[..., :NH] + dt_bias)
            dt_bw = jax.nn.softplus(jnp.flip(dt2[..., NH:], 1) + dt_bias)
            xBC = jax.nn.silu(_causal_conv(xBC, conv_w, conv_b))
            xs = xBC[..., :DIN]
            Bm = xBC[..., DIN:DIN + DST]
            Cm = xBC[..., DIN + DST:]
            A = -jnp.exp(A_log)
            x4 = xs.reshape(b, l, NH, HD)
            y_fw = _ssm_scan(x4, dt_fw, A, Bm, Cm).reshape(b, l, DIN)
            y_bw = jnp.flip(_ssm_scan(jnp.flip(x4, 1), dt_bw, A, jnp.flip(Bm, 1), jnp.flip(Cm, 1)).reshape(b, l, DIN), 1)
            zero = jnp.zeros((b, 1, DIN), u.dtype)
            y = jnp.concatenate([zero, y_fw[:, :-1]], 1) + jnp.concatenate([y_bw[:, 1:], zero], 1)
            y = y + xs * jnp.repeat(xs @ fcD_w.T + D, HD, axis=-1)
            yz = y * jax.nn.silu(z)
            y = yz * jax.lax.rsqrt(jnp.mean(jnp.square(yz), -1, keepdims=True) + 1e-05) * norm_w
            return y @ out_w.T
        x_init = x
        h = x @ w_down.T + b_down
        h = jnp.transpose(h, (1, 0, 2))
        h = jax.nn.gelu(h, approximate=False)
        xmid = h
        hp = (hy_in_w, hy_conv_w, hy_conv_b, hy_dt_bias, hy_A_log, hy_D, hy_fcD_w, hy_norm_w, hy_out_w)
        h = _hydra(h, *hp)
        h = _hydra(h, *hp)
        alpha = jax.nn.sigmoid(gate1)
        h = alpha * xmid + (1.0 - alpha) * h
        h = xmid + h
        h = h @ w_up.T + b_up
        return x_init + jnp.transpose(h, (1, 0, 2))

    def _L0_ffn_ref(x, base_W, router_W, lora_A, lora_B):
        import jax, jax.numpy as jnp
        import numpy as np
        R = 16
        ALPHA = 32
        SCALING = ALPHA / R
        E = 8
        TOP_K = 2
        base = jnp.einsum('bsd,od->bso', x, base_W)
        logits = jnp.einsum('bsd,ed->bse', x, router_W)
        probs = jax.nn.softmax(logits.astype(jnp.float32), axis=-1)
        top_vals, top_idx = jax.lax.top_k(probs, TOP_K)
        rw = top_vals / jnp.sum(top_vals, axis=-1, keepdims=True)
        w_dense = jnp.sum(jax.nn.one_hot(top_idx, E, dtype=rw.dtype) * rw[..., None], axis=-2).astype(x.dtype)
        mid = jnp.einsum('bsd,edr->bser', x, lora_A)
        mid = mid * w_dense[..., None]
        inc = jnp.einsum('bser,erd->bsd', mid, lora_B)
        return base + inc * SCALING

    def _L1_attn_ref(hidden_states, W_in, conv_w, conv_b, Wx, dt_ln_w, b_ln_w, c_ln_w, Wdt, dt_bias, A, D_param, W_out):
        import jax, jax.numpy as jnp
        import numpy as np
        H = 1024
        D = 2048
        N = 16
        K = 4
        R = 64
        BATCH = 1
        L = 512
        EPS = 1e-06

        def _rmsnorm(x, w):
            return x * jax.lax.rsqrt(jnp.mean(x * x, axis=-1, keepdims=True) + EPS) * w
        proj = hidden_states @ W_in.T
        u, gate = jnp.split(proj, 2, axis=-1)
        x = jnp.transpose(u, (0, 2, 1))
        x = jax.lax.conv_general_dilated(x, conv_w[:, None, :], window_strides=(1,), padding=[(K - 1, 0)], dimension_numbers=('NCH', 'OIH', 'NCH'), feature_group_count=D)
        u = jax.nn.silu(jnp.transpose(x, (0, 2, 1)) + conv_b)
        ssm_p = u @ Wx.T
        dt, Bm, Cm = jnp.split(ssm_p, [R, R + N], axis=-1)
        dt = _rmsnorm(dt, dt_ln_w)
        Bm = _rmsnorm(Bm, b_ln_w)
        Cm = _rmsnorm(Cm, c_ln_w)
        delta = jax.nn.softplus(dt @ Wdt.T + dt_bias)

        def step(state, xs):
            d_t, B_t, C_t, u_t = xs
            dA = jnp.exp(d_t[..., None] * A)
            state = dA * state + (d_t * u_t)[..., None] * B_t[:, None, :]
            y_t = jnp.einsum('bdn,bn->bd', state, C_t)
            return (state, y_t)
        init = jnp.zeros((hidden_states.shape[0], D, N), hidden_states.dtype)
        xs = (jnp.swapaxes(delta, 0, 1), jnp.swapaxes(Bm, 0, 1), jnp.swapaxes(Cm, 0, 1), jnp.swapaxes(u, 0, 1))
        _, ys = jax.lax.scan(step, init, xs)
        y = jnp.swapaxes(ys, 0, 1) + u * D_param
        y = y * jax.nn.silu(gate)
        return y @ W_out.T

    def _L1_ffn_ref(x, ternary, scales):
        import jax, jax.numpy as jnp
        import numpy as np
        IN_F = 1024
        OUT_F = 1024
        GROUP = 128
        s = scales.reshape(OUT_F, IN_F // GROUP, 1)
        w = ternary.astype(jnp.float32).reshape(OUT_F, IN_F // GROUP, GROUP) * s
        w = w.reshape(OUT_F, IN_F)
        return jnp.einsum('bsi,oi->bso', x, w)
    h = _L0_tok_ref(x, L0_tok_W, L0_tok_b)
    h = h + _L0_attn_ref(_layernorm(h, axis=-1), L0_attn_w_down, L0_attn_b_down, L0_attn_w_up, L0_attn_b_up, L0_attn_gate1, L0_attn_hy_in_w, L0_attn_hy_conv_w, L0_attn_hy_conv_b, L0_attn_hy_dt_bias, L0_attn_hy_A_log, L0_attn_hy_D, L0_attn_hy_fcD_w, L0_attn_hy_norm_w, L0_attn_hy_out_w)
    h = h + _L0_ffn_ref(_layernorm(h, axis=-1), L0_ffn_base_W, L0_ffn_router_W, L0_ffn_lora_A, L0_ffn_lora_B)
    h = h + _L1_attn_ref(_layernorm(h, axis=-1), L1_attn_W_in, L1_attn_conv_w, L1_attn_conv_b, L1_attn_Wx, L1_attn_dt_ln_w, L1_attn_b_ln_w, L1_attn_c_ln_w, L1_attn_Wdt, L1_attn_dt_bias, L1_attn_A, L1_attn_D_param, L1_attn_W_out)
    h = h + _L1_ffn_ref(_layernorm(h, axis=-1), L1_ffn_ternary, L1_ffn_scales)
    return h

_drawn_inputs = setup_inputs


def setup_inputs(seed=0):
    import zlib

    import numpy as np

    out = dict(_drawn_inputs(seed))
    spreads = {'L0_attn_b_down': (0.0, 0.284),
     'L0_attn_b_up': (0.0, 0.1),
     'L0_attn_hy_conv_b': (0.0, 0.8),
     'L0_attn_hy_D': (1.0, 0.6),
     'L0_attn_hy_norm_w': (1.0, 0.6),
     'L1_attn_dt_ln_w': (1.0, 0.6),
     'L1_attn_b_ln_w': (1.0, 0.6),
     'L1_attn_c_ln_w': (1.0, 0.6),
     'L1_attn_D_param': (1.0, 0.6)}
    factors = {'L0_attn_hy_in_w': 5.731,
     'L0_attn_hy_conv_w': 8.0,
     'L0_attn_hy_dt_bias': 64.0,
     'L0_attn_hy_fcD_w': 8.0,
     'L0_attn_hy_out_w': 6.189,
     'L1_attn_W_in': 2.901,
     'L1_attn_conv_w': 2.734,
     'L1_attn_conv_b': 2.753,
     'L1_attn_Wx': 2.702,
     'L1_attn_Wdt': 8.0,
     'L1_attn_dt_bias': 8.0,
     'L1_attn_A': 7.958,
     'L1_attn_W_out': 2.811}
    for name, (base, spread) in spreads.items():
        noise = np.random.default_rng([zlib.crc32(name.encode()), seed]).standard_normal(out[name].shape)
        drawn = base * np.exp(spread * noise) if base else spread * noise
        out[name] = jnp.asarray(drawn.astype(out[name].dtype))
    for name, factor in factors.items():
        out[name] = (out[name] * factor).astype(out[name].dtype)
    return out
```

```python
import concourse.bass as bass
from concourse import mybir
from contextlib import ExitStack

P = 128
FP = mybir.dt.float32
I32 = mybir.dt.int32
U32 = mybir.dt.uint32
ALU = mybir.AluOpType
ACT = mybir.ActivationFunctionType

HID = 1024
TOK = 2048
ROW = 1024
KT = HID // P
BANK = 512
LN_EPS = 1e-5

ORDER = 4
VOC1 = HID + 1
DIN = 256
DST = 16
TAP_NOW, TAP_BEFORE = 6, 5
EXPERTS, RANK = 8, 16
ER = EXPERTS * RANK
LORA_SCALE = 2.0
CHUNKS = 4
HALF = 256


class Steps:

    def __init__(self, engine, sem):
        self.engine, self.sem, self.at, self.reg = engine, sem, 0, None

    def value(self):
        return self.at if self.reg is None else self.reg + self.at

    def link(self, instruction):
        instruction.then_inc(self.sem, 1)
        self.at += 1
        self.engine.wait_ge(self.sem, self.value())

    def enter(self, i, per):
        self.start, self.per = self.at, per
        self.reg = i * per

    def leave(self, times):
        assert self.at - self.start == self.per, (self.at - self.start, self.per)
        self.reg, self.at = None, self.start + self.per * times


def apart(engine, sem):
    engine.sem_inc(sem, 1)


def identity(nc, pool, tile, sem):
    nc.gpsimd.memset(tile, 0.0).then_inc(sem, 1)
    pool.wait_ge(sem, 1)
    nc.gpsimd.affine_select(out=tile, in_=tile, compare_op=ALU.not_equal, fill=1.0, base=0,
                            pattern=[[-1, P]], channel_multiplier=1).then_inc(sem, 1)


def layer0(nc, a, h_dram):
    with ExitStack() as ctx:
        def sb(name, shape, dt=FP):
            return ctx.enter_context(nc.sbuf_tensor(name, shape, dt))

        def sem(name):
            return ctx.enter_context(nc.semaphore(name))

        ident = sb("l0_ident", [P, P])
        ones = sb("l0_ones", [P, P])
        iota_i = sb("l0_iota_i", [P, EXPERTS], I32)
        iota = sb("l0_iota", [P, EXPERTS])
        eps = sb("l0_eps", [P, 1])
        tok_b = sb("l0_tok_b", [P, HID])
        up_b = sb("l0_up_b", [P, HID])
        w_down = sb("l0_w_down", [P, KT, P])
        w_up = sb("l0_w_up", [P, HID])
        w_base = sb("l0_w_base", [P, KT, HID])
        w_lora = sb("l0_w_lora", [P, KT, ER + EXPERTS])
        w_lora_b = sb("l0_w_lora_b", [P, HID])
        in_z = sb("l0_in_z", [P, DIN])
        in_x = sb("l0_in_x", [P, DIN])
        in_bc = sb("l0_in_bc", [P, 2 * DST])
        in_dt = sb("l0_in_dt", [P, 2, DIN])
        w_fc = sb("l0_w_fc", [P, 2, DIN])
        w_out = sb("l0_w_out", [P, 2, P])
        col = sb("l0_col", [P, 8])
        conv_x = sb("l0_conv_x", [P, 2, 8])
        conv_bc = sb("l0_conv_bc", [DST, 2, 8])
        alpha = sb("l0_alpha", [P, 2])
        xi = sb("l0_xi", [16, ORDER, P], I32)
        xf = sb("l0_xf", [16, ORDER, P])
        idx = sb("l0_idx", [P, 16, ORDER], I32)
        idx_now = sb("l0_idx_now", [P, 4, ORDER], I32)
        emb = sb("l0_emb", [P, 2, ORDER, HID])
        H = sb("l0_H", [P, 4, HID])
        X = sb("l0_X", [P, 4, HID])
        xT = sb("l0_xT", [P, KT, BANK])
        stats = sb("l0_stats", [P, 4, 2, 6])
        mv = sb("l0_mv", [P, 4, 2])
        lnv = sb("l0_lnv", [P, 4])
        rstd = sb("l0_rstd", [P, 4])
        xm = sb("l0_xm", [P, BANK])
        hout = sb("l0_hout", [P, 2, BANK])
        hmix = sb("l0_hmix", [P, BANK])
        zs = sb("l0_zs", [P, 2, BANK])
        xs = sb("l0_xs", [P, 2, BANK])
        cv = sb("l0_cv", [P, 2, HALF])
        cvb = sb("l0_cvb", [DST, 2, HALF])
        Bs = sb("l0_Bs", [DST, BANK])
        Cs = sb("l0_Cs", [DST, BANK])
        BC = sb("l0_BC", [DST, BANK])
        sp = sb("l0_sp", [P, 2, BANK])
        dts = sb("l0_dts", [P, 2, BANK])
        yq = sb("l0_yq", [P, 2, BANK])
        yz = sb("l0_yz", [P, 2, BANK])
        sq = sb("l0_sq", [P, 2, BANK])
        rms = sb("l0_rms", [P, BANK])
        top = sb("l0_top", [P, 4, 8])
        topi = sb("l0_topi", [P, 4, 8], U32)
        rt = sb("l0_rt", [P, 4, 8])
        r2 = sb("l0_r2", [P, 4, 8])
        wd = sb("l0_wd", [P, 2, 2, EXPERTS])
        mid = sb("l0_mid", [P, 2, EXPERTS, RANK])
        midT = sb("l0_midT", [P, 2, P])
        ps = ctx.enter_context(nc.psum_tensor("l0_ps", [P, 8, BANK], FP))

        s_const = sem("l0_const")
        s_w = sem("l0_weights")
        s_wbig = sem("l0_weights_big")
        s_xi0 = sem("l0_xi_filled")
        s_xi = sem("l0_xi_loaded")
        s_xf = sem("l0_xf")
        s_ixT = sem("l0_ixT")
        s_idx = sem("l0_idx")
        s_now = sem("l0_idx_now")
        s_emb_free = sem("l0_emb_free")
        s_emb = [sem(f"l0_emb{n}") for n in range(2)]
        s_var = sem("l0_var")
        s_rstd = sem("l0_rstd")
        s_x = sem("l0_x")
        s_xt = sem("l0_xt")
        s_xT = sem("l0_xT")
        s_down = sem("l0_down")
        s_xm = sem("l0_xm")
        s_in = sem("l0_in")
        s_act = sem("l0_act_steps")
        s_dve = sem("l0_dve_steps")
        s_apart_dve = sem("l0_apart_dve")
        s_apart_pool = sem("l0_apart_pool")
        s_cv = sem("l0_cv")
        s_bcs = sem("l0_bcs")
        s_xs = sem("l0_xs")
        s_zs = sem("l0_zs")
        s_sp = sem("l0_sp")
        s_bcp = sem("l0_bcp")
        s_bc = sem("l0_bc")
        s_fc = sem("l0_fc")
        s_yz = sem("l0_yz")
        s_sq = sem("l0_sq")
        s_ms = sem("l0_ms")
        s_rms = sem("l0_rms")
        s_yn = sem("l0_yn")
        s_ho = sem("l0_ho")
        s_hout = sem("l0_hout")
        s_alpha = sem("l0_alpha")
        s_hmix = sem("l0_hmix")
        s_up = sem("l0_up")
        s_h1 = sem("l0_h1")
        s_rt = sem("l0_rt")
        s_gap = sem("l0_gap")
        s_e2 = sem("l0_e2")
        s_mid = sem("l0_mid")
        s_midt = sem("l0_midt")
        s_midT = sem("l0_midT")
        s_base = sem("l0_base")
        s_h2 = sem("l0_h2")
        s_store = [sem(f"l0_store{n}") for n in range(4)]

        b_down, gate = col[:, 0:1], col[:, 1:2]
        dt_bias, D_col, norm_w = col[:, 2:4], col[:, 4:6], col[:, 6:8]

        def rows(c, tt):
            return h_dram[bass.ds(c * HALF + ((tt // 2) * ROW + (tt % 2) * P), P), :]

        block = ctx.enter_context(nc.Block())

        @block.sync
        def _(sp_):
            sp_.wait_ge(s_xi0, 1)
            for k in range(ORDER):
                back = ORDER - 1 - k
                for b in range(2):
                    r0 = 8 * b
                    if back == 0:
                        sp_.dma_start(xi[r0:r0 + 8, k, :], a["x"][b, :].rearrange("(j p) -> j p", p=P)).then_inc(s_xi, 16)
                    else:
                        sp_.dma_start(xi[r0:r0 + 1, k, back:P], a["x"][b:b + 1, 0:P - back]).then_inc(s_xi, 16)
                        sp_.dma_start(xi[r0 + 1:r0 + 8, k, :],
                                      a["x"][b, P - back:ROW - back].rearrange("(j p) -> j p", p=P)).then_inc(s_xi, 16)
            sp_.dma_start(tok_b[:], a["tok_b"].partition_broadcast(P)).then_inc(s_w, 16)
            sp_.dma_start(up_b[:], a["up_b"].partition_broadcast(P)).then_inc(s_w, 16)
            for dst, name in ((in_z, "in_z"), (in_x, "in_x"), (in_bc, "in_bc"), (in_dt, "in_dt"),
                              (w_fc, "w_fc"), (w_out, "w_hout"), (col, "col"), (conv_x, "conv_x"),
                              (conv_bc, "conv_bc")):
                sp_.dma_start(dst[:], a[name]).then_inc(s_w, 16)
            for dst, name in ((w_down, "w_down"), (w_up, "w_up"), (w_lora, "w_lora"),
                              (w_lora_b, "w_lora_b"), (w_base, "w_base")):
                sp_.dma_start(dst[:], a[name]).then_inc(s_wbig, 16)
            for tt in range(4):
                sp_.sem_inc(s_store[tt], 16)
            with sp_.Fori(0, CHUNKS) as c:
                for tt in range(4):
                    sp_.wait_ge(s_h2, c * 4 + (tt + 1))
                    sp_.dma_start(rows(c, tt), H[:, tt, :]).then_inc(s_store[tt], 16)
            for tt in range(4):
                sp_.wait_ge(s_store[tt], 16 * (CHUNKS + 1))

        @block.gpsimd
        def _(pool):
            nc.gpsimd.memset(xi[:], HID).then_inc(s_xi0, 1)
            identity(nc, pool, ident[:], s_const)
            nc.gpsimd.memset(ones[:], 1.0).then_inc(s_const, 1)
            nc.gpsimd.memset(eps[:], LN_EPS).then_inc(s_const, 1)
            nc.gpsimd.iota(iota_i[:], pattern=[[1, EXPERTS]], base=0, channel_multiplier=0).then_inc(s_const, 1)
            pool.wait_ge(s_const, 5)
            nc.gpsimd.tensor_copy(iota[:], iota_i[:]).then_inc(s_const, 1)
            pool.wait_ge(s_idx, 1)
            with pool.Fori(0, CHUNKS) as c:
                for tt in range(4):
                    pool.wait_ge(s_emb_free, c * 4 + (tt + 1))
                    nc.gpsimd.tensor_copy(idx_now[:, tt, :],
                                          idx[:, bass.ds(c * 2 + (8 * (tt // 2) + tt % 2), 1), :]).then_inc(s_now, 1)
                    pool.wait_ge(s_now, c * 4 + (tt + 1))
                    apart(pool, s_apart_pool)
                    for k in range(ORDER):
                        nc.gpsimd.indirect_dma_start(
                            out=emb[:, tt % 2, k, :], out_offset=None, in_=a["tok_W"],
                            in_offset=bass.IndirectOffsetOnAxis(ap=idx_now[:, tt, k:k + 1], axis=0))\
                            .then_inc(s_emb[tt % 2], 16)

        @block.tensor
        def _(pe):
            pe.wait_ge(s_const, 2)
            pe.wait_ge(s_xf, 1)
            for k in range(ORDER):
                ins = nc.tensor.transpose(ps[:, 0, 16 * k:16 * k + 16], xf[:, k, :], ident[0:16, 0:16])
            ins.then_inc(s_ixT, 1)
            pe.wait_ge(s_idx, 1)
            pe.wait_ge(s_w, 16 * 11)
            pe.wait_ge(s_wbig, 16 * 5)

            def transposes(tt, base):
                pe.wait_ge(s_x, base + tt + 1)
                for h in range(2):
                    for q in range(4):
                        k = 4 * h + q
                        ins = nc.tensor.transpose(ps[:, 2 * tt + h, P * q:P * q + P],
                                                  X[:, tt, P * k:P * k + P], ident[:])
                    ins.then_inc(s_xt, 1)

            def product(out, parts):
                for n, (lhsT, rhs) in enumerate(parts):
                    ins = nc.tensor.matmul(out, lhsT, rhs, start=(n == 0), stop=(n == len(parts) - 1))
                return ins

            with pe.Fori(0, CHUNKS) as c:
                for tt in range(4):
                    transposes(tt, c * 8)
                pe.wait_ge(s_xT, c * 16 + 8)
                product(ps[:, 4, :], [(w_down[:, k, :], xT[:, k, :]) for k in range(KT)]).then_inc(s_down, 1)
                for r in range(2):
                    if r == 0:
                        pe.wait_ge(s_xm, c + 1)
                        u = xm
                    else:
                        pe.wait_ge(s_hout, c * 2 + 1)
                        u = hout[:, 0, :]
                    n = c * 2 + (r + 1)
                    for t in range(2):
                        ins = product(ps[:, 2 + t, :], [(in_x[:, P * t:P * t + P], u[:, :])])
                    ins.then_inc(s_in, 1)
                    for t in range(2):
                        ins = product(ps[0:DST, 4 + t, :], [(in_bc[:, DST * t:DST * t + DST], u[:, :])])
                    ins.then_inc(s_in, 1)
                    for t in range(2):
                        for d in range(2):
                            ins = product(ps[:, 6 + t, HALF * d:HALF * d + HALF],
                                          [(in_dt[:, d, P * t:P * t + P], u[:, HALF * d:HALF * d + HALF])])
                    ins.then_inc(s_in, 1)
                    for t in range(2):
                        ins = product(ps[:, t, :], [(in_z[:, P * t:P * t + P], u[:, :])])
                    ins.then_inc(s_in, 1)
                    pe.wait_ge(s_bcp, n)
                    product(ps[:, 4, :], [(ones[0:DST, :], BC[:])]).then_inc(s_bc, 1)
                    pe.wait_ge(s_xs, n * 2)
                    for t in range(2):
                        ins = product(ps[:, 2 + t, :], [(w_fc[:, k, P * t:P * t + P], xs[:, k, :]) for k in range(2)])
                    ins.then_inc(s_fc, 1)
                    pe.wait_ge(s_sq, n)
                    product(ps[:, 5, :], [(ones[:], sq[:, k, :]) for k in range(2)]).then_inc(s_ms, 1)
                    pe.wait_ge(s_yn, n)
                    product(ps[:, 6, :], [(w_out[:, k, :], yz[:, k, :]) for k in range(2)]).then_inc(s_ho, 1)
                pe.wait_ge(s_hmix, c + 1)
                for tt in range(4):
                    for h in range(2):
                        ins = product(ps[:, 2 * tt + h, :], [(hmix[:, P * tt:P * tt + P], w_up[:, BANK * h:BANK * h + BANK])])
                    ins.then_inc(s_up, 1)
                for tt in range(4):
                    transposes(tt, c * 8 + 4)
                for tt in range(4):
                    pe.wait_ge(s_xT, c * 16 + (8 + 2 * tt + 2))
                    product(ps[:, 2 * tt, 0:ER + EXPERTS],
                            [(xT[:, k, P * tt:P * tt + P], w_lora[:, k, :]) for k in range(KT)]).then_inc(s_rt, 1)
                for tt in range(4):
                    pe.wait_ge(s_mid, c * 4 + (tt + 1))
                    nc.tensor.transpose(ps[:, 2 * tt + 1, 0:P],
                                        mid[:, tt % 2, :, :].rearrange("p e r -> p (e r)"), ident[:]).then_inc(s_midt, 1)
                    pe.wait_ge(s_midT, c * 4 + (tt + 1))
                    for h in range(2):
                        ins = product(ps[:, 2 * tt + h, :],
                                      [(xT[:, k, P * tt:P * tt + P], w_base[:, k, BANK * h:BANK * h + BANK])
                                       for k in range(KT)]
                                      + [(midT[:, tt % 2, :], w_lora_b[:, BANK * h:BANK * h + BANK])])
                    ins.then_inc(s_base, 1)

        @block.scalar
        def _(act):
            act.wait_ge(s_const, 4)
            act.wait_ge(s_w, 16 * 11)
            step = Steps(act, s_act)
            step.link(nc.scalar.activation(alpha[:, 0:1], gate, ACT.Sigmoid))
            act.sem_inc(s_alpha, 1)

            def inverse_std(tt, base):
                act.wait_ge(s_var, base + tt + 1)
                step.link(nc.scalar.activation(lnv[:, tt:tt + 1], mv[:, tt, 1:2], ACT.Ln, bias=eps[:]))
                nc.scalar.activation(rstd[:, tt:tt + 1], lnv[:, tt:tt + 1], ACT.Exp, scale=-0.5).then_inc(s_rstd, 1)

            def transposed(tt, base):
                for h in range(2):
                    act.wait_ge(s_xt, base + (2 * tt + h + 1))
                    nc.scalar.activation(xT[:, 4 * h:4 * h + 4, P * tt:P * tt + P],
                                         ps[:, 2 * tt + h, :].rearrange("p (k t) -> p k t", t=P), ACT.Copy)\
                        .then_inc(s_xT, 1)

            with act.Fori(0, CHUNKS) as c:
                step.enter(c, 2 * 4 + 2 * (4 + 1))
                for tt in range(4):
                    inverse_std(tt, c * 8)
                for tt in range(4):
                    transposed(tt, c * 16)
                act.wait_ge(s_down, c + 1)
                nc.scalar.activation(xm[:], ps[:, 4, :], ACT.Gelu, bias=b_down).then_inc(s_xm, 1)
                for r in range(2):
                    n = c * 2 + (r + 1)
                    for t in range(2):
                        act.wait_ge(s_cv, n * 4 - 4 + (t + 1))
                        nc.scalar.activation(xs[:, t, 0:HALF], ps[:, 2 + t, 0:HALF], ACT.Silu,
                                             scale=conv_x[:, t, TAP_NOW:TAP_NOW + 1], bias=conv_x[:, t, 7:8])
                        nc.scalar.activation(xs[:, t, HALF:BANK], cv[:, t, :], ACT.Silu,
                                             bias=conv_x[:, t, 7:8]).then_inc(s_xs, 1)
                    for t, dst in ((0, Bs), (1, Cs)):
                        act.wait_ge(s_cv, n * 4 - 4 + (t + 3))
                        nc.scalar.activation(dst[:, 0:HALF], ps[0:DST, 4 + t, 0:HALF], ACT.Silu,
                                             scale=conv_bc[:, t, TAP_NOW:TAP_NOW + 1], bias=conv_bc[:, t, 7:8])
                        nc.scalar.activation(dst[:, HALF:BANK], cvb[:, t, :], ACT.Silu,
                                             bias=conv_bc[:, t, 7:8]).then_inc(s_bcs, 1)
                    act.wait_ge(s_in, n * 4)
                    nc.scalar.activation(zs[:], ps[:, 0:2, :], ACT.Silu).then_inc(s_zs, 1)
                    for t in range(2):
                        step.link(nc.scalar.activation(sp[:, t, :], ps[:, 6 + t, :], ACT.Abs, bias=dt_bias[:, t:t + 1]))
                    step.link(nc.scalar.activation(sp[:], sp[:], ACT.Exp, scale=-1.0))
                    nc.scalar.activation(sp[:], sp[:], ACT.Ln, bias=1.0).then_inc(s_sp, 1)
                    act.wait_ge(s_yz, n)
                    nc.scalar.activation(sq[:], yz[:], ACT.Square).then_inc(s_sq, 1)
                    act.wait_ge(s_ms, n)
                    step.link(nc.scalar.activation(rms[:], ps[:, 5, :], ACT.Ln, scale=1.0 / DIN, bias=eps[:]))
                    step.link(nc.scalar.activation(rms[:], rms[:], ACT.Exp, scale=-0.5))
                    act.sem_inc(s_rms, 1)
                    act.wait_ge(s_ho, n)
                    nc.scalar.activation(hout[:, r, :], ps[:, 6, :], ACT.Copy).then_inc(s_hout, 1)
                for tt in range(4):
                    inverse_std(tt, c * 8 + 4)
                for tt in range(4):
                    transposed(tt, c * 16 + 8)
                for tt in range(4):
                    act.wait_ge(s_gap, c * 4 + (tt + 1))
                    nc.scalar.activation(r2[:, tt, 1:2], r2[:, tt, 0:1], ACT.Exp).then_inc(s_e2, 1)
                for tt in range(4):
                    act.wait_ge(s_midt, c * 4 + (tt + 1))
                    nc.scalar.activation(midT[:, tt % 2, :], ps[:, 2 * tt + 1, 0:P], ACT.Copy).then_inc(s_midT, 1)
            step.leave(CHUNKS)

        @block.vector
        def _(dve):
            dve.sem_inc(s_emb_free, 2)
            step = Steps(dve, s_dve)
            tt_, ts_, stt = nc.vector.tensor_tensor, nc.vector.tensor_scalar, nc.vector.scalar_tensor_tensor
            dve.wait_ge(s_xi, 16 * 14)
            for k in range(ORDER):
                ins = ts_(xf[:, k, :], xi[:, k, :], float(k * VOC1), None, ALU.add)
            ins.then_inc(s_xf, 1)
            dve.wait_ge(s_ixT, 1)
            nc.vector.tensor_copy(idx[:].rearrange("p g k -> p k g"),
                                  ps[:, 0, 0:16 * ORDER].rearrange("p (k g) -> p k g", g=16)).then_inc(s_idx, 1)
            dve.wait_ge(s_const, 6)
            dve.wait_ge(s_w, 16 * 11)
            dve.wait_ge(s_alpha, 1)
            step.link(ts_(alpha[:, 1:2], alpha[:, 0:1], -1.0, 1.0, ALU.mult, ALU.add))

            def mean_var(tt):
                for h in range(2):
                    ins = nc.vector.bn_stats(stats[:, tt, h, :], H[:, tt, BANK * h:BANK * h + BANK])
                step.link(ins)
                apart(dve, s_apart_dve)
                nc.vector.bn_aggr(mv[:, tt, :], stats[:, tt, :, :]).then_inc(s_var, 1)

            def normalise(tt, base):
                dve.wait_ge(s_rstd, base + tt + 1)
                ts_(X[:, tt, :], H[:, tt, :], mv[:, tt, 0:1], rstd[:, tt:tt + 1], ALU.subtract, ALU.mult)\
                    .then_inc(s_x, 1)

            with dve.Fori(0, CHUNKS) as c:
                step.enter(c, 4 * 5 + 4 * 2 + 2 * 7 + 2 + 4 + 4 * 8)
                for tt in range(4):
                    dve.wait_ge(s_emb[tt % 2], c * (2 * ORDER * 16) + (tt // 2 + 1) * ORDER * 16)
                    dve.wait_ge(s_store[tt], c * 16 + 16)
                    step.link(tt_(H[:, tt, :], emb[:, tt % 2, 0, :], tok_b[:], ALU.add))
                    for k in range(1, ORDER):
                        step.link(tt_(H[:, tt, :], H[:, tt, :], emb[:, tt % 2, k, :], ALU.add))
                    dve.sem_inc(s_emb_free, 1)
                    mean_var(tt)
                for tt in range(4):
                    normalise(tt, c * 8)
                for tt in range(4):
                    dve.wait_ge(s_x, c * 8 + (tt + 1))
                    step.link(tt_(H[:, tt, :], H[:, tt, :], X[:, tt, :], ALU.add))
                    step.link(tt_(H[:, tt, :], H[:, tt, :], up_b[:], ALU.add))
                for r in range(2):
                    n = c * 2 + (r + 1)
                    dve.wait_ge(s_in, n * 4 - 3)
                    for t in range(2):
                        ins = ts_(cv[:, t, :], ps[:, 2 + t, 0:HALF], conv_x[:, t, TAP_BEFORE:TAP_BEFORE + 1], None, ALU.mult)
                    step.link(ins)
                    for t in range(2):
                        stt(cv[:, t, :], ps[:, 2 + t, HALF:BANK], conv_x[:, t, TAP_NOW:TAP_NOW + 1], cv[:, t, :],
                            ALU.mult, ALU.add).then_inc(s_cv, 1)
                    dve.wait_ge(s_in, n * 4 - 2)
                    for t in range(2):
                        ins = ts_(cvb[:, t, :], ps[0:DST, 4 + t, 0:HALF], conv_bc[:, t, TAP_BEFORE:TAP_BEFORE + 1], None, ALU.mult)
                    step.link(ins)
                    for t in range(2):
                        stt(cvb[:, t, :], ps[0:DST, 4 + t, HALF:BANK], conv_bc[:, t, TAP_NOW:TAP_NOW + 1], cvb[:, t, :],
                            ALU.mult, ALU.add).then_inc(s_cv, 1)
                    dve.wait_ge(s_bcs, n * 2)
                    tt_(BC[:], Bs[:], Cs[:], ALU.mult).then_inc(s_bcp, 1)
                    dve.wait_ge(s_sp, n)
                    for t in range(2):
                        ins = ts_(dts[:, t, :], ps[:, 6 + t, :], dt_bias[:, t:t + 1], 0.0, ALU.add, ALU.max)
                    step.link(ins)
                    step.link(tt_(dts[:], dts[:], sp[:], ALU.add))
                    dve.wait_ge(s_xs, n * 2)
                    step.link(tt_(dts[:], dts[:], xs[:], ALU.mult))
                    dve.wait_ge(s_bc, n)
                    for t in range(2):
                        for d in range(2):
                            ins = tt_(yq[:, t, HALF * (1 - d):HALF * (2 - d)], dts[:, t, HALF * d:HALF * d + HALF],
                                      ps[:, 4, HALF * d:HALF * d + HALF], ALU.mult)
                    dve.wait_ge(s_fc, n)
                    for t in range(2):
                        ins = stt(yz[:, t, :], ps[:, 2 + t, :], D_col[:, t:t + 1], xs[:, t, :], ALU.add, ALU.mult)
                    step.link(ins)
                    step.link(tt_(yq[:], yq[:], yz[:], ALU.add))
                    dve.wait_ge(s_zs, n)
                    tt_(yz[:], yq[:], zs[:], ALU.mult).then_inc(s_yz, 1)
                    dve.wait_ge(s_rms, n)
                    dve.wait_ge(s_sq, n)
                    for t in range(2):
                        ins = stt(yz[:, t, :], yz[:, t, :], norm_w[:, t:t + 1], rms[:], ALU.mult, ALU.mult)
                    ins.then_inc(s_yn, 1)
                dve.wait_ge(s_hout, c * 2 + 2)
                step.link(ts_(hmix[:], hout[:, 1, :], alpha[:, 1:2], None, ALU.mult))
                step.link(stt(hmix[:], xm[:], alpha[:, 0:1], hmix[:], ALU.mult, ALU.add))
                tt_(hmix[:], hmix[:], xm[:], ALU.add).then_inc(s_hmix, 1)
                for tt in range(4):
                    dve.wait_ge(s_up, c * 4 + (tt + 1))
                    tt_(H[:, tt, :].rearrange("p (h n) -> p h n", h=2), ps[:, 2 * tt:2 * tt + 2, :],
                        H[:, tt, :].rearrange("p (h n) -> p h n", h=2), ALU.add).then_inc(s_h1, 1)
                    dve.wait_ge(s_h1, c * 4 + (tt + 1))
                    mean_var(tt)
                for tt in range(4):
                    normalise(tt, c * 8 + 4)
                for tt in range(4):
                    dve.wait_ge(s_rt, c * 4 + (tt + 1))
                    step.link(nc.vector.tensor_copy(rt[:, tt, :], ps[:, 2 * tt, ER:ER + EXPERTS]))
                    apart(dve, s_apart_dve)
                    step.link(nc.vector.max(top[:, tt, :], rt[:, tt, :]))
                    tt_(r2[:, tt, 0:1], top[:, tt, 1:2], top[:, tt, 0:1], ALU.subtract).then_inc(s_gap, 1)
                    step.link(nc.vector.max_index(topi[:, tt, :], top[:, tt, :], rt[:, tt, :]))
                    nc.vector.tensor_copy(r2[:, tt, 5:7], topi[:, tt, 0:2])
                    dve.wait_ge(s_e2, c * 4 + (tt + 1))
                    step.link(ts_(r2[:, tt, 2:3], r2[:, tt, 1:2], 1.0, None, ALU.add))
                    step.link(nc.vector.reciprocal(r2[:, tt, 3:4], r2[:, tt, 2:3]))
                    step.link(tt_(r2[:, tt, 4:5], r2[:, tt, 1:2], r2[:, tt, 3:4], ALU.mult))
                    for j in range(2):
                        ins = ts_(wd[:, tt % 2, j, :], iota[:], r2[:, tt, 5 + j:6 + j], r2[:, tt, 3 + j:4 + j],
                                  ALU.is_equal, ALU.mult)
                    step.link(ins)
                    step.link(tt_(wd[:, tt % 2, 0, :], wd[:, tt % 2, 0, :], wd[:, tt % 2, 1, :], ALU.add))
                    if tt >= 2:
                        dve.wait_ge(s_midt, c * 4 + (tt - 1))
                    stt(mid[:, tt % 2, :, :], ps[:, 2 * tt, 0:ER].rearrange("p (e r) -> p e r", r=RANK), LORA_SCALE,
                        wd[:, tt % 2, 0, :].unsqueeze(2).to_broadcast([P, EXPERTS, RANK]), ALU.mult, ALU.mult)\
                        .then_inc(s_mid, 1)
                for tt in range(4):
                    dve.wait_ge(s_base, c * 4 + (tt + 1))
                    tt_(H[:, tt, :].rearrange("p (h n) -> p h n", h=2), ps[:, 2 * tt:2 * tt + 2, :],
                        H[:, tt, :].rearrange("p (h n) -> p h n", h=2), ALU.add).then_inc(s_h2, 1)
            step.leave(CHUNKS)


I8 = mybir.dt.int8
DI = 2048
DT = DI // P
NS = 16
DT_RANK = 64
B_ROW, C_ROW, SSM = 64, 96, 112
TAPS = 4
RMS_EPS = 1e-6
UNITS = TOK // BANK
COLS = TAPS + 3 + NS
DA, HB, DL, YB = 0, 2, 6, 7


def layer1(nc, a, h_dram, out):
    with ExitStack() as ctx:
        def sb(name, shape, dt=FP):
            return ctx.enter_context(nc.sbuf_tensor(name, shape, dt))

        def sem(name):
            return ctx.enter_context(nc.semaphore(name))

        ident = sb("l1_ident", [P, P])
        block1 = sb("l1_block1", [SSM, SSM])
        eps5 = sb("l1_eps5", [P, 1])
        eps6 = sb("l1_eps6", [P, 1])
        rlen = sb("l1_rlen", [SSM, 1])
        cols = sb("l1_cols", [P, DT, COLS])
        ln_w = sb("l1_ln_w", [SSM, 1])
        w_dt = sb("l1_w_dt", [DT_RANK, P])
        w_x = sb("l1_w_x", [P, DT, SSM])
        state = sb("l1_state", [P, DT, NS])
        halo = sb("l1_halo", [P, DT, TAPS - 1])
        ssm = sb("l1_ssm", [SSM, BANK])
        rep = sb("l1_rep", [P, 2 * NS, BANK])
        u = sb("l1_u", [P, DT, BANK])
        sg = sb("l1_sg", [P, DT, BANK])
        s1 = sb("l1_s1", [P, KT, BANK])
        s2 = sb("l1_s2", [P, 4, HID])
        s3 = sb("l1_s3", [P, 4, BANK])
        up = sb("l1_up", [P, TAPS - 1 + BANK])
        acc = sb("l1_acc", [P, 2, BANK])
        tern = sb("l1_tern", [P, 2, HID], I8)
        stats = sb("l1_stats", [P, 4, 2, 6])
        mv = sb("l1_mv", [P, 4, 2])
        lnv = sb("l1_lnv", [P, 4])
        rstd = sb("l1_rstd", [P, 4])
        ps = ctx.enter_context(nc.psum_tensor("l1_ps", [P, 8, BANK], FP))
        H = sg[:, 0:8, :].rearrange("p (t h) n -> p t (h n)", h=2)
        xT = s1
        dBu = s1[:, :, :].rearrange("p (g n) t -> p g n t", n=4)
        ring = s2
        g = s2[:, 0:2, :].rearrange("p g (n t) -> p g n t", n=2)
        spl = s2[:, 2, 0:BANK]
        dmax = s2[:, 2, BANK:]
        Xn = s3[:, :, :].rearrange("p (t h) n -> p t (h n)", h=2)
        raw, sqr, rr = s3[0:SSM, 0, :], s3[0:SSM, 1, :], s3[0:SSM, 2, :]
        delta, du = s3[:, 0:2, :], s3[:, 2:4, :]
        conv_w = cols[:, :, 0:TAPS]

        def column(j, n):
            return cols[:, bass.ds(j, 1), n:n + 1].rearrange("p a n -> p (a n)")

        CONV_B, DT_B, D_P, A_0 = TAPS, TAPS + 1, TAPS + 2, TAPS + 3

        def tile(t, j):
            return t[:, bass.ds(j, 1), :].rearrange("p a n -> p (a n)")

        s_const = sem("l1_const")
        s_w = sem("l1_weights")
        s_hl = sem("l1_hl")
        s_var = sem("l1_var")
        s_rstd = sem("l1_rstd")
        s_x = sem("l1_x")
        s_xt = sem("l1_xt")
        s_xT = sem("l1_xT")
        s_winu = sem("l1_win_u")
        s_wing = sem("l1_win_g")
        s_pu = sem("l1_pu")
        s_pg = sem("l1_pg")
        s_up = sem("l1_up_in")
        s_conv = sem("l1_conv")
        s_halo = sem("l1_halo_s")
        s_u = sem("l1_u_s")
        s_sg = sem("l1_sg_s")
        s_ssm = sem("l1_ssm_p")
        s_sqr = sem("l1_sqr")
        s_raw = sem("l1_raw")
        s_ms = sem("l1_ms")
        s_rr = sem("l1_rr")
        s_ssmn = sem("l1_ssmn")
        s_bp = sem("l1_bp")
        s_repa = sem("l1_rep_act")
        s_repd = sem("l1_rep_dve")
        s_wdt = sem("l1_wdt")
        s_dl = sem("l1_dl")
        s_spl = sem("l1_spl")
        s_delta = sem("l1_delta")
        s_du = sem("l1_du")
        s_dBu = sem("l1_dBu")
        s_dA = sem("l1_dA")
        s_scan = sem("l1_scan")
        s_save = sem("l1_save")
        s_g = sem("l1_g")
        s_sum = sem("l1_sum")
        s_yt = sem("l1_yt")
        s_y = sem("l1_y")
        s_wout = [sem(f"l1_wout{n}") for n in range(4)]
        s_po = sem("l1_po")
        s_h3 = sem("l1_h3")
        s_tern = [sem(f"l1_tern{n}") for n in range(2)]
        s_wf = sem("l1_wf")
        s_pf = sem("l1_pf")
        s_h4 = sem("l1_h4")
        s_out = sem("l1_out")
        s_act = sem("l1_act_steps")
        s_dve = sem("l1_dve_steps")
        s_apart = sem("l1_apart")
        s_apart_sp = sem("l1_apart_sp")

        block = ctx.enter_context(nc.Block())

        def rows(dram, K, t):
            return dram[bass.ds(K * BANK + t * P, P), :]

        @block.sync
        def _(sp):
            for dst, name in ((cols, "cols"), (ln_w, "ln_w"), (w_x, "w_x")):
                sp.dma_start(dst[:], a[name]).then_inc(s_w, 16)
            with sp.Fori(0, 2) as b:
                for hf in range(2):
                    K = b * 2 + hf
                    for t in range(4):
                        sp.dma_start(H[:, t, :], rows(h_dram, K, t)).then_inc(s_hl, 16)
                    with sp.Fori(0, DT) as j:
                        sp.wait_ge(s_pu, K * DT + (j + 1))
                        sp.dma_start(ring[:, 0, :], a["w_in"][bass.ds(j, 1), :, :].rearrange("a p n -> p (a n)")).then_inc(s_winu, 16)
                        sp.wait_ge(s_pg, K * DT + (j + 1))
                        sp.dma_start(ring[:, 1, :], a["w_in"][bass.ds(j + DT, 1), :, :].rearrange("a p n -> p (a n)")).then_inc(s_wing, 16)
                    with sp.Fori(0, DT) as j:
                        sp.wait_ge(s_dl, K * DT + (j + 1))
                        sp.dma_start(w_dt[:], a["w_dt"][bass.ds(j, 1), :, :].rearrange("a p n -> p (a n)")).then_inc(s_wdt, 16)
                    sp.wait_ge(s_y, K * DT + DT)
                    for t in range(4):
                        sp.dma_start(H[:, t, :], rows(h_dram, K, t)).then_inc(s_hl, 16)
                    for j in range(DT):
                        if j >= 4:
                            sp.wait_ge(s_po, K * DT + (j - 3))
                        sp.dma_start(ring[:, j % 4, :], a["w_out"][j, :, :]).then_inc(s_wout[j % 4], 16)
                    sp.wait_ge(s_po, K * DT + DT)
                    for k in range(KT):
                        if k >= 2:
                            sp.wait_ge(s_wf, K * KT + (k - 1))
                        sp.dma_start(tern[:, k % 2, :].bitcast(I32), a["tern"][k, :, :]).then_inc(s_tern[k % 2], 16)
                        sp.dma_start(ring[:, 2 + k % 2, :], a["scales"][k, :].partition_broadcast(P)).then_inc(s_tern[k % 2], 16)
                    for t in range(4):
                        sp.wait_ge(s_h4, K * 4 + (t + 1))
                        sp.dma_start(rows(out, K, t), H[:, t, :]).then_inc(s_out, 16)
                    sp.wait_ge(s_out, K * 64 + 64)
                    apart(sp, s_apart_sp)

        @block.gpsimd
        def _(pool):
            identity(nc, pool, ident[:], s_const)
            nc.gpsimd.memset(eps5[:], LN_EPS).then_inc(s_const, 1)
            nc.gpsimd.memset(eps6[:], RMS_EPS).then_inc(s_const, 1)
            nc.gpsimd.memset(block1[:], 0.0).then_inc(s_const, 1)
            pool.wait_ge(s_const, 5)
            for r0, r1, n in ((0, DT_RANK, DT_RANK), (B_ROW, C_ROW, NS), (C_ROW, SSM, NS)):
                nc.gpsimd.memset(block1[r0:r1, r0:r1], 1.0).then_inc(s_const, 1)
                nc.gpsimd.memset(rlen[r0:r1, :], 1.0 / n).then_inc(s_const, 1)

            def gated(j, done):
                pool.wait_ge(s_yt, done + 1)
                nc.gpsimd.tensor_tensor(tile(u, j), tile(u, j), tile(sg, j), ALU.mult).then_inc(s_y, 1)

            def states(K, j, par, first=False):
                m = K * DT + j
                pool.wait_ge(s_delta, m + 1)
                nc.gpsimd.tensor_tensor(du[:, par, :], delta[:, par, :], tile(u, j), ALU.mult).then_inc(s_du, 1)
                pool.wait_ge(s_du, m + 1)
                for q in range(4):
                    G = m * 4 + q
                    pool.wait_ge(s_scan, G * 4 + 4)
                    nc.gpsimd.tensor_tensor(dBu[:, q % 2, :, :], du[:, par, :].unsqueeze(1).to_broadcast([P, 4, BANK]),
                                            rep[:, 4 * q:4 * q + 4, :], ALU.mult).then_inc(s_dBu, 1)
                    if q == 1 and not first:
                        gated(j - 1, m)

            with pool.Fori(0, 2) as b:
                for hf in range(2):
                    K = b * 2 + hf
                    pool.wait_ge(s_sg, K * DT + DT)
                    pool.wait_ge(s_repa, K * NS + NS)
                    pool.wait_ge(s_repd, K * NS + NS)
                    states(K, 0, 0, first=True)
                    states(K, 1, 1)
                    with pool.Fori(1, DT // 2) as jj:
                        for par in range(2):
                            states(K, jj * 2 + par, par)
                    gated(DT - 1, K * DT + DT)

        @block.tensor
        def _(pe):
            pe.sem_inc(s_pu, 1)
            pe.sem_inc(s_pg, 1)
            pe.sem_inc(s_sum, 2)
            pe.sem_inc(s_dl, 1)
            pe.wait_ge(s_const, 11)
            pe.wait_ge(s_w, 16 * 3)

            def transposes(t, done):
                pe.wait_ge(s_x, done + (t + 1))
                for h in range(2):
                    for q in range(4):
                        k = 4 * h + q
                        ins = nc.tensor.transpose(ps[:, 2 * t + h, P * q:P * q + P],
                                                  Xn[:, t % 2, P * k:P * k + P], ident[:])
                    ins.then_inc(s_xt, 1)

            def product(out_, parts):
                for n, (lhsT, rhs) in enumerate(parts):
                    ins = nc.tensor.matmul(out_, lhsT, rhs, start=(n == 0), stop=(n == len(parts) - 1))
                return ins

            def dt_product(K, j, first=False):
                m = K * DT + j
                if not first:
                    pe.wait_ge(s_delta, m)
                pe.wait_ge(s_wdt, m * 16 + 16)
                product(ps[:, DL, :], [(w_dt[:], ssm[0:DT_RANK, :])]).then_inc(s_dl, 1)

            def y_sums(K, j, last=False):
                m = K * DT + j
                for p in range(8):
                    pe.wait_ge(s_g, m * 8 + (p + 1))
                    if p == 0:
                        pe.wait_ge(s_yt, m + 1)
                    for n in range(2):
                        ins = nc.tensor.matmul(ps[:, YB, :], ident[:], g[:, p % 2, n, :],
                                               start=(p == 0 and n == 0), stop=(p == 7 and n == 1))
                    ins.then_inc(s_sum, 1)
                    if p == 2 and not last:
                        dt_product(K, j + 1)

            with pe.Fori(0, 2) as b:
                for hf in range(2):
                    K = b * 2 + hf
                    for t in range(4):
                        transposes(t, K * 8)
                    pe.wait_ge(s_xT, K * 16 + 8)
                    apart(pe, s_apart)
                    with pe.Fori(0, DT) as j:
                        m = K * DT + j
                        pe.wait_ge(s_winu, m * 16 + 16)
                        pe.wait_ge(s_up, m + 1)
                        product(ps[:, 0, :], [(ring[:, 0, P * k:P * k + P], xT[:, k, :]) for k in range(KT)]).then_inc(s_pu, 1)
                        pe.wait_ge(s_wing, m * 16 + 16)
                        pe.wait_ge(s_sg, m + 1)
                        product(ps[:, 1, :], [(ring[:, 1, P * k:P * k + P], xT[:, k, :]) for k in range(KT)]).then_inc(s_pg, 1)
                    pe.wait_ge(s_u, K * DT + DT)
                    product(ps[0:SSM, 2, :], [(w_x[:, j, :], u[:, j, :]) for j in range(DT)]).then_inc(s_ssm, 1)
                    pe.wait_ge(s_sqr, K + 1)
                    product(ps[0:SSM, 3, :], [(block1[:], sqr)]).then_inc(s_ms, 1)
                    pe.wait_ge(s_ssmn, K + 1)
                    for n in range(2 * NS):
                        if n >= 4:
                            s = s_repd if n % 2 else s_repa
                            pe.wait_ge(s, K * NS + (n - 4) // 2 + 1)
                        r0 = B_ROW if n < NS else C_ROW
                        product(ps[:, 4 + n % 4, :], [(ident[r0:r0 + NS, r0 + n % NS:r0 + n % NS + 1].to_broadcast([NS, P]),
                                                       ssm[r0:r0 + NS, :])]).then_inc(s_bp, 1)
                    pe.wait_ge(s_repa, K * NS + NS)
                    pe.wait_ge(s_repd, K * NS + NS)
                    dt_product(K, 0, first=True)
                    with pe.Fori(0, DT - 1) as j:
                        y_sums(K, j)
                    y_sums(K, DT - 1, last=True)
                    pe.wait_ge(s_y, K * DT + DT)
                    for j in range(DT):
                        pe.wait_ge(s_wout[j % 4], K * 64 + (j // 4 * 16 + 16))
                        for t in range(4):
                            for h in range(2):
                                ins = nc.tensor.matmul(ps[:, 2 * t + h, :], u[:, j, P * t:P * t + P],
                                                       ring[:, j % 4, BANK * h:BANK * h + BANK],
                                                       start=(j == 0), stop=(j == DT - 1))
                        ins.then_inc(s_po, 1)
                    for t in range(4):
                        transposes(t, K * 8 + 4)
                    pe.wait_ge(s_xT, K * 16 + 16)
                    for k in range(KT):
                        pe.wait_ge(s_wf, K * KT + (k + 1))
                        for t in range(4):
                            for h in range(2):
                                ins = nc.tensor.matmul(ps[:, 2 * t + h, :], xT[:, k, P * t:P * t + P],
                                                       ring[:, k % 2, BANK * h:BANK * h + BANK],
                                                       start=(k == 0), stop=(k == KT - 1))
                        ins.then_inc(s_pf, 1)

        @block.scalar
        def _(act):
            act.wait_ge(s_const, 11)
            act.wait_ge(s_w, 16 * 3)
            act.sem_inc(s_up, 1)
            act.sem_inc(s_sg, 1)
            step = Steps(act, s_act)

            def inverse_std(t, done):
                act.wait_ge(s_var, done + (t + 1))
                step.link(nc.scalar.activation(lnv[:, t:t + 1], mv[:, t, 1:2], ACT.Ln, bias=eps5[:]))
                nc.scalar.activation(rstd[:, t:t + 1], lnv[:, t:t + 1], ACT.Exp, scale=-0.5).then_inc(s_rstd, 1)

            def transposed(t, done):
                for h in range(2):
                    act.wait_ge(s_xt, done + (2 * t + h + 1))
                    nc.scalar.activation(xT[:, 4 * h:4 * h + 4, P * t:P * t + P],
                                         ps[:, 2 * t + h, :].rearrange("p (k t) -> p k t", t=P), ACT.Copy)\
                        .then_inc(s_xT, 1)

            def softplus(K, j):
                act.wait_ge(s_dl, K * DT + j + 2)
                step.link(nc.scalar.activation(spl, ps[:, DL, :], ACT.Abs, bias=column(j, DT_B)))
                step.link(nc.scalar.activation(spl, spl, ACT.Exp, scale=-1.0))
                nc.scalar.activation(spl, spl, ACT.Ln, bias=1.0).then_inc(s_spl, 1)

            def decays(K, j, par, last=False):
                m = K * DT + j
                act.wait_ge(s_delta, m + 1)
                for n in range(NS):
                    act.wait_ge(s_scan, m * NS + (n + 7))
                    nc.scalar.activation(ps[:, DA + n % 2, :], delta[:, par, :], ACT.Exp, scale=column(j, A_0 + n))\
                        .then_inc(s_dA, 1)
                    if n == 9 and not last:
                        softplus(K, j + 1)

            with act.Fori(0, 2) as b:
                step.enter(b, 2 * (2 * 4 + 1 + 2 * DT))
                for hf in range(2):
                    K = b * 2 + hf
                    for t in range(4):
                        inverse_std(t, K * 8)
                        transposed(t, K * 16)
                    with act.Fori(0, DT) as j:
                        m = K * DT + j
                        act.wait_ge(s_pu, m + 2)
                        act.wait_ge(s_halo, m + 1)
                        nc.scalar.activation(up[:, TAPS - 1:], ps[:, 0, :], ACT.Copy).then_inc(s_up, 1)
                        act.wait_ge(s_pg, m + 2)
                        nc.scalar.activation(tile(sg, j), ps[:, 1, :], ACT.Silu).then_inc(s_sg, 1)
                        act.wait_ge(s_conv, m + 1)
                        nc.scalar.activation(tile(u, j), acc[:, 0, :], ACT.Silu, bias=column(j, CONV_B)).then_inc(s_u, 1)
                    act.wait_ge(s_ssm, K + 1)
                    nc.scalar.activation(sqr, ps[0:SSM, 2, :], ACT.Square).then_inc(s_sqr, 1)
                    act.wait_ge(s_ms, K + 1)
                    step.link(nc.scalar.activation(rr, ps[0:SSM, 3, :], ACT.Ln, scale=rlen[:], bias=eps6[0:SSM, :]))
                    nc.scalar.activation(rr, rr, ACT.Exp, scale=-0.5).then_inc(s_rr, 1)
                    for n in range(0, 2 * NS, 2):
                        act.wait_ge(s_bp, K * 2 * NS + (n + 1))
                        nc.scalar.activation(rep[:, n, :], ps[:, 4 + n % 4, :], ACT.Copy).then_inc(s_repa, 1)
                    softplus(K, 0)
                    at, reg = step.at, step.reg
                    with act.Fori(0, DT // 2 - 1) as jj:
                        step.reg = reg + jj * 4
                        for par in range(2):
                            decays(K, jj * 2 + par, par)
                    assert step.at == at + 4
                    step.reg, step.at = reg, at + 4 * (DT // 2 - 1)
                    decays(K, DT - 2, 0)
                    decays(K, DT - 1, 1, last=True)
                    for t in range(4):
                        inverse_std(t, K * 8 + 4)
                        transposed(t, K * 16 + 8)
            step.leave(2)

        @block.vector
        def _(dve):
            dve.sem_inc(s_scan, 8)
            dve.sem_inc(s_yt, 1)
            dve.wait_ge(s_const, 11)
            dve.wait_ge(s_w, 16 * 3)
            step = Steps(dve, s_dve)
            tt_, ts_, stt = nc.vector.tensor_tensor, nc.vector.tensor_scalar, nc.vector.scalar_tensor_tensor

            def mean_var(t):
                for h in range(2):
                    ins = nc.vector.bn_stats(stats[:, t, h, :], H[:, t, BANK * h:BANK * h + BANK])
                step.link(ins)
                apart(dve, s_apart)
                nc.vector.bn_aggr(mv[:, t, :], stats[:, t, :, :]).then_inc(s_var, 1)

            def normalise(t, done, halves):
                dve.wait_ge(s_rstd, done + (t + 1))
                if t >= 2:
                    dve.wait_ge(s_xt, halves + (2 * t - 2))
                ts_(Xn[:, t % 2, :], H[:, t, :], mv[:, t, 0:1], rstd[:, t:t + 1], ALU.subtract, ALU.mult)\
                    .then_inc(s_x, 1)

            def make_delta(K, j, par):
                m = K * DT + j
                dve.wait_ge(s_spl, m + 1)
                step.link(ts_(dmax, ps[:, DL, :], column(j, DT_B), 0.0, ALU.add, ALU.max))
                tt_(delta[:, par, :], dmax, spl, ALU.add).then_inc(s_delta, 1)

            def finish_y(K, j):
                m = K * DT + j
                dve.wait_ge(s_sum, m * 8 + 10)
                stt(tile(u, j), tile(u, j), column(j, D_P), ps[:, YB, :], ALU.mult, ALU.add).then_inc(s_yt, 1)

            def scan_tile(K, j, par, hf, first=False, last=False):
                m = K * DT + j

                def scan(n):
                    q = m * NS + n
                    dve.wait_ge(s_dA, q + 1)
                    if n % 4 == 0:
                        dve.wait_ge(s_dBu, m * 4 + (n // 4 + 1))
                    if n % 2 == 0:
                        if not (first and n < 4):
                            dve.wait_ge(s_g, m * 8 + (n // 2 - 1))
                            if hf == 0:
                                dve.wait_ge(s_save, b_ * (DT * 8) + j * 8 + (n // 2 - 1))
                    init = state[:, bass.ds(j, 1), n:n + 1].rearrange("p a n -> p (a n)") if hf else 0.0
                    nc.vector.tensor_tensor_scan(ps[:, HB + n % 4, :], ps[:, DA + n % 2, :],
                                                 dBu[:, (n // 4) % 2, n % 4, :], init, ALU.mult, ALU.add)\
                        .then_inc(s_scan, 1)

                def times_c(p):
                    dve.wait_ge(s_scan, m * NS + (2 * p + 2 + 8))
                    dve.wait_ge(s_sum, m * 8 + (p + 1))
                    h2 = ps[:, HB + 2 * (p % 2):HB + 2 * (p % 2) + 2, :]
                    tt_(g[:, p % 2, :, :], h2, rep[:, NS + 2 * p:NS + 2 * p + 2, :], ALU.mult).then_inc(s_g, 1)
                    if hf == 0:
                        nc.vector.tensor_copy(state[:, bass.ds(j, 1), 2 * p:2 * p + 2],
                                              h2[:, :, BANK - 1:BANK].rearrange("p n a -> p a n")).then_inc(s_save, 1)

                for p in range(8):
                    scan(2 * p)
                    scan(2 * p + 1)
                    if p:
                        times_c(p - 1)
                    if p == 1 and not first:
                        finish_y(K, j - 1)
                    if p == 6 and not last:
                        make_delta(K, j + 1, 1 - par)
                times_c(7)

            with dve.Fori(0, 2) as b:
                step.enter(b, 2 * (2 * 4 + (TAPS - 1) * DT + DT))
                for hf in range(2):
                    b_ = b
                    K = b * 2 + hf
                    dve.wait_ge(s_hl, K * 128 + 64)
                    for t in range(4):
                        mean_var(t)
                        if t:
                            normalise(t - 1, K * 8, K * 16)
                    normalise(3, K * 8, K * 16)
                    at, reg = step.at, step.reg
                    with dve.Fori(0, DT) as j:
                        step.reg = reg + j * (TAPS - 1)
                        m = K * DT + j
                        edge = up[:, 0:TAPS - 1]
                        if hf:
                            nc.vector.tensor_copy(edge, tile(halo, j)).then_inc(s_halo, 1)
                        else:
                            nc.vector.memset(edge, 0.0).then_inc(s_halo, 1)
                        dve.wait_ge(s_up, m + 2)
                        dve.wait_ge(s_halo, m + 1)
                        step.link(ts_(acc[:, 1, :], up[:, 0:BANK], column(j, 0), None, ALU.mult))
                        step.link(stt(acc[:, 1, :], up[:, 1:1 + BANK], column(j, 1), acc[:, 1, :], ALU.mult, ALU.add))
                        step.link(stt(acc[:, 1, :], up[:, 2:2 + BANK], column(j, 2), acc[:, 1, :], ALU.mult, ALU.add))
                        if not hf:
                            nc.vector.tensor_copy(tile(halo, j), up[:, BANK:BANK + TAPS - 1])
                        stt(acc[:, 0, :], up[:, 3:3 + BANK], column(j, 3), acc[:, 1, :], ALU.mult, ALU.add).then_inc(s_conv, 1)
                    assert step.at == at + TAPS - 1
                    step.reg, step.at = reg, at + (TAPS - 1) * DT
                    dve.wait_ge(s_sqr, K + 1)
                    ts_(raw, ps[0:SSM, 2, :], ln_w[:], None, ALU.mult).then_inc(s_raw, 1)
                    dve.wait_ge(s_raw, K + 1)
                    dve.wait_ge(s_rr, K + 1)
                    tt_(ssm[:], raw, rr, ALU.mult).then_inc(s_ssmn, 1)
                    for n in range(1, 2 * NS, 2):
                        dve.wait_ge(s_bp, K * 2 * NS + (n + 1))
                        nc.vector.tensor_copy(rep[:, n, :], ps[:, 4 + n % 4, :]).then_inc(s_repd, 1)
                    dve.wait_ge(s_repa, K * NS + NS)
                    make_delta(K, 0, 0)
                    scan_tile(K, 0, 0, hf, first=True)
                    at, reg = step.at, step.reg
                    with dve.Fori(0, DT // 2 - 1) as jj:
                        step.reg = reg + jj * 2
                        scan_tile(K, jj * 2 + 1, 1, hf)
                        scan_tile(K, jj * 2 + 2, 0, hf)
                    assert step.at == at + 2
                    step.reg, step.at = reg, at + 2 * (DT // 2 - 1)
                    scan_tile(K, DT - 1, 1, hf, last=True)
                    finish_y(K, DT - 1)
                    dve.wait_ge(s_po, K * DT + DT)
                    dve.wait_ge(s_hl, K * 128 + 128)
                    for t in range(4):
                        Ht = H[:, t, :].rearrange("p (h n) -> p h n", h=2)
                        tt_(Ht, ps[:, 2 * t:2 * t + 2, :], Ht, ALU.add).then_inc(s_h3, 1)
                        dve.wait_ge(s_h3, K * 4 + (t + 1))
                        mean_var(t)
                        if t:
                            normalise(t - 1, K * 8 + 4, K * 16 + 8)
                    normalise(3, K * 8 + 4, K * 16 + 8)
                    for k in range(KT):
                        dve.wait_ge(s_tern[k % 2], K * 128 + (k // 2 * 32 + 32))
                        if k >= 2:
                            dve.wait_ge(s_pf, K * KT + (k - 1))
                        tt_(ring[:, k % 2, :], tern[:, k % 2, :], ring[:, 2 + k % 2, :], ALU.mult).then_inc(s_wf, 1)
                    dve.wait_ge(s_pf, K * KT + KT)
                    for t in range(4):
                        Ht = H[:, t, :].rearrange("p (h n) -> p h n", h=2)
                        tt_(Ht, ps[:, 2 * t:2 * t + 2, :], Ht, ALU.add).then_inc(s_h4, 1)
            step.leave(2)


def layouts(x, L0_tok_W, L0_tok_b, L0_attn_w_down, L0_attn_b_down, L0_attn_w_up, L0_attn_b_up, L0_attn_gate1,
            L0_attn_hy_in_w, L0_attn_hy_conv_w, L0_attn_hy_conv_b, L0_attn_hy_dt_bias, L0_attn_hy_D,
            L0_attn_hy_fcD_w, L0_attn_hy_norm_w, L0_attn_hy_out_w, L0_ffn_base_W, L0_ffn_router_W,
            L0_ffn_lora_A, L0_ffn_lora_B, **rest):
    import numpy as np

    P, DIN, DST, HD = 128, 256, 16, 64

    def k_tiles(w_t):
        return w_t.reshape(-1, P, w_t.shape[1]).transpose(1, 0, 2)

    def channels(v):
        return v.reshape((-1, P) + v.shape[1:]).swapaxes(0, 1)

    o = {}
    o["x"] = x
    o["tok_W"] = L0_tok_W.T
    o["tok_b"] = L0_tok_b
    o["up_b"] = L0_attn_b_up
    o["w_down"] = k_tiles(L0_attn_w_down.T)
    o["w_up"] = L0_attn_w_up.T
    o["w_base"] = k_tiles(L0_ffn_base_W.T)
    lora_a = L0_ffn_lora_A.transpose(1, 0, 2).reshape(1024, 128)
    o["w_lora"] = k_tiles(np.concatenate([lora_a, L0_ffn_router_W.T], axis=1))
    o["w_lora_b"] = L0_ffn_lora_B.reshape(128, 1024)
    w = L0_attn_hy_in_w
    o["in_z"] = w[0:DIN].T
    o["in_x"] = w[DIN:2 * DIN].T
    o["in_bc"] = w[2 * DIN:2 * DIN + 2 * DST].T
    dt = w[2 * DIN + 2 * DST:].reshape(2, 4, P)
    o["in_dt"] = np.repeat(dt, HD, axis=1).transpose(2, 0, 1)
    o["w_fc"] = k_tiles(np.repeat(L0_attn_hy_fcD_w, HD, axis=0).T)
    o["w_hout"] = k_tiles(L0_attn_hy_out_w.T)
    o["col"] = np.concatenate(
        [L0_attn_b_down.reshape(P, 1), np.full((P, 1), L0_attn_gate1),
         channels(np.repeat(L0_attn_hy_dt_bias, HD)), channels(np.repeat(L0_attn_hy_D, HD)),
         channels(L0_attn_hy_norm_w)], axis=1).astype(L0_attn_b_down.dtype)
    conv = np.concatenate([L0_attn_hy_conv_w[:, 0, :], L0_attn_hy_conv_b[:, None]], axis=1)
    o["conv_x"] = channels(conv[:DIN])
    o["conv_bc"] = conv[DIN:].reshape(2, DST, 8).transpose(1, 0, 2)
    return o


def layouts1(L1_attn_W_in, L1_attn_conv_w, L1_attn_conv_b, L1_attn_Wx, L1_attn_dt_ln_w, L1_attn_b_ln_w,
             L1_attn_c_ln_w, L1_attn_Wdt, L1_attn_dt_bias, L1_attn_A, L1_attn_D_param, L1_attn_W_out,
             L1_ffn_ternary, L1_ffn_scales, **rest):
    import numpy as np

    P, DI, NS, RANK = 128, 2048, 16, 64
    f = L1_attn_W_in.dtype

    def channels(v):
        return v.reshape(-1, P, v.shape[1]).swapaxes(0, 1)

    def rows_padded(w):
        return np.concatenate([w[:RANK + NS], np.zeros((NS,) + w.shape[1:], f), w[RANK + NS:]], axis=0)

    o = {}
    o["w_in"] = L1_attn_W_in.reshape(2 * DI // P, P, 8, P).transpose(0, 3, 2, 1).reshape(2 * DI // P, P, 1024)
    o["w_x"] = rows_padded(L1_attn_Wx).T.reshape(DI // P, P, 112).swapaxes(0, 1)
    o["ln_w"] = rows_padded(np.concatenate([L1_attn_dt_ln_w, L1_attn_b_ln_w, L1_attn_c_ln_w])[:, None])
    o["w_dt"] = L1_attn_Wdt.reshape(DI // P, P, RANK).swapaxes(1, 2)
    o["cols"] = channels(np.concatenate([L1_attn_conv_w, L1_attn_conv_b[:, None], L1_attn_dt_bias[:, None],
                                         L1_attn_D_param[:, None], L1_attn_A], axis=1))
    o["w_out"] = L1_attn_W_out.T.reshape(DI // P, P, 1024)
    o["tern"] = np.ascontiguousarray(L1_ffn_ternary.T).view(np.int32).reshape(8, P, 256)
    o["scales"] = L1_ffn_scales.reshape(1024, 8).T
    return o


def tower(nc, a, out):
    h_dram = nc.dram_tensor("residual", (TOK, HID), FP).ap()
    layer0(nc, a, h_dram)
    layer1(nc, a, h_dram, out)


def kernel(**inputs):
    import numpy as np
    import concourse.bacc as bacc
    from concourse.bass_utils import run_bass_kernel_spmd

    inputs = {name: np.asarray(v) for name, v in inputs.items()}
    arrays = {name: np.ascontiguousarray(v) for name, v in {**layouts(**inputs), **layouts1(**inputs)}.items()}
    nc = bacc.Bacc("TRN2", target_bir_lowering=False, num_devices=1)
    a = {name: nc.dram_tensor(f"in_{name}", v.shape, mybir.dt.from_np(v.dtype), kind="ExternalInput").ap()
         for name, v in arrays.items()}
    out = nc.dram_tensor("out", (TOK, HID), FP, kind="ExternalOutput").ap()
    tower(nc, a, out)
    got = run_bass_kernel_spmd(nc, [{f"in_{name}": v for name, v in arrays.items()}], core_ids=[0])
    return got.results[0]["out"].reshape(2, ROW, HID)
```

```python
import concourse.bass as bass
from concourse import mybir
from contextlib import ExitStack

P = 128
FP = mybir.dt.float32
I32 = mybir.dt.int32
U32 = mybir.dt.uint32
ALU = mybir.AluOpType
ACT = mybir.ActivationFunctionType

HID = 1024
TOK = 2048
ROW = 1024
KT = HID // P
BANK = 512
LN_EPS = 1e-5

ORDER = 4
VOC1 = HID + 1
DIN = 256
DST = 16
TAP_NOW, TAP_BEFORE = 6, 5
EXPERTS, RANK = 8, 16
ER = EXPERTS * RANK
LORA_SCALE = 2.0
CHUNKS = 4
HALF = 256


class Steps:

    def __init__(self, engine, sem):
        self.engine, self.sem, self.at, self.reg = engine, sem, 0, None

    def value(self):
        return self.at if self.reg is None else self.reg + self.at

    def link(self, instruction):
        instruction.then_inc(self.sem, 1)
        self.at += 1
        self.engine.wait_ge(self.sem, self.value())

    def enter(self, i, per):
        self.start, self.per = self.at, per
        self.reg = i * per

    def leave(self, times):
        assert self.at - self.start == self.per, (self.at - self.start, self.per)
        self.reg, self.at = None, self.start + self.per * times


def apart(engine, sem):
    engine.sem_inc(sem, 1)


def identity(nc, pool, tile, sem):
    nc.gpsimd.memset(tile, 0.0).then_inc(sem, 1)
    pool.wait_ge(sem, 1)
    nc.gpsimd.affine_select(out=tile, in_=tile, compare_op=ALU.not_equal, fill=1.0, base=0,
                            pattern=[[-1, P]], channel_multiplier=1).then_inc(sem, 1)


def layer0(nc, a, h_dram):
    with ExitStack() as ctx:
        def sb(name, shape, dt=FP):
            return ctx.enter_context(nc.sbuf_tensor(name, shape, dt))

        def sem(name):
            return ctx.enter_context(nc.semaphore(name))

        ident = sb("l0_ident", [P, P])
        ones = sb("l0_ones", [P, P])
        iota_i = sb("l0_iota_i", [P, EXPERTS], I32)
        iota = sb("l0_iota", [P, EXPERTS])
        eps = sb("l0_eps", [P, 1])
        tok_b = sb("l0_tok_b", [P, HID])
        up_b = sb("l0_up_b", [P, HID])
        w_down = sb("l0_w_down", [P, KT, P])
        w_up = sb("l0_w_up", [P, HID])
        w_base = sb("l0_w_base", [P, KT, HID])
        w_lora = sb("l0_w_lora", [P, KT, ER + EXPERTS])
        w_lora_b = sb("l0_w_lora_b", [P, HID])
        in_z = sb("l0_in_z", [P, DIN])
        in_x = sb("l0_in_x", [P, DIN])
        in_bc = sb("l0_in_bc", [P, 2 * DST])
        in_dt = sb("l0_in_dt", [P, 2, DIN])
        w_fc = sb("l0_w_fc", [P, 2, DIN])
        w_out = sb("l0_w_out", [P, 2, P])
        col = sb("l0_col", [P, 8])
        conv_x = sb("l0_conv_x", [P, 2, 8])
        conv_bc = sb("l0_conv_bc", [DST, 2, 8])
        alpha = sb("l0_alpha", [P, 2])
        xi = sb("l0_xi", [16, ORDER, P], I32)
        xf = sb("l0_xf", [16, ORDER, P])
        idx = sb("l0_idx", [P, 16, ORDER], I32)
        idx_now = sb("l0_idx_now", [P, 4, ORDER], I32)
        emb = sb("l0_emb", [P, 2, ORDER, HID])
        H = sb("l0_H", [P, 4, HID])
        X = sb("l0_X", [P, 4, HID])
        xT = sb("l0_xT", [P, KT, BANK])
        stats = sb("l0_stats", [P, 4, 2, 6])
        mv = sb("l0_mv", [P, 4, 2])
        lnv = sb("l0_lnv", [P, 4])
        rstd = sb("l0_rstd", [P, 4])
        xm = sb("l0_xm", [P, BANK])
        hout = sb("l0_hout", [P, 2, BANK])
        hmix = sb("l0_hmix", [P, BANK])
        zs = sb("l0_zs", [P, 2, BANK])
        xs = sb("l0_xs", [P, 2, BANK])
        cv = sb("l0_cv", [P, 2, HALF])
        cvb = sb("l0_cvb", [DST, 2, HALF])
        Bs = sb("l0_Bs", [DST, BANK])
        Cs = sb("l0_Cs", [DST, BANK])
        BC = sb("l0_BC", [DST, BANK])
        sp = sb("l0_sp", [P, 2, BANK])
        dts = sb("l0_dts", [P, 2, BANK])
        yq = sb("l0_yq", [P, 2, BANK])
        yz = sb("l0_yz", [P, 2, BANK])
        sq = sb("l0_sq", [P, 2, BANK])
        rms = sb("l0_rms", [P, BANK])
        top = sb("l0_top", [P, 4, 8])
        topi = sb("l0_topi", [P, 4, 8], U32)
        rt = sb("l0_rt", [P, 4, 8])
        r2 = sb("l0_r2", [P, 4, 8])
        wd = sb("l0_wd", [P, 2, 2, EXPERTS])
        mid = sb("l0_mid", [P, 2, EXPERTS, RANK])
        midT = sb("l0_midT", [P, 2, P])
        ps = ctx.enter_context(nc.psum_tensor("l0_ps", [P, 8, BANK], FP))

        s_const = sem("l0_const")
        s_w = sem("l0_weights")
        s_wbig = sem("l0_weights_big")
        s_xi0 = sem("l0_xi_filled")
        s_xi = sem("l0_xi_loaded")
        s_xf = sem("l0_xf")
        s_ixT = sem("l0_ixT")
        s_idx = sem("l0_idx")
        s_now = sem("l0_idx_now")
        s_emb_free = sem("l0_emb_free")
        s_emb = [sem(f"l0_emb{n}") for n in range(2)]
        s_var = sem("l0_var")
        s_rstd = sem("l0_rstd")
        s_x = sem("l0_x")
        s_xt = sem("l0_xt")
        s_xT = sem("l0_xT")
        s_down = sem("l0_down")
        s_xm = sem("l0_xm")
        s_in = sem("l0_in")
        s_act = sem("l0_act_steps")
        s_dve = sem("l0_dve_steps")
        s_apart_dve = sem("l0_apart_dve")
        s_apart_pool = sem("l0_apart_pool")
        s_cv = sem("l0_cv")
        s_bcs = sem("l0_bcs")
        s_xs = sem("l0_xs")
        s_zs = sem("l0_zs")
        s_sp = sem("l0_sp")
        s_bcp = sem("l0_bcp")
        s_bc = sem("l0_bc")
        s_fc = sem("l0_fc")
        s_yz = sem("l0_yz")
        s_sq = sem("l0_sq")
        s_ms = sem("l0_ms")
        s_rms = sem("l0_rms")
        s_yn = sem("l0_yn")
        s_ho = sem("l0_ho")
        s_hout = sem("l0_hout")
        s_alpha = sem("l0_alpha")
        s_hmix = sem("l0_hmix")
        s_up = sem("l0_up")
        s_h1 = sem("l0_h1")
        s_rt = sem("l0_rt")
        s_gap = sem("l0_gap")
        s_e2 = sem("l0_e2")
        s_mid = sem("l0_mid")
        s_midt = sem("l0_midt")
        s_midT = sem("l0_midT")
        s_base = sem("l0_base")
        s_h2 = sem("l0_h2")
        s_store = [sem(f"l0_store{n}") for n in range(4)]

        b_down, gate = col[:, 0:1], col[:, 1:2]
        dt_bias, D_col, norm_w = col[:, 2:4], col[:, 4:6], col[:, 6:8]

        def rows(c, tt):
            return h_dram[bass.ds(c * HALF + ((tt // 2) * ROW + (tt % 2) * P), P), :]

        block = ctx.enter_context(nc.Block())

        @block.sync
        def _(sp_):
            sp_.wait_ge(s_xi0, 1)
            for k in range(ORDER):
                back = ORDER - 1 - k
                for b in range(2):
                    r0 = 8 * b
                    if back == 0:
                        sp_.dma_start(xi[r0:r0 + 8, k, :], a["x"][b, :].rearrange("(j p) -> j p", p=P)).then_inc(s_xi, 16)
                    else:
                        sp_.dma_start(xi[r0:r0 + 1, k, back:P], a["x"][b:b + 1, 0:P - back]).then_inc(s_xi, 16)
                        sp_.dma_start(xi[r0 + 1:r0 + 8, k, :],
                                      a["x"][b, P - back:ROW - back].rearrange("(j p) -> j p", p=P)).then_inc(s_xi, 16)
            sp_.dma_start(tok_b[:], a["tok_b"].partition_broadcast(P)).then_inc(s_w, 16)
            sp_.dma_start(up_b[:], a["up_b"].partition_broadcast(P)).then_inc(s_w, 16)
            for dst, name in ((in_z, "in_z"), (in_x, "in_x"), (in_bc, "in_bc"), (in_dt, "in_dt"),
                              (w_fc, "w_fc"), (w_out, "w_hout"), (col, "col"), (conv_x, "conv_x"),
                              (conv_bc, "conv_bc")):
                sp_.dma_start(dst[:], a[name]).then_inc(s_w, 16)
            for dst, name in ((w_down, "w_down"), (w_up, "w_up"), (w_lora, "w_lora"),
                              (w_lora_b, "w_lora_b"), (w_base, "w_base")):
                sp_.dma_start(dst[:], a[name]).then_inc(s_wbig, 16)
            for tt in range(4):
                sp_.sem_inc(s_store[tt], 16)
            with sp_.Fori(0, CHUNKS) as c:
                for tt in range(4):
                    sp_.wait_ge(s_h2, c * 4 + (tt + 1))
                    sp_.dma_start(rows(c, tt), H[:, tt, :]).then_inc(s_store[tt], 16)
            for tt in range(4):
                sp_.wait_ge(s_store[tt], 16 * (CHUNKS + 1))

        @block.gpsimd
        def _(pool):
            nc.gpsimd.memset(xi[:], HID).then_inc(s_xi0, 1)
            identity(nc, pool, ident[:], s_const)
            nc.gpsimd.memset(ones[:], 1.0).then_inc(s_const, 1)
            nc.gpsimd.memset(eps[:], LN_EPS).then_inc(s_const, 1)
            nc.gpsimd.iota(iota_i[:], pattern=[[1, EXPERTS]], base=0, channel_multiplier=0).then_inc(s_const, 1)
            pool.wait_ge(s_const, 5)
            nc.gpsimd.tensor_copy(iota[:], iota_i[:]).then_inc(s_const, 1)
            pool.wait_ge(s_idx, 1)
            with pool.Fori(0, CHUNKS) as c:
                for tt in range(4):
                    pool.wait_ge(s_emb_free, c * 4 + (tt + 1))
                    nc.gpsimd.tensor_copy(idx_now[:, tt, :],
                                          idx[:, bass.ds(c * 2 + (8 * (tt // 2) + tt % 2), 1), :]).then_inc(s_now, 1)
                    pool.wait_ge(s_now, c * 4 + (tt + 1))
                    apart(pool, s_apart_pool)
                    for k in range(ORDER):
                        nc.gpsimd.indirect_dma_start(
                            out=emb[:, tt % 2, k, :], out_offset=None, in_=a["tok_W"],
                            in_offset=bass.IndirectOffsetOnAxis(ap=idx_now[:, tt, k:k + 1], axis=0))\
                            .then_inc(s_emb[tt % 2], 16)

        @block.tensor
        def _(pe):
            pe.wait_ge(s_const, 2)
            pe.wait_ge(s_xf, 1)
            for k in range(ORDER):
                ins = nc.tensor.transpose(ps[:, 0, 16 * k:16 * k + 16], xf[:, k, :], ident[0:16, 0:16])
            ins.then_inc(s_ixT, 1)
            pe.wait_ge(s_idx, 1)
            pe.wait_ge(s_w, 16 * 11)
            pe.wait_ge(s_wbig, 16 * 5)

            def transposes(tt, base):
                pe.wait_ge(s_x, base + tt + 1)
                for h in range(2):
                    for q in range(4):
                        k = 4 * h + q
                        ins = nc.tensor.transpose(ps[:, 2 * tt + h, P * q:P * q + P],
                                                  X[:, tt, P * k:P * k + P], ident[:])
                    ins.then_inc(s_xt, 1)

            def product(out, parts):
                for n, (lhsT, rhs) in enumerate(parts):
                    ins = nc.tensor.matmul(out, lhsT, rhs, start=(n == 0), stop=(n == len(parts) - 1))
                return ins

            with pe.Fori(0, CHUNKS) as c:
                for tt in range(4):
                    transposes(tt, c * 8)
                pe.wait_ge(s_xT, c * 16 + 8)
                product(ps[:, 4, :], [(w_down[:, k, :], xT[:, k, :]) for k in range(KT)]).then_inc(s_down, 1)
                for r in range(2):
                    if r == 0:
                        pe.wait_ge(s_xm, c + 1)
                        u = xm
                    else:
                        pe.wait_ge(s_hout, c * 2 + 1)
                        u = hout[:, 0, :]
                    n = c * 2 + (r + 1)
                    for t in range(2):
                        ins = product(ps[:, 2 + t, :], [(in_x[:, P * t:P * t + P], u[:, :])])
                    ins.then_inc(s_in, 1)
                    for t in range(2):
                        ins = product(ps[0:DST, 4 + t, :], [(in_bc[:, DST * t:DST * t + DST], u[:, :])])
                    ins.then_inc(s_in, 1)
                    for t in range(2):
                        for d in range(2):
                            ins = product(ps[:, 6 + t, HALF * d:HALF * d + HALF],
                                          [(in_dt[:, d, P * t:P * t + P], u[:, HALF * d:HALF * d + HALF])])
                    ins.then_inc(s_in, 1)
                    for t in range(2):
                        ins = product(ps[:, t, :], [(in_z[:, P * t:P * t + P], u[:, :])])
                    ins.then_inc(s_in, 1)
                    pe.wait_ge(s_bcp, n)
                    product(ps[:, 4, :], [(ones[0:DST, :], BC[:])]).then_inc(s_bc, 1)
                    pe.wait_ge(s_xs, n * 2)
                    for t in range(2):
                        ins = product(ps[:, 2 + t, :], [(w_fc[:, k, P * t:P * t + P], xs[:, k, :]) for k in range(2)])
                    ins.then_inc(s_fc, 1)
                    pe.wait_ge(s_sq, n)
                    product(ps[:, 5, :], [(ones[:], sq[:, k, :]) for k in range(2)]).then_inc(s_ms, 1)
                    pe.wait_ge(s_yn, n)
                    product(ps[:, 6, :], [(w_out[:, k, :], yz[:, k, :]) for k in range(2)]).then_inc(s_ho, 1)
                pe.wait_ge(s_hmix, c + 1)
                for tt in range(4):
                    for h in range(2):
                        ins = product(ps[:, 2 * tt + h, :], [(hmix[:, P * tt:P * tt + P], w_up[:, BANK * h:BANK * h + BANK])])
                    ins.then_inc(s_up, 1)
                for tt in range(4):
                    transposes(tt, c * 8 + 4)
                for tt in range(4):
                    pe.wait_ge(s_xT, c * 16 + (8 + 2 * tt + 2))
                    product(ps[:, 2 * tt, 0:ER + EXPERTS],
                            [(xT[:, k, P * tt:P * tt + P], w_lora[:, k, :]) for k in range(KT)]).then_inc(s_rt, 1)
                for tt in range(4):
                    pe.wait_ge(s_mid, c * 4 + (tt + 1))
                    nc.tensor.transpose(ps[:, 2 * tt + 1, 0:P],
                                        mid[:, tt % 2, :, :].rearrange("p e r -> p (e r)"), ident[:]).then_inc(s_midt, 1)
                    pe.wait_ge(s_midT, c * 4 + (tt + 1))
                    for h in range(2):
                        ins = product(ps[:, 2 * tt + h, :],
                                      [(xT[:, k, P * tt:P * tt + P], w_base[:, k, BANK * h:BANK * h + BANK])
                                       for k in range(KT)]
                                      + [(midT[:, tt % 2, :], w_lora_b[:, BANK * h:BANK * h + BANK])])
                    ins.then_inc(s_base, 1)

        @block.scalar
        def _(act):
            act.wait_ge(s_const, 4)
            act.wait_ge(s_w, 16 * 11)
            step = Steps(act, s_act)
            step.link(nc.scalar.activation(alpha[:, 0:1], gate, ACT.Sigmoid))
            act.sem_inc(s_alpha, 1)

            def inverse_std(tt, base):
                act.wait_ge(s_var, base + tt + 1)
                step.link(nc.scalar.activation(lnv[:, tt:tt + 1], mv[:, tt, 1:2], ACT.Ln, bias=eps[:]))
                nc.scalar.activation(rstd[:, tt:tt + 1], lnv[:, tt:tt + 1], ACT.Exp, scale=-0.5).then_inc(s_rstd, 1)

            def transposed(tt, base):
                for h in range(2):
                    act.wait_ge(s_xt, base + (2 * tt + h + 1))
                    nc.scalar.activation(xT[:, 4 * h:4 * h + 4, P * tt:P * tt + P],
                                         ps[:, 2 * tt + h, :].rearrange("p (k t) -> p k t", t=P), ACT.Copy)\
                        .then_inc(s_xT, 1)

            with act.Fori(0, CHUNKS) as c:
                step.enter(c, 2 * 4 + 2 * (4 + 1))
                for tt in range(4):
                    inverse_std(tt, c * 8)
                for tt in range(4):
                    transposed(tt, c * 16)
                act.wait_ge(s_down, c + 1)
                nc.scalar.activation(xm[:], ps[:, 4, :], ACT.Gelu, bias=b_down).then_inc(s_xm, 1)
                for r in range(2):
                    n = c * 2 + (r + 1)
                    for t in range(2):
                        act.wait_ge(s_cv, n * 4 - 4 + (t + 1))
                        nc.scalar.activation(xs[:, t, 0:HALF], ps[:, 2 + t, 0:HALF], ACT.Silu,
                                             scale=conv_x[:, t, TAP_NOW:TAP_NOW + 1], bias=conv_x[:, t, 7:8])
                        nc.scalar.activation(xs[:, t, HALF:BANK], cv[:, t, :], ACT.Silu,
                                             bias=conv_x[:, t, 7:8]).then_inc(s_xs, 1)
                    for t, dst in ((0, Bs), (1, Cs)):
                        act.wait_ge(s_cv, n * 4 - 4 + (t + 3))
                        nc.scalar.activation(dst[:, 0:HALF], ps[0:DST, 4 + t, 0:HALF], ACT.Silu,
                                             scale=conv_bc[:, t, TAP_NOW:TAP_NOW + 1], bias=conv_bc[:, t, 7:8])
                        nc.scalar.activation(dst[:, HALF:BANK], cvb[:, t, :], ACT.Silu,
                                             bias=conv_bc[:, t, 7:8]).then_inc(s_bcs, 1)
                    act.wait_ge(s_in, n * 4)
                    nc.scalar.activation(zs[:], ps[:, 0:2, :], ACT.Silu).then_inc(s_zs, 1)
                    for t in range(2):
                        step.link(nc.scalar.activation(sp[:, t, :], ps[:, 6 + t, :], ACT.Abs, bias=dt_bias[:, t:t + 1]))
                    step.link(nc.scalar.activation(sp[:], sp[:], ACT.Exp, scale=-1.0))
                    nc.scalar.activation(sp[:], sp[:], ACT.Ln, bias=1.0).then_inc(s_sp, 1)
                    act.wait_ge(s_yz, n)
                    nc.scalar.activation(sq[:], yz[:], ACT.Square).then_inc(s_sq, 1)
                    act.wait_ge(s_ms, n)
                    step.link(nc.scalar.activation(rms[:], ps[:, 5, :], ACT.Ln, scale=1.0 / DIN, bias=eps[:]))
                    step.link(nc.scalar.activation(rms[:], rms[:], ACT.Exp, scale=-0.5))
                    act.sem_inc(s_rms, 1)
                    act.wait_ge(s_ho, n)
                    nc.scalar.activation(hout[:, r, :], ps[:, 6, :], ACT.Copy).then_inc(s_hout, 1)
                for tt in range(4):
                    inverse_std(tt, c * 8 + 4)
                for tt in range(4):
                    transposed(tt, c * 16 + 8)
                for tt in range(4):
                    act.wait_ge(s_gap, c * 4 + (tt + 1))
                    nc.scalar.activation(r2[:, tt, 1:2], r2[:, tt, 0:1], ACT.Exp).then_inc(s_e2, 1)
                for tt in range(4):
                    act.wait_ge(s_midt, c * 4 + (tt + 1))
                    nc.scalar.activation(midT[:, tt % 2, :], ps[:, 2 * tt + 1, 0:P], ACT.Copy).then_inc(s_midT, 1)
            step.leave(CHUNKS)

        @block.vector
        def _(dve):
            dve.sem_inc(s_emb_free, 2)
            step = Steps(dve, s_dve)
            tt_, ts_, stt = nc.vector.tensor_tensor, nc.vector.tensor_scalar, nc.vector.scalar_tensor_tensor
            dve.wait_ge(s_xi, 16 * 14)
            for k in range(ORDER):
                ins = ts_(xf[:, k, :], xi[:, k, :], float(k * VOC1), None, ALU.add)
            ins.then_inc(s_xf, 1)
            dve.wait_ge(s_ixT, 1)
            nc.vector.tensor_copy(idx[:].rearrange("p g k -> p k g"),
                                  ps[:, 0, 0:16 * ORDER].rearrange("p (k g) -> p k g", g=16)).then_inc(s_idx, 1)
            dve.wait_ge(s_const, 6)
            dve.wait_ge(s_w, 16 * 11)
            dve.wait_ge(s_alpha, 1)
            step.link(ts_(alpha[:, 1:2], alpha[:, 0:1], -1.0, 1.0, ALU.mult, ALU.add))

            def mean_var(tt):
                for h in range(2):
                    ins = nc.vector.bn_stats(stats[:, tt, h, :], H[:, tt, BANK * h:BANK * h + BANK])
                step.link(ins)
                apart(dve, s_apart_dve)
                nc.vector.bn_aggr(mv[:, tt, :], stats[:, tt, :, :]).then_inc(s_var, 1)

            def normalise(tt, base):
                dve.wait_ge(s_rstd, base + tt + 1)
                ts_(X[:, tt, :], H[:, tt, :], mv[:, tt, 0:1], rstd[:, tt:tt + 1], ALU.subtract, ALU.mult)\
                    .then_inc(s_x, 1)

            with dve.Fori(0, CHUNKS) as c:
                step.enter(c, 4 * 5 + 4 * 2 + 2 * 7 + 2 + 4 + 4 * 8)
                for tt in range(4):
                    dve.wait_ge(s_emb[tt % 2], c * (2 * ORDER * 16) + (tt // 2 + 1) * ORDER * 16)
                    dve.wait_ge(s_store[tt], c * 16 + 16)
                    step.link(tt_(H[:, tt, :], emb[:, tt % 2, 0, :], tok_b[:], ALU.add))
                    for k in range(1, ORDER):
                        step.link(tt_(H[:, tt, :], H[:, tt, :], emb[:, tt % 2, k, :], ALU.add))
                    dve.sem_inc(s_emb_free, 1)
                    mean_var(tt)
                for tt in range(4):
                    normalise(tt, c * 8)
                for tt in range(4):
                    dve.wait_ge(s_x, c * 8 + (tt + 1))
                    step.link(tt_(H[:, tt, :], H[:, tt, :], X[:, tt, :], ALU.add))
                    step.link(tt_(H[:, tt, :], H[:, tt, :], up_b[:], ALU.add))
                for r in range(2):
                    n = c * 2 + (r + 1)
                    dve.wait_ge(s_in, n * 4 - 3)
                    for t in range(2):
                        ins = ts_(cv[:, t, :], ps[:, 2 + t, 0:HALF], conv_x[:, t, TAP_BEFORE:TAP_BEFORE + 1], None, ALU.mult)
                    step.link(ins)
                    for t in range(2):
                        stt(cv[:, t, :], ps[:, 2 + t, HALF:BANK], conv_x[:, t, TAP_NOW:TAP_NOW + 1], cv[:, t, :],
                            ALU.mult, ALU.add).then_inc(s_cv, 1)
                    dve.wait_ge(s_in, n * 4 - 2)
                    for t in range(2):
                        ins = ts_(cvb[:, t, :], ps[0:DST, 4 + t, 0:HALF], conv_bc[:, t, TAP_BEFORE:TAP_BEFORE + 1], None, ALU.mult)
                    step.link(ins)
                    for t in range(2):
                        stt(cvb[:, t, :], ps[0:DST, 4 + t, HALF:BANK], conv_bc[:, t, TAP_NOW:TAP_NOW + 1], cvb[:, t, :],
                            ALU.mult, ALU.add).then_inc(s_cv, 1)
                    dve.wait_ge(s_bcs, n * 2)
                    tt_(BC[:], Bs[:], Cs[:], ALU.mult).then_inc(s_bcp, 1)
                    dve.wait_ge(s_sp, n)
                    for t in range(2):
                        ins = ts_(dts[:, t, :], ps[:, 6 + t, :], dt_bias[:, t:t + 1], 0.0, ALU.add, ALU.max)
                    step.link(ins)
                    step.link(tt_(dts[:], dts[:], sp[:], ALU.add))
                    dve.wait_ge(s_xs, n * 2)
                    step.link(tt_(dts[:], dts[:], xs[:], ALU.mult))
                    dve.wait_ge(s_bc, n)
                    for t in range(2):
                        for d in range(2):
                            ins = tt_(yq[:, t, HALF * (1 - d):HALF * (2 - d)], dts[:, t, HALF * d:HALF * d + HALF],
                                      ps[:, 4, HALF * d:HALF * d + HALF], ALU.mult)
                    dve.wait_ge(s_fc, n)
                    for t in range(2):
                        ins = stt(yz[:, t, :], ps[:, 2 + t, :], D_col[:, t:t + 1], xs[:, t, :], ALU.add, ALU.mult)
                    step.link(ins)
                    step.link(tt_(yq[:], yq[:], yz[:], ALU.add))
                    dve.wait_ge(s_zs, n)
                    tt_(yz[:], yq[:], zs[:], ALU.mult).then_inc(s_yz, 1)
                    dve.wait_ge(s_rms, n)
                    dve.wait_ge(s_sq, n)
                    for t in range(2):
                        ins = stt(yz[:, t, :], yz[:, t, :], norm_w[:, t:t + 1], rms[:], ALU.mult, ALU.mult)
                    ins.then_inc(s_yn, 1)
                dve.wait_ge(s_hout, c * 2 + 2)
                step.link(ts_(hmix[:], hout[:, 1, :], alpha[:, 1:2], None, ALU.mult))
                step.link(stt(hmix[:], xm[:], alpha[:, 0:1], hmix[:], ALU.mult, ALU.add))
                tt_(hmix[:], hmix[:], xm[:], ALU.add).then_inc(s_hmix, 1)
                for tt in range(4):
                    dve.wait_ge(s_up, c * 4 + (tt + 1))
                    tt_(H[:, tt, :].rearrange("p (h n) -> p h n", h=2), ps[:, 2 * tt:2 * tt + 2, :],
                        H[:, tt, :].rearrange("p (h n) -> p h n", h=2), ALU.add).then_inc(s_h1, 1)
                    dve.wait_ge(s_h1, c * 4 + (tt + 1))
                    mean_var(tt)
                for tt in range(4):
                    normalise(tt, c * 8 + 4)
                for tt in range(4):
                    dve.wait_ge(s_rt, c * 4 + (tt + 1))
                    step.link(nc.vector.tensor_copy(rt[:, tt, :], ps[:, 2 * tt, ER:ER + EXPERTS]))
                    apart(dve, s_apart_dve)
                    step.link(nc.vector.max(top[:, tt, :], rt[:, tt, :]))
                    tt_(r2[:, tt, 0:1], top[:, tt, 1:2], top[:, tt, 0:1], ALU.subtract).then_inc(s_gap, 1)
                    step.link(nc.vector.max_index(topi[:, tt, :], top[:, tt, :], rt[:, tt, :]))
                    nc.vector.tensor_copy(r2[:, tt, 5:7], topi[:, tt, 0:2])
                    dve.wait_ge(s_e2, c * 4 + (tt + 1))
                    step.link(ts_(r2[:, tt, 2:3], r2[:, tt, 1:2], 1.0, None, ALU.add))
                    step.link(nc.vector.reciprocal(r2[:, tt, 3:4], r2[:, tt, 2:3]))
                    step.link(tt_(r2[:, tt, 4:5], r2[:, tt, 1:2], r2[:, tt, 3:4], ALU.mult))
                    for j in range(2):
                        ins = ts_(wd[:, tt % 2, j, :], iota[:], r2[:, tt, 5 + j:6 + j], r2[:, tt, 3 + j:4 + j],
                                  ALU.is_equal, ALU.mult)
                    step.link(ins)
                    step.link(tt_(wd[:, tt % 2, 0, :], wd[:, tt % 2, 0, :], wd[:, tt % 2, 1, :], ALU.add))
                    if tt >= 2:
                        dve.wait_ge(s_midt, c * 4 + (tt - 1))
                    stt(mid[:, tt % 2, :, :], ps[:, 2 * tt, 0:ER].rearrange("p (e r) -> p e r", r=RANK), LORA_SCALE,
                        wd[:, tt % 2, 0, :].unsqueeze(2).to_broadcast([P, EXPERTS, RANK]), ALU.mult, ALU.mult)\
                        .then_inc(s_mid, 1)
                for tt in range(4):
                    dve.wait_ge(s_base, c * 4 + (tt + 1))
                    tt_(H[:, tt, :].rearrange("p (h n) -> p h n", h=2), ps[:, 2 * tt:2 * tt + 2, :],
                        H[:, tt, :].rearrange("p (h n) -> p h n", h=2), ALU.add).then_inc(s_h2, 1)
            step.leave(CHUNKS)


I8 = mybir.dt.int8
FR = mybir.dt.float32r
DI = 2048
DT = DI // P
NS = 16
DT_RANK = 64
B_ROW, C_ROW, SSM = 64, 96, 112
TAPS = 4
RMS_EPS = 1e-6
UNITS = TOK // BANK
COLS = TAPS + 3 + NS
CONV_B, DT_B, D_P, A_0 = TAPS, TAPS + 1, TAPS + 2, TAPS + 3
HB, DL, YB, UB, GB = 0, 4, 5, 6, 7
LN_EXP = "natural_log_exp_and_others"


def layer1(nc, a, h_dram, y_dram, out):
    with ExitStack() as ctx:
        def sb(name, shape, dt=FP):
            return ctx.enter_context(nc.sbuf_tensor(name, shape, dt))

        def sem(name):
            return ctx.enter_context(nc.semaphore("l1_" + name))

        ident = sb("l1_ident", [P, P])
        identr = sb("l1_identr", [P, P], FR)
        block1 = sb("l1_block1", [SSM, SSM])
        eps5 = sb("l1_eps5", [P, 1])
        eps6 = sb("l1_eps6", [P, 1])
        rlen = sb("l1_rlen", [SSM, 1])
        cols = sb("l1_cols", [P, DT, COLS])
        ln_w = sb("l1_ln_w", [SSM, 1])
        w_dt = sb("l1_w_dt", [DT_RANK, P])
        state = sb("l1_state", [P, DT, NS])
        halo = sb("l1_halo", [P, DT, TAPS - 1])
        ssm = sb("l1_ssm", [SSM, BANK])
        u = sb("l1_u", [P, DT, BANK])
        sg = sb("l1_sg", [P, DT, BANK])
        xT = sb("l1_xT", [P, KT, BANK])
        g_at = -(-nc.sbuf_base // 32) * 32
        g = sb("l1_g", [P, 2, 2, BANK])
        ring = sb("l1_ring", [P, 2, HID])
        s3 = sb("l1_s3", [P, 4, BANK])
        spl = sb("l1_spl", [P, BANK])
        dmax = sb("l1_dmax", [P, BANK])
        up = sb("l1_up", [P, TAPS - 1 + BANK])
        acc = sb("l1_acc", [P, 2, BANK])
        tern = sb("l1_tern", [P, 2, HID], I8)
        stats = sb("l1_stats", [P, 8, 2, 6])
        mv = sb("l1_mv", [P, 8, 2])
        lnv = sb("l1_lnv", [P, 8])
        rstd = sb("l1_rstd", [P, 8])
        ps = ctx.enter_context(nc.psum_tensor("l1_ps", [P, 8, BANK], FP))
        slab_at = -(-nc.sbuf_base // 32) * 32
        slab = sb("l1_slab", [P, 20 * HID + 16])

        def at(name, offset, shape, dt=FP, base=slab_at):
            return nc.alloc_sbuf_tensor_at("l1_" + name, shape, dt, offset=base + offset)

        KB = 1024
        rep = at("rep", 0, [P, 2 * NS, BANK])
        dBu = at("dBu", 64 * KB, [P, 2, 4, BANK])
        H = at("H", 0, [P, 4, HID])
        xh = at("xh", 16 * KB, [P, KT, BANK], FR)
        xl = at("xl", 32 * KB, [P, KT, BANK], FR)
        wh = at("wh", 48 * KB, [P, 2, HID], FR)
        wl = at("wl", 56 * KB, [P, 2, HID], FR)
        yr = at("yr", 64 * KB, [P, 2, BANK])
        yh = at("yh", 68 * KB, [P, 2, BANK], FR)
        yl = at("yl", 72 * KB, [P, 2, BANK], FR)
        w_x = at("w_x", 64 * KB, [P, DT, SSM])
        raw = at("raw", 72 * KB, [SSM, BANK])
        sqr = at("squares", 74 * KB, [SSM, BANK])
        rr = at("rr", 76 * KB, [SSM, BANK])
        sh = at("ssm_high", 0, [SSM, BANK], FR, base=g_at)
        sl = at("ssm_low", 2 * KB, [SSM, BANK], FR, base=g_at)
        srow = g[:, :, :, :].rearrange("p s n t -> p s (n t)")
        Hn = s3[:, :, :].rearrange("p (t h) n -> p t (h n)", h=2)
        delta, du = s3[:, 0:2, :], s3[:, 2:4, :]

        def column(j, n):
            return cols[:, bass.ds(j, 1), n:n + 1].rearrange("p a n -> p (a n)")

        def tile(t, j):
            return t[:, bass.ds(j, 1), :].rearrange("p a n -> p (a n)")

        def slice3(t, j):
            return t[bass.ds(j, 1), :, :].rearrange("a p n -> p (a n)")

        s_const = sem("const")
        s_w = sem("weights")
        s_wx = sem("wx")
        s_hn = [sem(f"hn{n}") for n in range(2)]
        s_hl = sem("hl")
        s_var = sem("var")
        s_rstd = sem("rstd")
        s_x = sem("x")
        s_xt = sem("xt")
        s_xT = sem("xT_s")
        s_xl = sem("xl_s")
        s_winu = sem("win_u")
        s_wing = sem("win_g")
        s_pu = sem("pu")
        s_pg = sem("pg")
        s_up = sem("up_in")
        s_edge = sem("edge")
        s_conv = sem("conv")
        s_u = sem("u_s")
        s_sg = sem("sg_s")
        s_ssm = sem("ssm_p")
        s_sqr = sem("sqr")
        s_raw = sem("raw")
        s_ms = sem("ms")
        s_rr = sem("rr")
        s_ssmn = sem("ssmn")
        s_sh = sem("ssm_h")
        s_sl = sem("ssm_l")
        s_bp = sem("bp")
        s_repa = sem("rep_act")
        s_repd = sem("rep_dve")
        s_wdt = sem("wdt")
        s_dl = sem("dl")
        s_spl = sem("spl_s")
        s_delta = sem("delta")
        s_du = sem("du")
        s_dBu = sem("dBu_s")
        s_dA = sem("dA")
        s_scan = sem("scan")
        s_g = sem("g_s")
        s_sum = sem("sum")
        s_yt = sem("yt")
        s_y = sem("y")
        s_ys = sem("ys")
        s_fin = [sem(f"fin{n}") for n in range(2)]
        s_hi = sem("hi")
        s_lo = sem("lo")
        s_po = sem("po")
        s_h3 = sem("h3")
        s_tern = [sem(f"tern{n}") for n in range(2)]
        s_wf = sem("wf")
        s_fh = sem("fh")
        s_fl = sem("fl")
        s_pf = sem("pf")
        s_h4 = sem("h4")
        s_out = sem("out")
        s_act = sem("act_steps")
        s_dve = sem("dve_steps")
        s_apart = [sem(f"apart{n}") for n in range(4)]

        block = ctx.enter_context(nc.Block())

        def rows(dram, K, t):
            return dram[K * BANK + t * P:K * BANK + (t + 1) * P, :]

        def norms_before(K):
            return 4 * (min(K + 2, UNITS) + K)

        def tiles(engine, body, first, last):
            for j in range(first):
                body(j, j % 2, j, False)
            with engine.Fori(0, (last - first) // 2) as jj:
                for par in range(2):
                    body(jj * 2 + (first + par), (first + par) % 2, first, False)
            for j in range(last, DT):
                body(j, j % 2, first, j == DT - 1)

        @block.sync
        def _(sp):
            for dst, name in ((cols, "cols"), (ln_w, "ln_w")):
                sp.dma_start(dst[:], a[name]).then_inc(s_w, 16)

            def norm_loads(K, before, tiles_=range(4)):
                for t in tiles_:
                    if t >= 2:
                        sp.wait_ge(s_xt, 2 * (before + t - 1))
                    sp.dma_start(Hn[:, t % 2, :], rows(h_dram, K, t)).then_inc(s_hn[t % 2], 16)

            def w_u(K, i):
                sp.dma_start(ring[:, 0, :], slice3(a["w_in"], i)).then_inc(s_winu, 16)

            def w_g(K, i):
                sp.dma_start(ring[:, 1, :], slice3(a["w_in"], i + DT)).then_inc(s_wing, 16)

            norm_loads(0, 0)
            w_u(0, 0)
            w_g(0, 0)
            with sp.Fori(1, DT) as i:
                sp.wait_ge(s_pu, i)
                w_u(0, i)
                sp.wait_ge(s_pg, i)
                w_g(0, i)
            sp.wait_ge(s_pg, DT)
            sp.wait_ge(s_xt, 8)
            norm_loads(1, 4)
            sp.dma_start(w_x[:], a["w_x"]).then_inc(s_wx, 16)
            for K in range(UNITS):
                more = K + 1 < UNITS
                sp.dma_start(w_dt[:], a["w_dt"][0, :, :]).then_inc(s_wdt, 16)
                if more:
                    w_u(K + 1, 0)
                    w_g(K + 1, 0)
                sp.wait_ge(s_dl, K * DT + 1)
                sp.dma_start(w_dt[:], a["w_dt"][1, :, :]).then_inc(s_wdt, 16)

                def tile_transfers(j, par, early, last, K=K, more=more):
                    m = K * DT + j
                    if early >= 1:
                        sp.wait_ge(s_y, m)
                        sp.dma_start(slice3(y_dram, m - 1), tile(u, j - 1)).then_inc(s_ys, 16)
                    if last is not True and not (isinstance(j, int) and j >= DT - 2):
                        sp.wait_ge(s_dl, m + 2)
                        sp.dma_start(w_dt[:], slice3(a["w_dt"], j + 2)).then_inc(s_wdt, 16)
                    if more and early >= 1:
                        sp.wait_ge(s_pu, m + DT)
                        w_u(K + 1, j)
                        sp.wait_ge(s_pg, m + DT)
                        w_g(K + 1, j)

                tiles(sp, tile_transfers, 4, 14)
                sp.wait_ge(s_y, K * DT + DT)
                sp.dma_start(slice3(y_dram, K * DT + DT - 1), tile(u, DT - 1)).then_inc(s_ys, 16)
                if more:
                    sp.wait_ge(s_pg, (K + 2) * DT)
                    sp.wait_ge(s_pu, (K + 2) * DT)
                for t in range(4):
                    sp.dma_start(H[:, t, :], rows(h_dram, K, t)).then_inc(s_hl, 16)
                for j in range(DT):
                    sp.wait_ge(s_ys, 16 * (K * DT + j + 1))
                    if j >= 2:
                        sp.wait_ge(s_lo, K * DT + j - 1)
                    sp.dma_start(yr[:, j % 2, :], y_dram[K * DT + j, :, :]).then_inc(s_fin[j % 2], 16)
                    sp.dma_start(ring[:, j % 2, :], a["w_out"][j, :, :]).then_inc(s_fin[j % 2], 16)

                def tern_loads(k, K=K):
                    if k >= 2:
                        sp.wait_ge(s_wf, K * KT + k - 1)
                    sp.dma_start(tern[:, k % 2, :].bitcast(I32), a["tern"][k, :, :]).then_inc(s_tern[k % 2], 16)
                    sp.dma_start(srow[:, k % 2, :], a["scales"][k, :].partition_broadcast(P)).then_inc(s_tern[k % 2], 16)

                tern_loads(0)
                tern_loads(1)
                if K + 2 < UNITS:
                    norm_loads(K + 2, norms_before(K), range(2))
                if more:
                    sp.wait_ge(s_po, (K + 1) * DT)
                    sp.dma_start(w_x[:], a["w_x"]).then_inc(s_wx, 16)
                if K + 2 < UNITS:
                    norm_loads(K + 2, norms_before(K), range(2, 4))
                for k in range(2, KT):
                    tern_loads(k)
                for t in range(4):
                    sp.wait_ge(s_h4, K * 4 + t + 1)
                    sp.dma_start(rows(out, K, t), H[:, t, :]).then_inc(s_out, 16)
            sp.wait_ge(s_out, UNITS * 64)

        @block.gpsimd
        def _(pool):
            identity(nc, pool, ident[:], s_const)
            nc.gpsimd.memset(eps5[:], LN_EPS).then_inc(s_const, 1)
            nc.gpsimd.memset(eps6[:], RMS_EPS).then_inc(s_const, 1)
            nc.gpsimd.memset(block1[:], 0.0).then_inc(s_const, 1)
            pool.wait_ge(s_const, 5)
            for r0, r1, n in ((0, DT_RANK, DT_RANK), (B_ROW, C_ROW, NS), (C_ROW, SSM, NS)):
                nc.gpsimd.memset(block1[r0:r1, r0:r1], 1.0).then_inc(s_const, 1)
                nc.gpsimd.memset(rlen[r0:r1, :], 1.0 / n).then_inc(s_const, 1)

            for K in range(UNITS):
                pool.wait_ge(s_sg, K * DT + DT + 1)
                pool.wait_ge(s_u, K * DT + DT + 1)
                pool.wait_ge(s_repa, K * NS + NS)
                pool.wait_ge(s_repd, K * NS + NS)

                def gated(j, K=K):
                    pool.wait_ge(s_yt, K * DT + j + 2)
                    nc.gpsimd.tensor_tensor(tile(u, j), tile(u, j), tile(sg, j), ALU.mult).then_inc(s_y, 1)

                def states(j, par, early, last, K=K, gated=gated):
                    m = K * DT + j
                    pool.wait_ge(s_delta, m + 1)
                    nc.gpsimd.tensor_tensor(du[:, par, :], delta[:, par, :], tile(u, j), ALU.mult).then_inc(s_du, 1)
                    pool.wait_ge(s_du, m + 1)
                    for q in range(4):
                        pool.wait_ge(s_scan, m * NS + (q * 4 + 4))
                        nc.gpsimd.tensor_tensor(dBu[:, q % 2, :, :], du[:, par, :].unsqueeze(1).to_broadcast([P, 4, BANK]),
                                                rep[:, 4 * q:4 * q + 4, :], ALU.mult).then_inc(s_dBu, 1)
                        if q == 1 and early >= 1:
                            gated(j - 1)

                tiles(pool, states, 2, 16)
                gated(DT - 1)

        @block.tensor
        def _(pe):
            pe.sem_inc(s_sum, 2)
            pe.wait_ge(s_const, 11)

            def transposes(t, src, x_done):
                pe.wait_ge(s_x, x_done)
                for h in range(2):
                    for q in range(4):
                        k = 4 * h + q
                        ins = nc.tensor.transpose(ps[:, 2 * t + h, P * q:P * q + P],
                                                  src[:, t % 2, P * k:P * k + P], ident[:])
                    ins.then_inc(s_xt, 1)

            def product(out_, parts):
                for n, (lhsT, rhs) in enumerate(parts):
                    ins = nc.tensor.matmul(out_, lhsT, rhs, start=(n == 0), stop=(n == len(parts) - 1))
                return ins

            def project_step(K, i, s):
                m = K * DT + i
                slot, bank, k = (0, UB, s) if s < KT else (1, GB, s - KT)
                if s == 0:
                    pe.wait_ge(s_winu, m * 16 + 16)
                    pe.wait_ge(s_up, m + 1)
                if s == KT:
                    pe.wait_ge(s_wing, m * 16 + 16)
                    pe.wait_ge(s_sg, m + 1)
                ins = nc.tensor.matmul(ps[:, bank, :], ring[:, slot, P * k:P * k + P], xT[:, k, :],
                                       start=(k == 0), stop=(k == KT - 1))
                if k == KT - 1:
                    ins.then_inc((s_pu, s_pg)[slot], 1)

            def dt_product(K, j):
                m = K * DT + j
                pe.wait_ge(s_wdt, m * 16 + 16)
                if not (K == 0 and isinstance(j, int) and j == 0):
                    pe.wait_ge(s_delta, m)
                product(ps[:, DL, :], [(w_dt[:], ssm[0:DT_RANK, :])]).then_inc(s_dl, 1)

            for t in range(4):
                transposes(t, Hn, t + 1)
            pe.wait_ge(s_xT, 8)
            with pe.Fori(0, DT) as i:
                for s in range(2 * KT):
                    project_step(0, i, s)
            for t in range(4):
                transposes(t, Hn, 4 + t + 1)
            pe.wait_ge(s_xT, 16)

            def dt_b_c(K):
                pe.wait_ge(s_wx, K * 16 + 16)
                pe.wait_ge(s_u, K * DT + DT + 1)
                product(ps[0:SSM, 0, :], [(w_x[:, j, :], u[:, j, :]) for j in range(DT)]).then_inc(s_ssm, 1)
                pe.wait_ge(s_sqr, K + 1)
                product(ps[0:SSM, 1, :], [(block1[:], sqr[:])]).then_inc(s_ms, 1)

            dt_b_c(0)
            for K in range(UNITS):
                more = K + 1 < UNITS
                pe.wait_ge(s_sh, K + 1)
                pe.wait_ge(s_sl, K + 1)
                for n in range(2 * NS):
                    if n >= 4:
                        s = s_repd if n % 2 else s_repa
                        pe.wait_ge(s, K * NS + (n - 4) // 2 + 1)
                    r0 = B_ROW if n < NS else C_ROW
                    pick = identr[r0:r0 + NS, r0 + n % NS:r0 + n % NS + 1].to_broadcast([NS, P])
                    product(ps[:, 4 + n % 4, :], [(pick, sh[r0:r0 + NS, :]), (pick, sl[r0:r0 + NS, :])]).then_inc(s_bp, 1)
                pe.wait_ge(s_repa, K * NS + NS)
                pe.wait_ge(s_repd, K * NS + NS)
                dt_product(K, 0)

                def y_sums(j, par, early, last, K=K, more=more):
                    m = K * DT + j
                    for p in range(8):
                        if more and early >= 1:
                            for s in (range(4) if p == 0 else range(2 * p + 2, 2 * p + 4) if p < 7 else ()):
                                project_step(K + 1, j - 1, s)
                        pe.wait_ge(s_g, m * 8 + (p + 3))
                        if p == 0:
                            pe.wait_ge(s_yt, m + 1)
                        for n in range(2):
                            ins = nc.tensor.matmul(ps[:, YB, :], ident[:], g[:, p % 2, n, :],
                                                   start=(p == 0 and n == 0), stop=(p == 7 and n == 1))
                        ins.then_inc(s_sum, 1)
                        if p == 0 and not last:
                            dt_product(K, j + 1)

                tiles(pe, y_sums, 2, 14)
                if more:
                    for s in range(2 * KT):
                        project_step(K + 1, DT - 1, s)
                pe.wait_ge(s_y, K * DT + DT)
                if more:
                    pe.wait_ge(s_up, (K + 2) * DT + 1)
                    pe.wait_ge(s_sg, (K + 2) * DT + 1)

                def split_products(parts, w, first, last):
                    for t in range(4):
                        xh_, xl_ = parts(t)
                        for n, (l, r) in enumerate(((xh_, 0), (xh_, 1), (xl_, 0))):
                            for h in range(2):
                                ins = nc.tensor.matmul(ps[:, 2 * t + h, :], l, w[r][:, BANK * h:BANK * h + BANK],
                                                       start=(first and n == 0), stop=(last and n == 2))
                    return ins

                for j in range(DT):
                    pe.wait_ge(s_lo, K * DT + j + 1)
                    split_products(lambda t: (yh[:, j % 2, P * t:P * t + P], yl[:, j % 2, P * t:P * t + P]),
                                   (wh[:, j % 2, :], wl[:, j % 2, :]), j == 0, j == DT - 1).then_inc(s_po, 1)
                if more:
                    pe.wait_ge(s_h3, K * 4 + 1)
                    dt_b_c(K + 1)
                    pe.wait_ge(s_raw, K + 2)
                    pe.wait_ge(s_rr, K + 2)
                pe.wait_ge(s_h3, K * 4 + 4)
                x0 = norms_before(K)
                if K + 2 < UNITS:
                    for t in range(4):
                        transposes(t, Hn, x0 + t + 1)
                    pe.wait_ge(s_xT, 2 * x0 + 8)
                    x0 += 4
                for t in range(4):
                    transposes(t, ring, x0 + t + 1)
                pe.wait_ge(s_xl, 8 * (K + 1))
                for k in range(KT):
                    pe.wait_ge(s_fl, K * KT + k + 1)
                    split_products(lambda t: (xh[:, k, P * t:P * t + P], xl[:, k, P * t:P * t + P]),
                                   (wh[:, k % 2, :], wl[:, k % 2, :]), k == 0, k == KT - 1).then_inc(s_pf, 1)
                pe.wait_ge(s_h4, K * 4 + 4)

        @block.scalar
        def _(act):
            act.wait_ge(s_const, 11)
            act.wait_ge(s_w, 16 * 2)
            act.sem_inc(s_up, 1)
            act.sem_inc(s_sg, 1)
            act.sem_inc(s_u, 1)
            step = Steps(act, s_act)
            nc.scalar.activation(identr[:], ident[:], ACT.Copy)

            def inverse_std(t, done):
                act.wait_ge(s_var, done)
                step.link(nc.scalar.activation(lnv[:, t:t + 1], mv[:, t, 1:2], ACT.Ln, bias=eps5[:]))
                nc.scalar.activation(rstd[:, t:t + 1], lnv[:, t:t + 1], ACT.Exp, scale=-0.5).then_inc(s_rstd, 1)

            def transposed(t, dst, done):
                for h in range(2):
                    act.wait_ge(s_xt, done + 2 * t + h + 1)
                    nc.scalar.activation(dst[:, 4 * h:4 * h + 4, P * t:P * t + P],
                                         ps[:, 2 * t + h, :].rearrange("p (k t) -> p k t", t=P), ACT.Copy)\
                        .then_inc(s_xT, 1)

            def softplus(K, j, part):
                if part == 0:
                    act.wait_ge(s_dl, K * DT + j + 1)
                    step.link(nc.scalar.activation(spl[:], ps[:, DL, :], ACT.Abs, bias=column(j, DT_B)))
                elif part == 1:
                    step.link(nc.scalar.activation(spl[:], spl[:], ACT.Exp, scale=-1.0))
                else:
                    nc.scalar.activation(spl[:], spl[:], ACT.Ln, bias=1.0).then_inc(s_spl, 1)

            def take_u(K, i):
                m = K * DT + i
                act.wait_ge(s_pu, m + 1)
                act.wait_ge(s_edge, m + 1)
                nc.scalar.activation(up[:, TAPS - 1:], ps[:, UB, :], ACT.Copy).then_inc(s_up, 1)

            def silu_gate(K, i):
                m = K * DT + i
                act.wait_ge(s_pg, m + 1)
                if K:
                    act.wait_ge(s_y, m - DT + 1)
                nc.scalar.activation(tile(sg, i), ps[:, GB, :], ACT.Silu).then_inc(s_sg, 1)

            def silu_u(K, i):
                m = K * DT + i
                act.wait_ge(s_conv, m + 1)
                if K:
                    act.wait_ge(s_ys, (m - DT + 1) * 16)
                nc.scalar.activation(tile(u, i), acc[:, 0, :], ACT.Silu, bias=column(i, CONV_B)).then_inc(s_u, 1)

            nc.scalar.preload_act_table_set(LN_EXP)
            for t in range(4):
                inverse_std(t, t + 1)
                transposed(t, xT, 0)
            nc.scalar.preload_act_table(ACT.Silu)
            with act.Fori(0, DT) as i:
                take_u(0, i)
                silu_gate(0, i)
                silu_u(0, i)
            nc.scalar.preload_act_table_set(LN_EXP)
            for t in range(4):
                inverse_std(t, 4 + t + 1)
                transposed(t, xT, 8)

            def inverse_rms(K):
                act.wait_ge(s_ssm, K + 1)
                nc.scalar.activation(sqr[:], ps[0:SSM, 0, :], ACT.Square).then_inc(s_sqr, 1)
                act.wait_ge(s_ms, K + 1)
                step.link(nc.scalar.activation(rr[:], ps[0:SSM, 1, :], ACT.Ln, scale=rlen[:], bias=eps6[0:SSM, :]))
                nc.scalar.activation(rr[:], rr[:], ACT.Exp, scale=-0.5).then_inc(s_rr, 1)

            inverse_rms(0)
            for K in range(UNITS):
                more = K + 1 < UNITS
                act.wait_ge(s_ssmn, K + 1)
                if K:
                    act.wait_ge(s_fl, K * KT)
                    act.wait_ge(s_out, K * 64)
                nc.scalar.activation(sh[:], ssm[:], ACT.Copy).then_inc(s_sh, 1)
                for n in range(0, 2 * NS, 2):
                    act.wait_ge(s_bp, K * 2 * NS + n + 1)
                    nc.scalar.activation(rep[:, n, :], ps[:, 4 + n % 4, :], ACT.Copy).then_inc(s_repa, 1)
                for part in range(3):
                    softplus(K, 0, part)

                def decays(j, par, early, last, K=K, more=more):
                    m = K * DT + j
                    act.wait_ge(s_delta, m + 1)
                    for n in range(NS):
                        if n % 2 == 0:
                            act.wait_ge(s_g, m * 8 + (n // 2 + 1))
                        nc.scalar.activation(ps[:, HB + n % 4, :], delta[:, par, :], ACT.Exp, scale=column(j, A_0 + n))\
                            .then_inc(s_dA, 1)
                        if n == 3 and more and early >= 2:
                            if early >= 3:
                                silu_u(K + 1, j - 3)
                            silu_gate(K + 1, j - 2)
                            nc.scalar.preload_act_table_set(LN_EXP)
                        if 4 <= n < 7 and not last:
                            softplus(K, j + 1, n - 4)
                        if n == 13 and more and early >= 1:
                            take_u(K + 1, j - 1)

                for j in range(4):
                    decays(j, j % 2, j, False)
                at_, pairs = step.at, 5
                with act.Fori(0, pairs) as jj:
                    step.reg = jj * 4
                    for par in range(2):
                        decays(jj * 2 + (4 + par), par, 4, False)
                assert step.at == at_ + 4
                step.reg, step.at = None, at_ + 4 * pairs
                decays(DT - 2, 0, 4, False)
                decays(DT - 1, 1, 4, True)
                if more:
                    silu_u(K + 1, DT - 3)
                    silu_gate(K + 1, DT - 2)
                    take_u(K + 1, DT - 1)
                    silu_u(K + 1, DT - 2)
                    silu_gate(K + 1, DT - 1)
                    silu_u(K + 1, DT - 1)
                nc.scalar.preload_act_table_set(LN_EXP)
                for j in range(DT):
                    act.wait_ge(s_fin[j % 2], K * 256 + (j // 2) * 32 + 32)
                    if j >= 2:
                        act.wait_ge(s_po, K * DT + j - 1)
                    elif K:
                        act.wait_ge(s_pf, K * KT)
                    nc.scalar.activation(yh[:, j % 2, :], yr[:, j % 2, :], ACT.Copy)
                    nc.scalar.activation(wh[:, j % 2, :], ring[:, j % 2, :], ACT.Copy).then_inc(s_hi, 1)
                if more:
                    inverse_rms(K + 1)
                v0 = norms_before(K)
                x0 = 2 * v0
                if K + 2 < UNITS:
                    for t in range(4):
                        inverse_std(t, v0 + t + 1)
                    for t in range(4):
                        transposed(t, xT, x0)
                    v0, x0 = v0 + 4, x0 + 8
                for t in range(4):
                    inverse_std(4 + t, v0 + t + 1)
                for t in range(4):
                    transposed(t, xh, x0)
                for k in range(KT):
                    act.wait_ge(s_wf, K * KT + k + 1)
                    if k >= 2:
                        act.wait_ge(s_pf, K * KT + k - 1)
                    nc.scalar.activation(wh[:, k % 2, :], ring[:, k % 2, :], ACT.Copy).then_inc(s_fh, 1)

        @block.vector
        def _(dve):
            dve.sem_inc(s_scan, 8)
            dve.sem_inc(s_g, 2)
            dve.sem_inc(s_yt, 1)
            dve.wait_ge(s_const, 11)
            dve.wait_ge(s_w, 16 * 2)
            step = Steps(dve, s_dve)
            tt_, ts_, stt = nc.vector.tensor_tensor, nc.vector.tensor_scalar, nc.vector.scalar_tensor_tensor

            def mean_var(t, src):
                for h in range(2):
                    ins = nc.vector.bn_stats(stats[:, t, h, :], src[:, BANK * h:BANK * h + BANK])
                step.link(ins)
                nc.vector.bn_aggr(mv[:, t, :], stats[:, t, :, :]).then_inc(s_var, 1)

            def project_norm(K, v0):
                for t in range(4):
                    dve.wait_ge(s_hn[t % 2], K * 32 + (t // 2) * 16 + 16)
                    mean_var(t, Hn[:, t % 2, :])
                    dve.wait_ge(s_rstd, v0 + t + 1)
                    ts_(Hn[:, t % 2, :], Hn[:, t % 2, :], mv[:, t, 0:1], rstd[:, t:t + 1], ALU.subtract, ALU.mult)\
                        .then_inc(s_x, 1)

            def normalise_dt_b_c(K):
                dve.wait_ge(s_sqr, K + 1)
                ts_(raw[:], ps[0:SSM, 0, :], ln_w[:], None, ALU.mult).then_inc(s_raw, 1)
                dve.wait_ge(s_raw, K + 1)
                dve.wait_ge(s_rr, K + 1)
                tt_(ssm[:], raw[:], rr[:], ALU.mult).then_inc(s_ssmn, 1)

            def edge(K, i):
                if K % 2:
                    nc.vector.tensor_copy(up[:, 0:TAPS - 1], tile(halo, i)).then_inc(s_edge, 1)
                else:
                    nc.vector.memset(up[:, 0:TAPS - 1], 0.0).then_inc(s_edge, 1)

            def conv(K, i, last=False):
                m = K * DT + i
                dve.wait_ge(s_up, m + 2)
                dve.wait_ge(s_edge, m + 1)
                step.link(ts_(acc[:, 1, :], up[:, 0:BANK], column(i, 0), None, ALU.mult))
                step.link(stt(acc[:, 1, :], up[:, 1:1 + BANK], column(i, 1), acc[:, 1, :], ALU.mult, ALU.add))
                step.link(stt(acc[:, 1, :], up[:, 2:2 + BANK], column(i, 2), acc[:, 1, :], ALU.mult, ALU.add))
                if K % 2 == 0:
                    nc.vector.tensor_copy(tile(halo, i), up[:, BANK:BANK + TAPS - 1])
                dve.wait_ge(s_u, m + 1)
                stt(acc[:, 0, :], up[:, 3:3 + BANK], column(i, 3), acc[:, 1, :], ALU.mult, ALU.add).then_inc(s_conv, 1)
                if not last:
                    edge(K, i + 1)

            def make_delta(K, j, par):
                m = K * DT + j
                dve.wait_ge(s_spl, m + 1)
                step.link(ts_(dmax[:], ps[:, DL, :], column(j, DT_B), 0.0, ALU.add, ALU.max))
                tt_(delta[:, par, :], dmax[:], spl[:], ALU.add).then_inc(s_delta, 1)

            def finish_y(K, j):
                m = K * DT + j
                dve.wait_ge(s_sum, m * 8 + 10)
                stt(tile(u, j), tile(u, j), column(j, D_P), ps[:, YB, :], ALU.mult, ALU.add).then_inc(s_yt, 1)

            def low(dst, src, high, sem_):
                tt_(dst, src, high.bitcast(FP), ALU.subtract).then_inc(sem_, 1)

            project_norm(0, 0)
            edge(0, 0)
            at_, per = step.at, TAPS - 1
            with dve.Fori(0, DT - 1) as i:
                step.reg = i * per
                conv(0, i)
            step.reg, step.at = None, at_ + per * (DT - 1)
            conv(0, DT - 1, last=True)
            project_norm(1, 4)
            normalise_dt_b_c(0)
            for K in range(UNITS):
                more = K + 1 < UNITS
                hf = K % 2
                dve.wait_ge(s_sh, K + 1)
                low(sl[:], ssm[:], sh[:], s_sl)
                for n in range(1, 2 * NS, 2):
                    dve.wait_ge(s_bp, K * 2 * NS + n + 1)
                    nc.vector.tensor_copy(rep[:, n, :], ps[:, 4 + n % 4, :]).then_inc(s_repd, 1)
                dve.wait_ge(s_repa, K * NS + NS)
                make_delta(K, 0, 0)
                if more:
                    edge(K + 1, 0)

                def scan_tile(j, par, early, last, K=K, more=more, hf=hf):
                    m = K * DT + j

                    def scan(n):
                        dve.wait_ge(s_dA, m * NS + (n + 1))
                        if n % 4 == 0:
                            dve.wait_ge(s_dBu, m * 4 + (n // 4 + 1))
                        init = state[:, bass.ds(j, 1), n:n + 1].rearrange("p a n -> p (a n)") if hf else 0.0
                        nc.vector.tensor_tensor_scan(ps[:, HB + n % 4, :], ps[:, HB + n % 4, :],
                                                     dBu[:, (n // 4) % 2, n % 4, :], init, ALU.mult, ALU.add)\
                            .then_inc(s_scan, 1)

                    for p in range(8):
                        scan(2 * p)
                        scan(2 * p + 1)
                        dve.wait_ge(s_sum, m * 8 + (p + 1))
                        dve.wait_ge(s_scan, m * NS + (2 * p + 2 + 8))
                        h2 = ps[:, HB + 2 * (p % 2):HB + 2 * (p % 2) + 2, :]
                        if hf == 0:
                            nc.vector.tensor_copy(state[:, bass.ds(j, 1), 2 * p:2 * p + 2],
                                                  h2[:, :, BANK - 1:BANK].rearrange("p n a -> p a n"))
                        tt_(g[:, p % 2, :, :], h2, rep[:, NS + 2 * p:NS + 2 * p + 2, :], ALU.mult).then_inc(s_g, 1)
                        if p == 0 and early >= 1:
                            finish_y(K, j - 1)
                        if p == 1:
                            if more and early >= 2:
                                conv(K + 1, j - 2)
                        if p == 4 and not last:
                            make_delta(K, j + 1, 1 - par)

                for j in range(4):
                    scan_tile(j, j % 2, j, False)
                at_, pairs = step.at, 5
                per = 2 * (1 + (TAPS - 1 if more else 0))
                with dve.Fori(0, pairs) as jj:
                    step.reg = jj * per
                    for par in range(2):
                        scan_tile(jj * 2 + (4 + par), par, 4, False)
                assert step.at == at_ + per, (step.at - at_, per)
                step.reg, step.at = None, at_ + per * pairs
                scan_tile(DT - 2, 0, 4, False)
                scan_tile(DT - 1, 1, 4, True)
                finish_y(K, DT - 1)
                if more:
                    conv(K + 1, DT - 2)
                    conv(K + 1, DT - 1, last=True)
                for j in range(DT):
                    if j >= 2:
                        dve.wait_ge(s_po, K * DT + j - 1)
                    dve.wait_ge(s_hi, K * DT + j + 1)
                    tt_(yl[:, j % 2, :], yr[:, j % 2, :], yh[:, j % 2, :].bitcast(FP), ALU.subtract)
                    low(wl[:, j % 2, :], ring[:, j % 2, :], wh[:, j % 2, :], s_lo)
                dve.wait_ge(s_po, K * DT + DT)
                dve.wait_ge(s_hl, K * 64 + 64)
                for t in range(4):
                    Ht = H[:, t, :].rearrange("p (h n) -> p h n", h=2)
                    tt_(Ht, ps[:, 2 * t:2 * t + 2, :], Ht, ALU.add).then_inc(s_h3, 1)
                if more:
                    normalise_dt_b_c(K + 1)
                v0 = norms_before(K)
                x0 = 2 * v0
                if K + 2 < UNITS:
                    project_norm(K + 2, v0)
                    v0, x0 = v0 + 4, x0 + 8
                dve.wait_ge(s_h3, K * 4 + 4)
                for t in range(4):
                    mean_var(4 + t, H[:, t, :])
                for t in range(4):
                    dve.wait_ge(s_rstd, v0 + t + 1)
                    if t >= 2:
                        dve.wait_ge(s_xt, x0 + 2 * t - 2)
                    ts_(ring[:, t % 2, :], H[:, t, :], mv[:, 4 + t, 0:1], rstd[:, 4 + t:5 + t], ALU.subtract, ALU.mult)\
                        .then_inc(s_x, 1)
                for t in range(4):
                    for h in range(2):
                        dve.wait_ge(s_xT, x0 + 2 * t + h + 1)
                        tile_of = lambda x: x[:, 4 * h:4 * h + 4, P * t:P * t + P]
                        tt_(tile_of(xl), ps[:, 2 * t + h, :].rearrange("p (k t) -> p k t", t=P),
                            tile_of(xh).bitcast(FP), ALU.subtract).then_inc(s_xl, 1)
                for k in range(KT):
                    dve.wait_ge(s_tern[k % 2], K * 128 + (k // 2) * 32 + 32)
                    if k >= 2:
                        dve.wait_ge(s_fl, K * KT + k - 1)
                    tt_(ring[:, k % 2, :], tern[:, k % 2, :], srow[:, k % 2, :], ALU.mult).then_inc(s_wf, 1)
                    dve.wait_ge(s_fh, K * KT + k + 1)
                    if k >= 2:
                        dve.wait_ge(s_pf, K * KT + k - 1)
                    low(wl[:, k % 2, :], ring[:, k % 2, :], wh[:, k % 2, :], s_fl)
                dve.wait_ge(s_pf, K * KT + KT)
                for t in range(4):
                    Ht = H[:, t, :].rearrange("p (h n) -> p h n", h=2)
                    tt_(Ht, ps[:, 2 * t:2 * t + 2, :], Ht, ALU.add).then_inc(s_h4, 1)


def layouts(x, L0_tok_W, L0_tok_b, L0_attn_w_down, L0_attn_b_down, L0_attn_w_up, L0_attn_b_up, L0_attn_gate1,
            L0_attn_hy_in_w, L0_attn_hy_conv_w, L0_attn_hy_conv_b, L0_attn_hy_dt_bias, L0_attn_hy_D,
            L0_attn_hy_fcD_w, L0_attn_hy_norm_w, L0_attn_hy_out_w, L0_ffn_base_W, L0_ffn_router_W,
            L0_ffn_lora_A, L0_ffn_lora_B, **rest):
    import numpy as np

    P, DIN, DST, HD = 128, 256, 16, 64

    def k_tiles(w_t):
        return w_t.reshape(-1, P, w_t.shape[1]).transpose(1, 0, 2)

    def channels(v):
        return v.reshape((-1, P) + v.shape[1:]).swapaxes(0, 1)

    o = {}
    o["x"] = x
    o["tok_W"] = L0_tok_W.T
    o["tok_b"] = L0_tok_b
    o["up_b"] = L0_attn_b_up
    o["w_down"] = k_tiles(L0_attn_w_down.T)
    o["w_up"] = L0_attn_w_up.T
    o["w_base"] = k_tiles(L0_ffn_base_W.T)
    lora_a = L0_ffn_lora_A.transpose(1, 0, 2).reshape(1024, 128)
    o["w_lora"] = k_tiles(np.concatenate([lora_a, L0_ffn_router_W.T], axis=1))
    o["w_lora_b"] = L0_ffn_lora_B.reshape(128, 1024)
    w = L0_attn_hy_in_w
    o["in_z"] = w[0:DIN].T
    o["in_x"] = w[DIN:2 * DIN].T
    o["in_bc"] = w[2 * DIN:2 * DIN + 2 * DST].T
    dt = w[2 * DIN + 2 * DST:].reshape(2, 4, P)
    o["in_dt"] = np.repeat(dt, HD, axis=1).transpose(2, 0, 1)
    o["w_fc"] = k_tiles(np.repeat(L0_attn_hy_fcD_w, HD, axis=0).T)
    o["w_hout"] = k_tiles(L0_attn_hy_out_w.T)
    o["col"] = np.concatenate(
        [L0_attn_b_down.reshape(P, 1), np.full((P, 1), L0_attn_gate1),
         channels(np.repeat(L0_attn_hy_dt_bias, HD)), channels(np.repeat(L0_attn_hy_D, HD)),
         channels(L0_attn_hy_norm_w)], axis=1).astype(L0_attn_b_down.dtype)
    conv = np.concatenate([L0_attn_hy_conv_w[:, 0, :], L0_attn_hy_conv_b[:, None]], axis=1)
    o["conv_x"] = channels(conv[:DIN])
    o["conv_bc"] = conv[DIN:].reshape(2, DST, 8).transpose(1, 0, 2)
    return o


def layouts1(L1_attn_W_in, L1_attn_conv_w, L1_attn_conv_b, L1_attn_Wx, L1_attn_dt_ln_w, L1_attn_b_ln_w,
             L1_attn_c_ln_w, L1_attn_Wdt, L1_attn_dt_bias, L1_attn_A, L1_attn_D_param, L1_attn_W_out,
             L1_ffn_ternary, L1_ffn_scales, **rest):
    import numpy as np

    P, DI, NS, RANK = 128, 2048, 16, 64
    f = L1_attn_W_in.dtype

    def channels(v):
        return v.reshape(-1, P, v.shape[1]).swapaxes(0, 1)

    def rows_padded(w):
        return np.concatenate([w[:RANK + NS], np.zeros((NS,) + w.shape[1:], f), w[RANK + NS:]], axis=0)

    o = {}
    o["w_in"] = L1_attn_W_in.reshape(2 * DI // P, P, 8, P).transpose(0, 3, 2, 1).reshape(2 * DI // P, P, 1024)
    o["w_x"] = rows_padded(L1_attn_Wx).T.reshape(DI // P, P, 112).swapaxes(0, 1)
    o["ln_w"] = rows_padded(np.concatenate([L1_attn_dt_ln_w, L1_attn_b_ln_w, L1_attn_c_ln_w])[:, None])
    o["w_dt"] = L1_attn_Wdt.reshape(DI // P, P, RANK).swapaxes(1, 2)
    o["cols"] = channels(np.concatenate([L1_attn_conv_w, L1_attn_conv_b[:, None], L1_attn_dt_bias[:, None],
                                         L1_attn_D_param[:, None], L1_attn_A], axis=1))
    o["w_out"] = L1_attn_W_out.T.reshape(DI // P, P, 1024)
    o["tern"] = np.ascontiguousarray(L1_ffn_ternary.T).view(np.int32).reshape(8, P, 256)
    o["scales"] = L1_ffn_scales.reshape(1024, 8).T
    return o


def tower(nc, a, out):
    h_dram = nc.dram_tensor("residual", (TOK, HID), FP).ap()
    layer0(nc, a, h_dram)
    y_dram = nc.dram_tensor("gated_y", (UNITS * DT, P, BANK), FP).ap()
    layer1(nc, a, h_dram, y_dram, out)


def kernel(**inputs):
    import numpy as np
    import concourse.bacc as bacc
    from concourse.bass_utils import run_bass_kernel_spmd

    inputs = {name: np.asarray(v) for name, v in inputs.items()}
    arrays = {name: np.ascontiguousarray(v) for name, v in {**layouts(**inputs), **layouts1(**inputs)}.items()}
    nc = bacc.Bacc("TRN2", target_bir_lowering=False, num_devices=1)
    a = {name: nc.dram_tensor(f"in_{name}", v.shape, mybir.dt.from_np(v.dtype), kind="ExternalInput").ap()
         for name, v in arrays.items()}
    out = nc.dram_tensor("out", (TOK, HID), FP, kind="ExternalOutput").ap()
    tower(nc, a, out)
    got = run_bass_kernel_spmd(nc, [{f"in_{name}": v for name, v in arrays.items()}], core_ids=[0])
    return got.results[0]["out"].reshape(2, ROW, HID)
```

```python
import concourse.bass as bass
from concourse import mybir
from contextlib import ExitStack

P = 128
FP = mybir.dt.float32
I32 = mybir.dt.int32
U32 = mybir.dt.uint32
ALU = mybir.AluOpType
ACT = mybir.ActivationFunctionType

HID = 1024
TOK = 2048
ROW = 1024
KT = HID // P
BANK = 512
LN_EPS = 1e-5

ORDER = 4
VOC1 = HID + 1
DIN = 256
DST = 16
TAP_NOW, TAP_BEFORE = 6, 5
EXPERTS, RANK = 8, 16
ER = EXPERTS * RANK
LORA_SCALE = 2.0
CHUNKS = 4
HALF = 256


LN_EXP = "natural_log_exp_and_others"


C_ROW0 = 32


class Steps:

    def __init__(self, engine, sem):
        self.engine, self.sem, self.at, self.reg = engine, sem, 0, None

    def value(self):
        return self.at if self.reg is None else self.reg + self.at

    def link(self, instruction):
        self.mark(instruction)
        self.wait()

    def mark(self, instruction):
        instruction.then_inc(self.sem, 1)
        self.at += 1

    def wait(self):
        self.engine.wait_ge(self.sem, self.value())


def apart(engine, sem):
    engine.sem_inc(sem, 1)


def identity(nc, pool, tile, sem):
    nc.gpsimd.memset(tile, 0.0).then_inc(sem, 1)
    pool.wait_ge(sem, 1)
    nc.gpsimd.affine_select(out=tile, in_=tile, compare_op=ALU.not_equal, fill=1.0, base=0,
                            pattern=[[-1, P]], channel_multiplier=1).then_inc(sem, 1)


def layer0(nc, a, h_dram):
    with ExitStack() as ctx:
        def sb(name, shape, dt=FP):
            return ctx.enter_context(nc.sbuf_tensor(name, shape, dt))

        def sem(name):
            return ctx.enter_context(nc.semaphore(name))

        ident = sb("l0_ident", [P, P])
        ones = sb("l0_ones", [P, P])
        iota_i = sb("l0_iota_i", [P, EXPERTS], I32)
        iota = sb("l0_iota", [P, EXPERTS])
        eps = sb("l0_eps", [P, 1])
        tok_b = sb("l0_tok_b", [P, HID])
        up_b = sb("l0_up_b", [P, HID])
        w_down = sb("l0_w_down", [P, KT, P])
        w_up = sb("l0_w_up", [P, HID])
        w_base = sb("l0_w_base", [P, KT, HID])
        w_lora = sb("l0_w_lora", [P, KT, ER + EXPERTS])
        w_lora_b = sb("l0_w_lora_b", [P, HID])
        in_z = sb("l0_in_z", [P, DIN])
        in_x = sb("l0_in_x", [P, DIN])
        in_bc = sb("l0_in_bc", [P, C_ROW0 + DST])
        in_dt = sb("l0_in_dt", [P, 2, DIN])
        w_fc = sb("l0_w_fc", [P, 2, DIN])
        w_out = sb("l0_w_out", [P, 2, P])
        col = sb("l0_col", [P, 8])
        conv_x = sb("l0_conv_x", [P, 2, 8])
        conv_bc = sb("l0_conv_bc", [C_ROW0 + DST, 8])
        alpha = sb("l0_alpha", [P, 2])
        xi = sb("l0_xi", [16, ORDER, P], I32)
        idx = sb("l0_idx", [P, 16, ORDER], I32)
        idx_now = sb("l0_idx_now", [P, 4, ORDER], I32)
        emb = sb("l0_emb", [P, 2, ORDER, HID])
        H = sb("l0_H", [P, 2, 4, HID])
        X = sb("l0_X", [P, 2, HID])
        xTa = sb("l0_xTa", [P, KT, BANK])
        xTb = sb("l0_xTb", [P, KT, BANK])
        stats = sb("l0_stats", [P, 4, 2, 6])
        mv = sb("l0_mv", [P, 4, 2])
        lnv = sb("l0_lnv", [P, 4])
        rstd = sb("l0_rstd", [P, 4])
        xm = sb("l0_xm", [P, BANK])
        hout = sb("l0_hout", [P, 2, BANK])
        hmix = hout[:, 1, :]
        zs = sb("l0_zs", [P, 2, BANK])
        xs = sb("l0_xs", [P, 2, BANK])
        cvb = sb("l0_cvb", [C_ROW0 + DST, HALF])
        Bs = sb("l0_Bs", [DST, BANK])
        Cs = sb("l0_Cs", [DST, BANK])
        BC = Bs
        sp = sb("l0_sp", [P, 2, BANK])
        dts = sb("l0_dts", [P, 2, BANK])
        xf = dts[0:16, 0, :].rearrange("p (k n) -> p k n", k=ORDER)
        yq = sb("l0_yq", [P, 2, BANK])
        cv = yq[:, :, 0:HALF]
        w_fx, yz = sp, zs
        sq, rms = dts, sp[:, 0, :]
        top = sb("l0_top", [P, 4, 8])
        topi = sb("l0_topi", [P, 4, 8], U32)
        rt = sb("l0_rt", [P, 4, 8])
        r2 = sb("l0_r2", [P, 4, 8])
        wd = sb("l0_wd", [P, 2, 2, EXPERTS])
        mid = sb("l0_mid", [P, 2, EXPERTS, RANK])
        midT = sb("l0_midT", [P, 4, P])
        ps = ctx.enter_context(nc.psum_tensor("l0_ps", [P, 8, BANK], FP))

        s_const = sem("l0_const")
        s_w = sem("l0_weights")
        s_wdown = sem("l0_w_down_s")
        s_wbig = sem("l0_weights_big")
        s_xi0 = sem("l0_xi_filled")
        s_xi = sem("l0_xi_loaded")
        s_xf = sem("l0_xf")
        s_ixT = sem("l0_ixT")
        s_idx = sem("l0_idx")
        s_now = sem("l0_idx_now")
        s_emb_free = sem("l0_emb_free")
        s_emb = [sem(f"l0_emb{n}") for n in range(2)]
        s_var = sem("l0_var")
        s_rstd = sem("l0_rstd")
        s_x = sem("l0_x")
        s_hx = sem("l0_hx")
        s_hb = sem("l0_hb")
        s_xt = sem("l0_xt")
        s_xT = sem("l0_xT")
        s_down = sem("l0_down")
        s_xm = sem("l0_xm")
        s_in = sem("l0_in")
        s_act = sem("l0_act_steps")
        s_dve = sem("l0_dve_steps")
        s_apart_dve = sem("l0_apart_dve")
        s_cv = sem("l0_cv")
        s_bcs = sem("l0_bcs")
        s_xs = sem("l0_xs")
        s_zs = sem("l0_zs")
        s_sp = sem("l0_sp")
        s_bcp = sem("l0_bcp")
        s_bc = sem("l0_bc")
        s_fc = sem("l0_fc")
        s_yz = sem("l0_yz")
        s_sq = sem("l0_sq")
        s_ms = sem("l0_ms")
        s_rms = sem("l0_rms")
        s_yn = sem("l0_yn")
        s_ho = sem("l0_ho")
        s_hout = sem("l0_hout")
        s_alpha = sem("l0_alpha")
        s_hmix = sem("l0_hmix")
        s_up = sem("l0_up")
        s_h1 = sem("l0_h1")
        s_rt = sem("l0_rt")
        s_gap = sem("l0_gap")
        s_e2 = sem("l0_e2")
        s_mid = sem("l0_mid")
        s_midt = sem("l0_midt")
        s_midT = sem("l0_midT")
        s_base = sem("l0_base")
        s_h2 = sem("l0_h2")
        s_store = [sem(f"l0_store{n}") for n in range(4)]

        b_down, gate = col[:, 0:1], col[:, 1:2]
        dt_bias, D_col, norm_w = col[:, 2:4], col[:, 4:6], col[:, 6:8]

        def group(q, last):
            return q // 2, q % 2, (4 + q) % 8 if q < 4 or last else (5, 0)[q % 2]

        def rows(c, tt):
            return h_dram[bass.ds(c * HALF + ((tt // 2) * ROW + (tt % 2) * P), P), :]

        block = ctx.enter_context(nc.Block())

        @block.sync
        def _(sp_):
            sp_.wait_ge(s_xi0, 1)
            for k in range(ORDER):
                back = ORDER - 1 - k
                for b in range(2):
                    r0 = 8 * b
                    if back == 0:
                        sp_.dma_start(xi[r0:r0 + 8, k, :], a["x"][b, :].rearrange("(j p) -> j p", p=P)).then_inc(s_xi, 16)
                    else:
                        sp_.dma_start(xi[r0:r0 + 1, k, back:P], a["x"][b:b + 1, 0:P - back]).then_inc(s_xi, 16)
                        sp_.dma_start(xi[r0 + 1:r0 + 8, k, :],
                                      a["x"][b, P - back:ROW - back].rearrange("(j p) -> j p", p=P)).then_inc(s_xi, 16)
            sp_.dma_start(tok_b[:], a["tok_b"].partition_broadcast(P)).then_inc(s_w, 16)
            sp_.dma_start(up_b[:], a["up_b"].partition_broadcast(P)).then_inc(s_w, 16)
            for dst, name in ((in_z, "in_z"), (in_x, "in_x"), (in_bc, "in_bc"), (in_dt, "in_dt"),
                              (w_fc, "w_fc"), (w_out, "w_hout"), (col, "col"), (conv_x, "conv_x"),
                              (conv_bc, "conv_bc")):
                sp_.dma_start(dst[:], a[name]).then_inc(s_w, 16)
            sp_.wait_ge(s_emb[0], 16 * ORDER)
            sp_.dma_start(w_down[:], a["w_down"]).then_inc(s_wdown, 16)
            sp_.wait_ge(s_emb[1], 16 * ORDER * 2)
            for dst, name in ((w_up, "w_up"), (w_lora, "w_lora"), (w_lora_b, "w_lora_b"), (w_base, "w_base")):
                sp_.dma_start(dst[:], a[name]).then_inc(s_wbig, 16)
            for c in range(CHUNKS):
                for tt in range(4):
                    sp_.wait_ge(s_h2, c * 8 + 2 * tt + 2)
                    sp_.dma_start(rows(c, tt), H[:, c % 2, tt, :]).then_inc(s_store[tt], 16)
            for tt in range(4):
                sp_.wait_ge(s_store[tt], 16 * CHUNKS)

        @block.gpsimd
        def _(pool):
            nc.gpsimd.memset(xi[:], HID).then_inc(s_xi0, 1)
            identity(nc, pool, ident[:], s_const)
            nc.gpsimd.memset(ones[:], 1.0).then_inc(s_const, 1)
            nc.gpsimd.memset(eps[:], LN_EPS).then_inc(s_const, 1)
            nc.gpsimd.iota(iota_i[:], pattern=[[1, EXPERTS]], base=0, channel_multiplier=0).then_inc(s_const, 1)
            pool.wait_ge(s_const, 5)
            nc.gpsimd.tensor_copy(iota[:], iota_i[:]).then_inc(s_const, 1)
            pool.wait_ge(s_idx, 1)

            def gather(c, tt):
                pool.wait_ge(s_emb_free, c * 4 + (tt + 1))
                nc.gpsimd.tensor_copy(idx_now[:, tt, :], idx[:, c * 2 + 8 * (tt // 2) + tt % 2, :]).then_inc(s_now, 1)
                pool.wait_ge(s_now, c * 4 + (tt + 1))
                for k in range(ORDER):
                    nc.gpsimd.indirect_dma_start(
                        out=emb[:, tt % 2, k, :], out_offset=None, in_=a["tok_W"],
                        in_offset=bass.IndirectOffsetOnAxis(ap=idx_now[:, tt, k:k + 1], axis=0))\
                        .then_inc(s_emb[tt % 2], 16)

            def up_base(c, tt):
                h = H[:, c % 2, tt, :]
                if c == 0 and tt == 0:
                    pool.wait_ge(s_w, 16 * 11)
                pool.wait_ge(s_x, c * 8 + (tt + 1))
                nc.gpsimd.tensor_tensor(h, h, X[:, tt % 2, :], ALU.add).then_inc(s_hx, 1)
                pool.wait_ge(s_hx, c * 4 + (tt + 1))
                nc.gpsimd.tensor_tensor(h, h, up_b[:], ALU.add).then_inc(s_hb, 1)

            for n in range(4 * CHUNKS + 2):
                if n < 4 * CHUNKS:
                    gather(n // 4, n % 4)
                if n >= 2:
                    up_base((n - 2) // 4, (n - 2) % 4)

        @block.tensor
        def _(pe):
            pe.wait_ge(s_const, 2)
            pe.wait_ge(s_xf, 1)
            for k in range(ORDER):
                ins = nc.tensor.transpose(ps[:, 0, 16 * k:16 * k + 16], xf[:, k, :], ident[0:16, 0:16])
            ins.then_inc(s_ixT, 1)
            pe.wait_ge(s_idx, 1)

            def transposes(tt, base):
                pe.wait_ge(s_x, base + tt + 1)
                for h in range(2):
                    for q in range(4):
                        k = 4 * h + q
                        ins = nc.tensor.transpose(ps[:, 2 * tt + h, P * q:P * q + P],
                                                  X[:, tt % 2, P * k:P * k + P], ident[:])
                    ins.then_inc(s_xt, 1)

            def product(out, parts):
                for n, (lhsT, rhs) in enumerate(parts):
                    ins = nc.tensor.matmul(out, lhsT, rhs, start=(n == 0), stop=(n == len(parts) - 1))
                return ins

            def mixture(q, last=False):
                tt, h, bank = group(q, last)
                product(ps[:, bank, :], [(xTb[:, k, P * tt:P * tt + P], w_base[:, k, BANK * h:BANK * h + BANK])
                                         for k in range(KT)]
                        + [(midT[:, tt, :], w_lora_b[:, BANK * h:BANK * h + BANK])]).then_inc(s_base, 1)

            for tt in range(4):
                transposes(tt, 0)
            pe.wait_ge(s_w, 16 * 11)
            pe.wait_ge(s_wdown, 16)
            for c in range(CHUNKS):
                last = c == CHUNKS - 1
                pe.wait_ge(s_xT, c * 16 + 8)
                product(ps[:, 4, :], [(w_down[:, k, :], xTa[:, k, :]) for k in range(KT)]).then_inc(s_down, 1)
                for r in range(2):
                    if r == 0:
                        pe.wait_ge(s_xm, c + 1)
                        u = xm
                    else:
                        pe.wait_ge(s_hout, c * 2 + 1)
                        u = hout[:, 0, :]
                    n = c * 2 + (r + 1)
                    for t in range(2):
                        ins = product(ps[:, 2 + t, :], [(in_x[:, P * t:P * t + P], u[:, :])])
                    ins.then_inc(s_in, 1)
                    product(ps[0:C_ROW0 + DST, 4, :], [(in_bc[:], u[:, :])]).then_inc(s_in, 1)
                    for t in range(2):
                        for d in range(2):
                            ins = product(ps[:, 6 + t, HALF * d:HALF * d + HALF],
                                          [(in_dt[:, d, P * t:P * t + P], u[:, HALF * d:HALF * d + HALF])])
                    ins.then_inc(s_in, 1)
                    if c and r:
                        pe.wait_ge(s_h2, c * 8 - 2)
                    for t in range(2):
                        ins = product(ps[:, t, :], [(in_z[:, P * t:P * t + P], u[:, :])])
                    ins.then_inc(s_in, 1)
                    if c:
                        mixture(4 + 2 * r)
                    pe.wait_ge(s_bcp, n)
                    product(ps[:, 4, :], [(ones[0:DST, :], BC[:])]).then_inc(s_bc, 1)
                    pe.wait_ge(s_xs, n * 2)
                    for t in range(2):
                        ins = product(ps[:, 2 + t, :], [(w_fc[:, k, P * t:P * t + P], xs[:, k, :]) for k in range(2)])
                    ins.then_inc(s_fc, 1)
                    if c:
                        pe.wait_ge(s_zs, n)
                        mixture(5 + 2 * r)
                    pe.wait_ge(s_sq, n)
                    product(ps[:, 4, :], [(ones[:], sq[:, k, :]) for k in range(2)]).then_inc(s_ms, 1)
                    pe.wait_ge(s_yn, n)
                    product(ps[:, 6, :], [(w_out[:, k, :], yz[:, k, :]) for k in range(2)]).then_inc(s_ho, 1)
                if c == 0:
                    pe.wait_ge(s_wbig, 16 * 4)
                pe.wait_ge(s_hmix, c + 1)
                if c:
                    pe.wait_ge(s_h2, c * 8)
                for tt in range(4):
                    for h in range(2):
                        ins = product(ps[:, 2 * tt + h, :], [(hmix[:, P * tt:P * tt + P], w_up[:, BANK * h:BANK * h + BANK])])
                    ins.then_inc(s_up, 1)
                for tt in range(4):
                    transposes(tt, c * 8 + 4)
                for tt in range(4):
                    pe.wait_ge(s_xT, c * 16 + (8 + 2 * tt + 2))
                    product(ps[:, 2 * tt, 0:ER + EXPERTS],
                            [(xTb[:, k, P * tt:P * tt + P], w_lora[:, k, :]) for k in range(KT)]).then_inc(s_rt, 1)
                for tt in range(4):
                    pe.wait_ge(s_mid, c * 4 + (tt + 1))
                    nc.tensor.transpose(ps[:, 2 * tt + 1, 0:P],
                                        mid[:, tt % 2, :, :].rearrange("p e r -> p (e r)"), ident[:]).then_inc(s_midt, 1)
                pe.wait_ge(s_midT, c * 4 + 4)
                if last:
                    for q in range(8):
                        mixture(q, last)
                else:
                    mixture(0)
                    mixture(1)
                    transposes(0, c * 8 + 8)
                    mixture(2)
                    transposes(1, c * 8 + 8)
                    mixture(3)
                    pe.wait_ge(s_h2, c * 8 + 4)
                    transposes(2, c * 8 + 8)
                    transposes(3, c * 8 + 8)

        @block.scalar
        def _(act):
            act.wait_ge(s_const, 4)
            act.wait_ge(s_w, 16 * 11)
            step = Steps(act, s_act)
            step.link(nc.scalar.activation(alpha[:, 0:1], gate, ACT.Sigmoid))
            act.sem_inc(s_alpha, 1)

            def inverse_std(tt, base):
                act.wait_ge(s_var, base + tt + 1)
                step.link(nc.scalar.activation(lnv[:, tt:tt + 1], mv[:, tt, 1:2], ACT.Ln, bias=eps[:]))
                nc.scalar.activation(rstd[:, tt:tt + 1], lnv[:, tt:tt + 1], ACT.Exp, scale=-0.5).then_inc(s_rstd, 1)

            def transposed(tt, base, xT):
                for h in range(2):
                    act.wait_ge(s_xt, base + (2 * tt + h + 1))
                    nc.scalar.activation(xT[:, 4 * h:4 * h + 4, P * tt:P * tt + P],
                                         ps[:, 2 * tt + h, :].rearrange("p (k t) -> p k t", t=P), ACT.Copy)\
                        .then_inc(s_xT, 1)

            def embedded(c):
                inverse_std(0, c * 8)
                for tt in range(1, 4):
                    inverse_std(tt, c * 8)
                    transposed(tt - 1, c * 16, xTa)
                transposed(3, c * 16, xTa)

            nc.scalar.preload_act_table_set(LN_EXP)
            embedded(0)
            for c in range(CHUNKS):
                act.wait_ge(s_down, c + 1)
                nc.scalar.activation(xm[:], ps[:, 4, :], ACT.Gelu, bias=b_down).then_inc(s_xm, 1)
                for r in range(2):
                    n = c * 2 + (r + 1)
                    nc.scalar.preload_act_table(ACT.Silu)
                    for t in range(2):
                        act.wait_ge(s_cv, n * 3 - 3 + (t + 1))
                        nc.scalar.activation(xs[:, t, 0:HALF], ps[:, 2 + t, 0:HALF], ACT.Silu,
                                             scale=conv_x[:, t, TAP_NOW:TAP_NOW + 1], bias=conv_x[:, t, 7:8])
                        nc.scalar.activation(xs[:, t, HALF:BANK], cv[:, t, :], ACT.Silu,
                                             bias=conv_x[:, t, 7:8]).then_inc(s_xs, 1)
                    act.wait_ge(s_cv, n * 3)
                    for r0, dst in ((0, Bs), (C_ROW0, Cs)):
                        r1 = r0 + DST
                        nc.scalar.activation(dst[:, 0:HALF], ps[r0:r1, 4, 0:HALF], ACT.Silu,
                                             scale=conv_bc[r0:r1, TAP_NOW:TAP_NOW + 1], bias=conv_bc[r0:r1, 7:8])
                        nc.scalar.activation(dst[:, HALF:BANK], cvb[r0:r1, :], ACT.Silu,
                                             bias=conv_bc[r0:r1, 7:8]).then_inc(s_bcs, 1)
                    act.wait_ge(s_in, n * 4)
                    nc.scalar.activation(zs[:], ps[:, 0:2, :], ACT.Silu).then_inc(s_zs, 1)
                    nc.scalar.preload_act_table_set(LN_EXP)
                    for t in range(2):
                        step.link(nc.scalar.activation(sp[:, t, :], ps[:, 6 + t, :], ACT.Abs, bias=dt_bias[:, t:t + 1]))
                    step.link(nc.scalar.activation(sp[:], sp[:], ACT.Exp, scale=-1.0))
                    nc.scalar.activation(sp[:], sp[:], ACT.Ln, bias=1.0).then_inc(s_sp, 1)
                    act.wait_ge(s_yz, n)
                    nc.scalar.activation(sq[:], yz[:], ACT.Square).then_inc(s_sq, 1)
                    act.wait_ge(s_ms, n)
                    step.link(nc.scalar.activation(rms, ps[:, 4, :], ACT.Ln, scale=1.0 / DIN, bias=eps[:]))
                    step.link(nc.scalar.activation(rms, rms, ACT.Exp, scale=-0.5))
                    act.sem_inc(s_rms, 1)
                    act.wait_ge(s_ho, n)
                    nc.scalar.activation(hout[:, r, :], ps[:, 6, :], ACT.Copy).then_inc(s_hout, 1)
                for tt in range(4):
                    inverse_std(tt, c * 8 + 4)
                for tt in range(4):
                    transposed(tt, c * 16 + 8, xTb)
                for tt in range(4):
                    act.wait_ge(s_gap, c * 4 + (tt + 1))
                    nc.scalar.activation(r2[:, tt, 1:2], r2[:, tt, 0:1], ACT.Exp).then_inc(s_e2, 1)
                for tt in range(4):
                    act.wait_ge(s_midt, c * 4 + (tt + 1))
                    nc.scalar.activation(midT[:, tt, :], ps[:, 2 * tt + 1, 0:P], ACT.Copy).then_inc(s_midT, 1)
                if c < CHUNKS - 1:
                    embedded(c + 1)

        @block.vector
        def _(dve):
            dve.sem_inc(s_emb_free, 2)
            step = Steps(dve, s_dve)
            tt_, ts_, stt = nc.vector.tensor_tensor, nc.vector.tensor_scalar, nc.vector.scalar_tensor_tensor
            dve.wait_ge(s_xi, 16 * 14)
            for k in range(ORDER):
                ins = ts_(xf[:, k, :], xi[:, k, :], float(k * VOC1), None, ALU.add)
            ins.then_inc(s_xf, 1)
            dve.wait_ge(s_ixT, 1)
            nc.vector.tensor_copy(idx[:].rearrange("p g k -> p k g"),
                                  ps[:, 0, 0:16 * ORDER].rearrange("p (k g) -> p k g", g=16)).then_inc(s_idx, 1)
            dve.wait_ge(s_const, 6)
            dve.wait_ge(s_w, 16 * 11)
            dve.wait_ge(s_alpha, 1)
            step.link(ts_(alpha[:, 1:2], alpha[:, 0:1], -1.0, 1.0, ALU.mult, ALU.add))

            def mean_var(tt, src):
                for h in range(2):
                    ins = nc.vector.bn_stats(stats[:, tt, h, :], src[:, tt, BANK * h:BANK * h + BANK])
                step.link(ins)
                apart(dve, s_apart_dve)
                nc.vector.bn_aggr(mv[:, tt, :], stats[:, tt, :, :]).then_inc(s_var, 1)

            def normalise(tt, base, src):
                if base + tt >= 2:
                    dve.wait_ge(s_xt, 2 * (base + tt - 1))
                dve.wait_ge(s_rstd, base + tt + 1)
                ts_(X[:, tt % 2, :], src[:, tt, :], mv[:, tt, 0:1], rstd[:, tt:tt + 1], ALU.subtract, ALU.mult)\
                    .then_inc(s_x, 1)

            def embed(c, tt):
                h = H[:, c % 2]
                dve.wait_ge(s_emb[tt % 2], c * (2 * ORDER * 16) + (tt // 2 + 1) * ORDER * 16)
                if c >= 2:
                    dve.wait_ge(s_store[tt], 16 * (c - 1))
                step.link(tt_(h[:, tt, :], emb[:, tt % 2, 0, :], tok_b[:], ALU.add))
                for k in range(1, ORDER):
                    step.link(tt_(h[:, tt, :], h[:, tt, :], emb[:, tt % 2, k, :], ALU.add))
                dve.sem_inc(s_emb_free, 1)
                mean_var(tt, h)
                if tt >= 2:
                    dve.wait_ge(s_hb, c * 4 + (tt - 1))
                normalise(tt, c * 8, h)

            def mixed(c, q):
                tt, h, bank = group(q, c == CHUNKS - 1)
                half = H[:, c % 2, tt, BANK * h:BANK * h + BANK]
                dve.wait_ge(s_base, c * 8 + q + 1)
                tt_(half, ps[:, bank, :], half, ALU.add).then_inc(s_h2, 1)

            for tt in range(4):
                embed(0, tt)
            for c in range(CHUNKS):
                h = H[:, c % 2]
                for r in range(2):
                    n = c * 2 + (r + 1)
                    dve.wait_ge(s_in, n * 4 - 3)
                    for t in range(2):
                        ins = ts_(cv[:, t, :], ps[:, 2 + t, 0:HALF], conv_x[:, t, TAP_BEFORE:TAP_BEFORE + 1], None, ALU.mult)
                    step.link(ins)
                    for t in range(2):
                        stt(cv[:, t, :], ps[:, 2 + t, HALF:BANK], conv_x[:, t, TAP_NOW:TAP_NOW + 1], cv[:, t, :],
                            ALU.mult, ALU.add).then_inc(s_cv, 1)
                    dve.wait_ge(s_in, n * 4 - 2)
                    n_bc = C_ROW0 + DST
                    step.link(ts_(cvb[:], ps[0:n_bc, 4, 0:HALF], conv_bc[:, TAP_BEFORE:TAP_BEFORE + 1], None, ALU.mult))
                    stt(cvb[:], ps[0:n_bc, 4, HALF:BANK], conv_bc[:, TAP_NOW:TAP_NOW + 1], cvb[:],
                        ALU.mult, ALU.add).then_inc(s_cv, 1)
                    dve.wait_ge(s_bcs, n * 2)
                    tt_(BC[:], Bs[:], Cs[:], ALU.mult).then_inc(s_bcp, 1)
                    dve.wait_ge(s_sp, n)
                    for t in range(2):
                        ins = ts_(dts[:, t, :], ps[:, 6 + t, :], dt_bias[:, t:t + 1], 0.0, ALU.add, ALU.max)
                    step.link(ins)
                    step.link(tt_(dts[:], dts[:], sp[:], ALU.add))
                    dve.wait_ge(s_xs, n * 2)
                    step.link(tt_(dts[:], dts[:], xs[:], ALU.mult))
                    dve.wait_ge(s_bc, n)
                    for t in range(2):
                        for d in range(2):
                            ins = tt_(yq[:, t, HALF * (1 - d):HALF * (2 - d)], dts[:, t, HALF * d:HALF * d + HALF],
                                      ps[:, 4, HALF * d:HALF * d + HALF], ALU.mult)
                    dve.wait_ge(s_fc, n)
                    for t in range(2):
                        ins = stt(w_fx[:, t, :], ps[:, 2 + t, :], D_col[:, t:t + 1], xs[:, t, :], ALU.add, ALU.mult)
                    step.link(ins)
                    step.link(tt_(yq[:], yq[:], w_fx[:], ALU.add))
                    dve.wait_ge(s_zs, n)
                    tt_(yz[:], yq[:], zs[:], ALU.mult).then_inc(s_yz, 1)
                    if c:
                        mixed(c - 1, 4 + 2 * r)
                        mixed(c - 1, 5 + 2 * r)
                    dve.wait_ge(s_rms, n)
                    dve.wait_ge(s_sq, n)
                    for t in range(2):
                        ins = stt(yz[:, t, :], yz[:, t, :], norm_w[:, t:t + 1], rms, ALU.mult, ALU.mult)
                    ins.then_inc(s_yn, 1)
                dve.wait_ge(s_hout, c * 2 + 2)
                step.link(ts_(hmix, hout[:, 1, :], alpha[:, 1:2], None, ALU.mult))
                step.link(stt(hmix, xm[:], alpha[:, 0:1], hmix, ALU.mult, ALU.add))
                tt_(hmix, hmix, xm[:], ALU.add).then_inc(s_hmix, 1)
                for tt in range(4):
                    dve.wait_ge(s_up, c * 4 + (tt + 1))
                    dve.wait_ge(s_hb, c * 4 + (tt + 1))
                    tile_h = h[:, tt, :].rearrange("p (h n) -> p h n", h=2)
                    tt_(tile_h, ps[:, 2 * tt:2 * tt + 2, :], tile_h, ALU.add).then_inc(s_h1, 1)
                    dve.wait_ge(s_h1, c * 4 + (tt + 1))
                    mean_var(tt, h)
                for tt in range(4):
                    normalise(tt, c * 8 + 4, h)
                for tt in range(4):
                    dve.wait_ge(s_rt, c * 4 + (tt + 1))
                    step.link(nc.vector.tensor_copy(rt[:, tt, :], ps[:, 2 * tt, ER:ER + EXPERTS]))
                    apart(dve, s_apart_dve)
                    step.link(nc.vector.max(top[:, tt, :], rt[:, tt, :]))
                    tt_(r2[:, tt, 0:1], top[:, tt, 1:2], top[:, tt, 0:1], ALU.subtract).then_inc(s_gap, 1)
                    step.link(nc.vector.max_index(topi[:, tt, :], top[:, tt, :], rt[:, tt, :]))
                    nc.vector.tensor_copy(r2[:, tt, 5:7], topi[:, tt, 0:2])
                    dve.wait_ge(s_e2, c * 4 + (tt + 1))
                    step.link(ts_(r2[:, tt, 2:3], r2[:, tt, 1:2], 1.0, None, ALU.add))
                    step.link(nc.vector.reciprocal(r2[:, tt, 3:4], r2[:, tt, 2:3]))
                    step.link(tt_(r2[:, tt, 4:5], r2[:, tt, 1:2], r2[:, tt, 3:4], ALU.mult))
                    for j in range(2):
                        ins = ts_(wd[:, tt % 2, j, :], iota[:], r2[:, tt, 5 + j:6 + j], r2[:, tt, 3 + j:4 + j],
                                  ALU.is_equal, ALU.mult)
                    step.link(ins)
                    step.link(tt_(wd[:, tt % 2, 0, :], wd[:, tt % 2, 0, :], wd[:, tt % 2, 1, :], ALU.add))
                    if tt >= 2:
                        dve.wait_ge(s_midt, c * 4 + (tt - 1))
                    stt(mid[:, tt % 2, :, :], ps[:, 2 * tt, 0:ER].rearrange("p (e r) -> p e r", r=RANK), LORA_SCALE,
                        wd[:, tt % 2, 0, :].unsqueeze(2).to_broadcast([P, EXPERTS, RANK]), ALU.mult, ALU.mult)\
                        .then_inc(s_mid, 1)
                for q in range(8 if c == CHUNKS - 1 else 4):
                    if c < CHUNKS - 1:
                        embed(c + 1, q)
                    mixed(c, q)


I8 = mybir.dt.int8
FR = mybir.dt.float32r
DI = 2048
DT = DI // P
NS = 16
DT_RANK = 64
B_ROW, C_ROW, SSM = 64, 96, 112
TAPS = 4
RMS_EPS = 1e-6
UNITS = TOK // BANK
COLS = TAPS + 3 + NS
CONV_B, DT_B, D_P, A_0 = TAPS, TAPS + 1, TAPS + 2, TAPS + 3
HB, DL, YB, UB, GB = 0, 4, 5, 6, 7
SX = 6
OUT_ORDER = (2, 3, 0, 1)
OVER_H = 24
REP = 5
FOLDED = (0, 2, 4)
CONV_AT = (0, 2, 5, 6)
DELTA_AT = (3, 4)
PROJECT_AT = (0, 4, 8, 10, 12, 14, 16, 16, 16)
ORDER_Y = (1, 0, 3, 2, 5, 4, 6, 7)


def layer1(nc, a, h_dram, y_dram, out):
    with ExitStack() as ctx:
        def sb(name, shape, dt=FP):
            return ctx.enter_context(nc.sbuf_tensor(name, shape, dt))

        def sem(name):
            return ctx.enter_context(nc.semaphore("l1_" + name))

        ident = sb("l1_ident", [P, P])
        identr = sb("l1_identr", [P, P], FR)
        block1 = sb("l1_block1", [SSM, SSM])
        eps5 = sb("l1_eps5", [P, 1])
        eps6 = sb("l1_eps6", [P, 1])
        rlen = sb("l1_rlen", [SSM, 1])
        cols = sb("l1_cols", [P, DT, COLS])
        ln_w = sb("l1_ln_w", [SSM, 1])
        w_dt = sb("l1_w_dt", [DT_RANK, P])
        state = sb("l1_state", [P, DT, NS])
        halo = sb("l1_halo", [P, DT, TAPS - 1])
        ssm = sb("l1_ssm", [SSM, BANK])
        u = sb("l1_u", [P, DT, BANK])
        sg = sb("l1_sg", [P, DT, BANK])
        xT = sb("l1_xT", [P, KT, BANK])
        g_at = -(-nc.sbuf_base // 32) * 32
        g = sb("l1_g", [P, 4, 2, BANK])
        ring = sb("l1_ring", [P, 2, HID])
        s3 = sb("l1_s3", [P, 4, BANK])
        spl = sb("l1_spl", [P, BANK])
        up = sb("l1_up", [P, TAPS - 1 + BANK])
        acc = sb("l1_acc", [P, 2, BANK])
        stats = sb("l1_stats", [P, 8, 2, 6])
        mv = sb("l1_mv", [P, 8, 2])
        lnv = sb("l1_lnv", [P, 8])
        rstd = sb("l1_rstd", [P, 8])
        ps = ctx.enter_context(nc.psum_tensor("l1_ps", [P, 8, BANK], FP))
        slab_at = -(-nc.sbuf_base // 32) * 32
        slab = sb("l1_slab", [P, 20 * HID + 16])

        def at(name, offset, shape, dt=FP, base=slab_at):
            return nc.alloc_sbuf_tensor_at("l1_" + name, shape, dt, offset=base + offset)

        KB = 1024
        rep = at("rep", 0, [P, 2 * NS, BANK])
        dBu = at("dBu", 64 * KB, [P, 2, 4, BANK])
        H = at("H", 48 * KB, [P, 4, HID])
        xh = at("xh", 16 * KB, [P, KT, BANK], FR)
        xl = at("xl", 32 * KB, [P, KT, BANK], FR)
        wr = at("w_out_rows", 16 * KB, [P, 4, HID])
        wh = at("wh", 0, [P, 2, HID], FR)
        wl = at("wl", 8 * KB, [P, 2, HID], FR)
        yr = at("yr", 64 * KB, [P, 2, BANK])
        yh = at("yh", 68 * KB, [P, 2, BANK], FR)
        yl = at("yl", 72 * KB, [P, 2, BANK], FR)
        w_x = at("w_x", 32 * KB, [P, DT, SSM])
        w_x0 = at("w_x0", 64 * KB, [P, DT, SSM])
        raw = at("raw", 72 * KB, [SSM, BANK])
        sqr = at("squares", 74 * KB, [SSM, BANK])
        rr = at("rr", 76 * KB, [SSM, BANK])
        tern = at("tern", 8 * KB, [P, 2, HID], I8, base=g_at)
        sh = at("ssm_high", 0, [SSM, BANK], FR, base=g_at)
        sl = at("ssm_low", 2 * KB, [SSM, BANK], FR, base=g_at)
        srow = g[:, 0:2, :, :].rearrange("p s n t -> p s (n t)")
        Hn = s3[:, :, :].rearrange("p (t h) n -> p t (h n)", h=2)
        delta, du = s3[:, 0:2, :], s3[:, 2:4, :]

        def column(j, n):
            return cols[:, bass.ds(j, 1), n:n + 1].rearrange("p a n -> p (a n)")

        def tile(t, j):
            return t[:, bass.ds(j, 1), :].rearrange("p a n -> p (a n)")

        def slice3(t, j):
            return t[bass.ds(j, 1), :, :].rearrange("a p n -> p (a n)")

        s_const = sem("const")
        s_w = sem("weights")
        s_wx = sem("wx")
        s_hn = [sem(f"hn{n}") for n in range(2)]
        s_hl = sem("hl")
        s_var = sem("var")
        s_rstd = sem("rstd")
        s_x = sem("x")
        s_xt = sem("xt")
        s_xT = sem("xT_s")
        s_xl = sem("xl_s")
        s_winu = sem("win_u")
        s_wing = sem("win_g")
        s_wh = [sem(f"win_high{n}") for n in range(2)]
        s_wl = [sem(f"win_low{n}") for n in range(2)]
        s_pu = sem("pu")
        s_pg = sem("pg")
        s_up = sem("up_in")
        s_edge = sem("edge")
        s_conv = sem("conv")
        s_u = sem("u_s")
        s_sg = sem("sg_s")
        s_ssm = sem("ssm_p")
        s_sqr = sem("sqr")
        s_raw = sem("raw")
        s_ms = sem("ms")
        s_rr = sem("rr")
        s_ssmn = sem("ssmn")
        s_sh = sem("ssm_h")
        s_sl = sem("ssm_l")
        s_bp = sem("bp")
        s_repa = sem("rep_act")
        s_repd = sem("rep_dve")
        s_wdt = sem("wdt")
        s_dl = sem("dl")
        s_spl = sem("spl_s")
        s_delta = sem("delta")
        s_du = sem("du")
        s_dBu = sem("dBu_s")
        s_dA = sem("dA")
        s_scan = sem("scan")
        s_g = sem("g_s")
        s_gs = sem("g_sum")
        s_sum = sem("sum")
        s_yt = sem("yt")
        s_y = sem("y")
        s_ys = sem("ys")
        s_fin = [sem(f"fin{n}") for n in range(2)]
        s_hi = sem("hi")
        s_lo = sem("lo")
        s_po = sem("po")
        s_h3 = sem("h3")
        s_tern = [sem(f"tern{n}") for n in range(2)]
        s_wf = sem("wf")
        s_fh = sem("fh")
        s_fl = sem("fl")
        s_pf = sem("pf")
        s_h4 = sem("h4")
        s_out = sem("out")
        s_act = sem("act_steps")
        s_dve = sem("dve_steps")
    

        block = ctx.enter_context(nc.Block())

        def rows(dram, K, t):
            return dram[K * BANK + t * P:K * BANK + (t + 1) * P, :]

        def norms_before(K):
            return 4 * (min(K + 2, UNITS) + K)

        def tiles(engine, body, first, last):
            for j in range(first):
                body(j, j % 2, j, False)
            with engine.Fori(0, (last - first) // 2) as jj:
                for par in range(2):
                    body(jj * 2 + (first + par), (first + par) % 2, first, False)
            for j in range(last, DT):
                body(j, j % 2, first, j == DT - 1)

        @block.sync
        def _(sp):
            for dst, name in ((cols, "cols"), (ln_w, "ln_w")):
                sp.dma_start(dst[:], a[name]).then_inc(s_w, 16)

            def norm_loads(K, before, tiles_=range(4)):
                for t in tiles_:
                    if t >= 2:
                        sp.wait_ge(s_xt, 2 * (before + t - 1))
                    sp.dma_start(Hn[:, t % 2, :], rows(h_dram, K, t)).then_inc(s_hn[t % 2], 16)

            def w_u(K, i):
                sp.dma_start(ring[:, 0, :], slice3(a["w_in"], i)).then_inc(s_winu, 16)

            def w_g(K, i):
                sp.dma_start(ring[:, 1, :], slice3(a["w_in"], i + DT)).then_inc(s_wing, 16)

            norm_loads(0, 0)
            w_u(0, 0)
            w_g(0, 0)
            with sp.Fori(1, DT) as i:
                sp.wait_ge(s_wl[0], i)
                w_u(0, i)
                sp.wait_ge(s_wl[1], i)
                w_g(0, i)
            sp.wait_ge(s_xt, 8)
            norm_loads(1, 4)
            sp.dma_start(w_x0[:], a["w_x"]).then_inc(s_wx, 16)
            for K in range(UNITS):
                more = K + 1 < UNITS
                if K == 0:
                    sp.dma_start(w_dt[:], a["w_dt"][0, :, :]).then_inc(s_wdt, 16)
                if more:
                    w_u(K + 1, 0)
                    w_g(K + 1, 0)
                sp.wait_ge(s_dl, K * DT + 1)
                sp.dma_start(w_dt[:], a["w_dt"][1, :, :]).then_inc(s_wdt, 16)

                def tile_transfers(j, par, early, last, K=K, more=more):
                    m = K * DT + j
                    if early >= 1:
                        sp.wait_ge(s_y, m)
                        sp.dma_start(slice3(y_dram, m - 1), tile(u, j - 1)).then_inc(s_ys, 16)
                    if last is not True and not (isinstance(j, int) and j >= DT - 2):
                        sp.wait_ge(s_dl, m + 2)
                        sp.dma_start(w_dt[:], slice3(a["w_dt"], j + 2)).then_inc(s_wdt, 16)
                    if more and early >= 1:
                        sp.wait_ge(s_pu, m + DT)
                        w_u(K + 1, j)
                        sp.wait_ge(s_pg, m + DT)
                        w_g(K + 1, j)

                tiles(sp, tile_transfers, 4, 14)
                sp.wait_ge(s_y, K * DT + DT)
                sp.dma_start(slice3(y_dram, K * DT + DT - 1), tile(u, DT - 1)).then_inc(s_ys, 16)
                for j in range(DT):
                    sp.wait_ge(s_ys, 16 * (K * DT + j + 1))
                    if j >= 2:
                        sp.wait_ge(s_lo, K * DT + j - 1)
                    sp.dma_start(yr[:, j % 2, :], y_dram[K * DT + j, :, :]).then_inc(s_fin[j % 2], 16)
                    sp.dma_start(wr[:, j % 4, :], a["w_out"][j, :, :]).then_inc(s_fin[j % 2], 16)
                    if j % 4 == 1:
                        t = j // 4
                        sp.dma_start(H[:, t, :], rows(h_dram, K, t)).then_inc(s_hl, 16)

                def tern_loads(k, K=K):
                    if k >= 2:
                        sp.wait_ge(s_wf, K * KT + k - 1)
                    sp.dma_start(tern[:, k % 2, :].bitcast(I32), a["tern"][k, :, :]).then_inc(s_tern[k % 2], 16)
                    sp.dma_start(srow[:, k % 2, :], a["scales"][k, :].partition_broadcast(P)).then_inc(s_tern[k % 2], 16)

                if more:
                    sp.dma_start(w_x[:], a["w_x"]).then_inc(s_wx, 16)
                    sp.wait_ge(s_dl, (K + 1) * DT)
                    sp.dma_start(w_dt[:], a["w_dt"][0, :, :]).then_inc(s_wdt, 16)
                tern_loads(0)
                tern_loads(1)
                if K + 2 < UNITS:
                    norm_loads(K + 2, norms_before(K), range(2))
                if K + 2 < UNITS:
                    norm_loads(K + 2, norms_before(K), range(2, 4))
                for k in range(2, KT):
                    tern_loads(k)
                for n, t in enumerate(OUT_ORDER):
                    sp.wait_ge(s_h4, K * 4 + n + 1)
                    sp.dma_start(rows(out, K, t), H[:, t, :]).then_inc(s_out, 16)
            sp.wait_ge(s_out, UNITS * 64)

        @block.gpsimd
        def _(pool):
            identity(nc, pool, ident[:], s_const)
            nc.gpsimd.memset(eps5[:], LN_EPS).then_inc(s_const, 1)
            nc.gpsimd.memset(eps6[:], RMS_EPS).then_inc(s_const, 1)
            nc.gpsimd.memset(block1[:], 0.0).then_inc(s_const, 1)
            pool.wait_ge(s_const, 5)
            for r0, r1, n in ((0, DT_RANK, DT_RANK), (B_ROW, C_ROW, NS), (C_ROW, SSM, NS)):
                nc.gpsimd.memset(block1[r0:r1, r0:r1], 1.0).then_inc(s_const, 1)
                nc.gpsimd.memset(rlen[r0:r1, :], 1.0 / n).then_inc(s_const, 1)

            for K in range(UNITS):
                pool.wait_ge(s_sg, K * DT + DT + 1)
                pool.wait_ge(s_u, K * DT + DT + 1)
                pool.wait_ge(s_repa, K * NS + NS // 2)
                pool.wait_ge(s_repd, K * NS + NS // 2)

                def gated(j, K=K):
                    pool.wait_ge(s_yt, K * DT + j + 2)
                    nc.gpsimd.tensor_tensor(tile(u, j), tile(u, j), tile(sg, j), ALU.mult).then_inc(s_y, 1)

                def fold(j, n, K=K):
                    p = FOLDED[n]
                    pool.wait_ge(s_g, (K * DT + j) * 8 + (p + 3))
                    nc.gpsimd.tensor_tensor(g[:, p % 4, 0, :], g[:, p % 4, 0, :], g[:, p % 4, 1, :], ALU.add)\
                        .then_inc(s_gs, 1)

                def states(j, par, early, last, K=K, gated=gated):
                    m = K * DT + j
                    pool.wait_ge(s_delta, m + 1)
                    nc.gpsimd.tensor_tensor(du[:, par, :], delta[:, par, :], tile(u, j), ALU.mult).then_inc(s_du, 1)
                    pool.wait_ge(s_du, m + 1)
                    for q in range(4):
                        if q == 0 and early >= 1:
                            fold(j - 1, 2)
                        if q >= 2:
                            fold(j, q - 2)
                        pool.wait_ge(s_scan, m * NS + (q * 4 + 4))
                        nc.gpsimd.tensor_tensor(dBu[:, q % 2, :, :], du[:, par, :].unsqueeze(1).to_broadcast([P, 4, BANK]),
                                                rep[:, 4 * q:4 * q + 4, :], ALU.mult).then_inc(s_dBu, 1)
                        if q == 1 and early >= 1:
                            gated(j - 1)

                tiles(pool, states, 2, 16)
                fold(DT - 1, 2)
                gated(DT - 1)

        @block.tensor
        def _(pe):
            pe.sem_inc(s_sum, 8)
            pe.wait_ge(s_const, 11)

            def transposes(t, src, x_done):
                pe.wait_ge(s_x, x_done)
                for h in range(2):
                    for q in range(4):
                        k = 4 * h + q
                        ins = nc.tensor.transpose(ps[:, 2 * t + h, P * q:P * q + P],
                                                  src[:, t % 2, P * k:P * k + P], ident[:])
                    ins.then_inc(s_xt, 1)

            def product(out_, parts):
                for n, (lhsT, rhs) in enumerate(parts):
                    ins = nc.tensor.matmul(out_, lhsT, rhs, start=(n == 0), stop=(n == len(parts) - 1))
                return ins

            def project_step(K, i, s):
                m = K * DT + i
                slot, bank, k = (0, UB, s) if s < KT else (1, GB, s - KT)
                if s == 0:
                    pe.wait_ge(s_winu, m * 16 + 16)
                    pe.wait_ge(s_up, m + 1)
                if s == KT:
                    pe.wait_ge(s_wing, m * 16 + 16)
                    pe.wait_ge(s_sg, m + 1)
                ins = nc.tensor.matmul(ps[:, bank, :], ring[:, slot, P * k:P * k + P], xT[:, k, :],
                                       start=(k == 0), stop=(k == KT - 1))
                if k == KT - 1:
                    ins.then_inc((s_pu, s_pg)[slot], 1)

            def dt_product(K, j):
                m = K * DT + j
                pe.wait_ge(s_wdt, m * 16 + 16)
                if not (K == 0 and isinstance(j, int) and j == 0):
                    pe.wait_ge(s_delta, m)
                product(ps[:, DL, :], [(w_dt[:], ssm[0:DT_RANK, :])]).then_inc(s_dl, 1)

            for t in range(4):
                transposes(t, Hn, t + 1)
            pe.wait_ge(s_xl, 8)
            with pe.Fori(0, DT) as i:
                for slot, bank, read, done in ((0, UB, s_up, s_pu), (1, GB, s_sg, s_pg)):
                    pe.wait_ge(s_wl[slot], i + 1)
                    pe.wait_ge(read, i + 1)
                    product(ps[:, bank, :],
                            [(w[:, slot, P * k:P * k + P], x[:, k, :])
                             for k in range(KT) for w, x in ((wh, xh), (wl, xh), (wh, xl))]).then_inc(done, 1)
            for t in range(4):
                transposes(t, Hn, 4 + t + 1)
            pe.wait_ge(s_xT, 16)

            def dt_b_c(K):
                w = w_x if K else w_x0
                pe.wait_ge(s_wx, K * 16 + 16)
                pe.wait_ge(s_u, K * DT + DT + 1)
                product(ps[0:SSM, SX, :], [(w[:, j, :], u[:, j, :]) for j in range(DT)]).then_inc(s_ssm, 1)

            def mean_squares(K):
                pe.wait_ge(s_sqr, K + 1)
                product(ps[0:SSM, SX + 1, :], [(block1[:], sqr[:])]).then_inc(s_ms, 1)

            dt_b_c(0)
            mean_squares(0)
            for K in range(UNITS):
                more = K + 1 < UNITS
                pe.wait_ge(s_sh, K + 1)
                pe.wait_ge(s_sl, K + 1)
                dt_product(K, 0)
                for n in range(2 * NS):
                    if n >= 3:
                        s = s_repa if n % 2 else s_repd
                        pe.wait_ge(s, K * NS + (n - 3) // 2 + 1)
                    row = (B_ROW if n < NS else C_ROW) + n % NS
                    pick = identr[0:SSM, row:row + 1].to_broadcast([SSM, P])
                    product(ps[:, REP + n % 3, :], [(pick, sh[:]), (pick, sl[:])]).then_inc(s_bp, 1)
                pe.wait_ge(s_repa, K * NS + NS)
                pe.wait_ge(s_repd, K * NS + NS)

                def y_sums(j, par, early, last, K=K, more=more):
                    m = K * DT + j
                    for at_, p in enumerate(ORDER_Y):
                        if more and early >= 1:
                            for s in range(PROJECT_AT[at_], PROJECT_AT[at_ + 1]):
                                project_step(K + 1, j - 1, s)
                        if at_ == 0:
                            if not last:
                                dt_product(K, j + 1)
                            pe.wait_ge(s_yt, m + 1)
                        if p in FOLDED:
                            pe.wait_ge(s_gs, m * len(FOLDED) + (FOLDED.index(p) + 1))
                        else:
                            pe.wait_ge(s_g, m * 8 + (p + 3))
                        for n in range(1 if p in FOLDED else 2):
                            ins = nc.tensor.matmul(ps[:, YB, :], ident[:], g[:, p % 4, n, :],
                                                   start=(at_ == 0 and n == 0), stop=(at_ == 7 and n == 1))
                        ins.then_inc(s_sum, 1)

                tiles(pe, y_sums, 2, 14)
                if more:
                    for s in range(2 * KT):
                        project_step(K + 1, DT - 1, s)
                pe.wait_ge(s_yt, K * DT + DT + 1)
                if more:
                    pe.wait_ge(s_up, (K + 2) * DT + 1)
                    pe.wait_ge(s_sg, (K + 2) * DT + 1)

                def split_products(parts, w, first, last):
                    for t in range(4):
                        xh_, xl_ = parts(t)
                        for n, (l, r) in enumerate(((xh_, 0), (xh_, 1), (xl_, 0))):
                            for h in range(2):
                                ins = nc.tensor.matmul(ps[:, 2 * t + h, :], l, w[r][:, BANK * h:BANK * h + BANK],
                                                       start=(first and n == 0), stop=(last and n == 2))
                    return ins

                for j in range(DT):
                    pe.wait_ge(s_lo, K * DT + j + 1)
                    split_products(lambda t: (yh[:, j % 2, P * t:P * t + P], yl[:, j % 2, P * t:P * t + P]),
                                   (wh[:, j % 2, :], wl[:, j % 2, :]), j == 0, j == DT - 1).then_inc(s_po, 1)
                if more:
                    pe.wait_ge(s_h3, K * 4 + 1)
                    dt_b_c(K + 1)
                pe.wait_ge(s_h3, K * 4 + 4)
                x0 = norms_before(K)
                if K + 2 < UNITS:
                    for t in range(4):
                        if t == 2:
                            mean_squares(K + 1)
                        if t == 3:
                            pe.wait_ge(s_raw, K + 2)
                            pe.wait_ge(s_rr, K + 2)
                        transposes(t, Hn, x0 + t + 1)
                    pe.wait_ge(s_xT, 2 * x0 + 8)
                    x0 += 4
                elif more:
                    mean_squares(K + 1)
                    pe.wait_ge(s_raw, K + 2)
                    pe.wait_ge(s_rr, K + 2)
                for t in range(4):
                    transposes(t, ring, x0 + t + 1)
                pe.wait_ge(s_xl, 8 * (K + 2))
                for k in range(KT):
                    pe.wait_ge(s_fl, K * KT + k + 1)
                    split_products(lambda t: (xh[:, k, P * t:P * t + P], xl[:, k, P * t:P * t + P]),
                                   (wh[:, k % 2, :], wl[:, k % 2, :]), k == 0, k == KT - 1).then_inc(s_pf, 1)
                pe.wait_ge(s_h4, K * 4 + (2 if more else 4))

        @block.scalar
        def _(act):
            act.wait_ge(s_const, 11)
            act.wait_ge(s_w, 16 * 2)
            act.sem_inc(s_up, 1)
            act.sem_inc(s_sg, 1)
            act.sem_inc(s_u, 1)
            step = Steps(act, s_act)
            nc.scalar.activation(identr[:], ident[:], ACT.Copy)

            def inverse_std(t, done):
                act.wait_ge(s_var, done)
                step.link(nc.scalar.activation(lnv[:, t:t + 1], mv[:, t, 1:2], ACT.Ln, bias=eps5[:]))
                nc.scalar.activation(rstd[:, t:t + 1], lnv[:, t:t + 1], ACT.Exp, scale=-0.5).then_inc(s_rstd, 1)

            def transposed(t, dst, done):
                for h in range(2):
                    act.wait_ge(s_xt, done + 2 * t + h + 1)
                    nc.scalar.activation(dst[:, 4 * h:4 * h + 4, P * t:P * t + P],
                                         ps[:, 2 * t + h, :].rearrange("p (k t) -> p k t", t=P), ACT.Copy)\
                        .then_inc(s_xT, 1)

            def softplus(K, j, part):
                if part == 0:
                    act.wait_ge(s_dl, K * DT + j + 1)
                    step.link(nc.scalar.activation(spl[:], ps[:, DL, :], ACT.Abs, bias=column(j, DT_B)))
                elif part == 1:
                    step.link(nc.scalar.activation(spl[:], spl[:], ACT.Exp, scale=-1.0))
                else:
                    nc.scalar.activation(spl[:], spl[:], ACT.Ln, bias=1.0).then_inc(s_spl, 1)

            def take_u(K, i):
                m = K * DT + i
                act.wait_ge(s_pu, m + 1)
                act.wait_ge(s_edge, m + 1)
                nc.scalar.activation(up[:, TAPS - 1:], ps[:, UB, :], ACT.Copy).then_inc(s_up, 1)

            def silu_gate(K, i):
                m = K * DT + i
                act.wait_ge(s_pg, m + 1)
                if K:
                    act.wait_ge(s_y, m - DT + 1)
                nc.scalar.activation(tile(sg, i), ps[:, GB, :], ACT.Silu).then_inc(s_sg, 1)

            def silu_u(K, i):
                m = K * DT + i
                act.wait_ge(s_conv, m + 1)
                if K:
                    act.wait_ge(s_ys, (m - DT + 1) * 16)
                nc.scalar.activation(tile(u, i), acc[:, 0, :], ACT.Silu, bias=column(i, CONV_B)).then_inc(s_u, 1)

            nc.scalar.preload_act_table_set(LN_EXP)
            for t in range(4):
                inverse_std(t, t + 1)
                transposed(t, xh, 0)

            def high_weights(i, slot):
                act.wait_ge((s_winu, s_wing)[slot], 16 * i + 16)
                nc.scalar.activation(wh[:, slot, :], ring[:, slot, :], ACT.Copy).then_inc(s_wh[slot], 1)

            def project_0(i, more):
                take_u(0, i)
                if more:
                    high_weights(i + 1, 0)
                silu_gate(0, i)
                if more:
                    high_weights(i + 1, 1)
                silu_u(0, i)

            high_weights(0, 0)
            high_weights(0, 1)
            nc.scalar.preload_act_table(ACT.Silu)
            with act.Fori(0, DT - 1) as i:
                project_0(i, True)
            project_0(DT - 1, False)
            nc.scalar.preload_act_table_set(LN_EXP)
            for t in range(4):
                inverse_std(t, 4 + t + 1)
                transposed(t, xT, 8)

            def inverse_rms(K):
                act.wait_ge(s_ssm, K + 1)
                nc.scalar.activation(sqr[:], ps[0:SSM, SX, :], ACT.Square).then_inc(s_sqr, 1)
                act.wait_ge(s_ms, K + 1)
                step.link(nc.scalar.activation(rr[:], ps[0:SSM, SX + 1, :], ACT.Ln, scale=rlen[:], bias=eps6[0:SSM, :]))
                nc.scalar.activation(rr[:], rr[:], ACT.Exp, scale=-0.5).then_inc(s_rr, 1)

            inverse_rms(0)
            for K in range(UNITS):
                more = K + 1 < UNITS
                act.wait_ge(s_ssmn, K + 1)
                if K:
                    act.wait_ge(s_fl, K * KT)
                nc.scalar.activation(sh[:], ssm[:], ACT.Copy).then_inc(s_sh, 1)
                for part in range(3):
                    softplus(K, 0, part)
                for n in range(0, 2 * NS, 2):
                    act.wait_ge(s_bp, K * 2 * NS + n + 1)
                    if K and n == OVER_H:
                        act.wait_ge(s_out, K * 64)
                    nc.scalar.activation(rep[:, n, :], ps[:, REP + n % 3, :], ACT.Copy).then_inc(s_repa, 1)

                def decays(j, par, early, last, K=K, more=more):
                    m = K * DT + j
                    act.wait_ge(s_delta, m + 1)
                    for n in range(NS):
                        if n % 2 == 0:
                            act.wait_ge(s_g, m * 8 + (n // 2 + 1))
                        nc.scalar.activation(ps[:, HB + n % 4, :], delta[:, par, :], ACT.Exp, scale=column(j, A_0 + n))\
                            .then_inc(s_dA, 1)
                        if n == 3 and more and early >= 2:
                            if early >= 3:
                                silu_u(K + 1, j - 3)
                            silu_gate(K + 1, j - 2)
                            nc.scalar.preload_act_table_set(LN_EXP)
                        if 4 <= n < 7 and not last:
                            softplus(K, j + 1, n - 4)
                        if n == 13 and more and early >= 1:
                            take_u(K + 1, j - 1)

                for j in range(4):
                    decays(j, j % 2, j, False)
                at_, pairs = step.at, 5
                with act.Fori(0, pairs) as jj:
                    step.reg = jj * 4
                    for par in range(2):
                        decays(jj * 2 + (4 + par), par, 4, False)
                assert step.at == at_ + 4
                step.reg, step.at = None, at_ + 4 * pairs
                decays(DT - 2, 0, 4, False)
                decays(DT - 1, 1, 4, True)

                def high(j, K=K):
                    act.wait_ge(s_fin[j % 2], K * 256 + (j // 2) * 32 + 32)
                    if j >= 2:
                        act.wait_ge(s_po, K * DT + j - 1)
                    elif K:
                        act.wait_ge(s_pf, K * KT)
                    nc.scalar.activation(yh[:, j % 2, :], yr[:, j % 2, :], ACT.Copy)
                    nc.scalar.activation(wh[:, j % 2, :], wr[:, j % 4, :], ACT.Copy).then_inc(s_hi, 1)

                if more:
                    silu_u(K + 1, DT - 3)
                    silu_gate(K + 1, DT - 2)
                    take_u(K + 1, DT - 1)
                    silu_u(K + 1, DT - 2)
                high(0)
                high(1)
                if more:
                    silu_gate(K + 1, DT - 1)
                    silu_u(K + 1, DT - 1)
                nc.scalar.preload_act_table_set(LN_EXP)
                for j in range(2, DT):
                    high(j)
                v0 = norms_before(K)
                x0 = 2 * v0
                if K + 2 < UNITS:
                    for t in range(2):
                        inverse_std(t, v0 + t + 1)
                    v0 += 2
                for t in range(4):
                    inverse_std(4 + t, v0 + t + 1)
                if more:
                    inverse_rms(K + 1)
                if K + 2 < UNITS:
                    for t in range(2, 4):
                        inverse_std(t, v0 + 4 + t - 1)
                    for t in range(4):
                        transposed(t, xT, x0)
                    x0 += 8
                for t in range(4):
                    transposed(t, xh, x0)
                for k in range(KT):
                    act.wait_ge(s_wf, K * KT + k + 1)
                    if k >= 2:
                        act.wait_ge(s_pf, K * KT + k - 1)
                    nc.scalar.activation(wh[:, k % 2, :], ring[:, k % 2, :], ACT.Copy).then_inc(s_fh, 1)

        @block.vector
        def _(dve):
            dve.sem_inc(s_scan, 8)
            dve.sem_inc(s_g, 2)
            dve.sem_inc(s_yt, 1)
            dve.wait_ge(s_const, 11)
            dve.wait_ge(s_w, 16 * 2)
            step = Steps(dve, s_dve)
            tt_, ts_, stt = nc.vector.tensor_tensor, nc.vector.tensor_scalar, nc.vector.scalar_tensor_tensor

            def mean_var(t, src):
                for h in range(2):
                    ins = nc.vector.bn_stats(stats[:, t, h, :], src[:, BANK * h:BANK * h + BANK])
                step.link(ins)
                nc.vector.bn_aggr(mv[:, t, :], stats[:, t, :, :]).then_inc(s_var, 1)

            def project_norm(K, v0, tiles_=range(4)):
                for t in tiles_:
                    dve.wait_ge(s_hn[t % 2], K * 32 + (t // 2) * 16 + 16)
                    mean_var(t, Hn[:, t % 2, :])
                    dve.wait_ge(s_rstd, v0 + t + 1)
                    ts_(Hn[:, t % 2, :], Hn[:, t % 2, :], mv[:, t, 0:1], rstd[:, t:t + 1], ALU.subtract, ALU.mult)\
                        .then_inc(s_x, 1)

            def normalise_dt_b_c(K):
                dve.wait_ge(s_sqr, K + 1)
                ts_(raw[:], ps[0:SSM, SX, :], ln_w[:], None, ALU.mult).then_inc(s_raw, 1)
                dve.wait_ge(s_raw, K + 1)
                dve.wait_ge(s_rr, K + 1)
                tt_(ssm[:], raw[:], rr[:], ALU.mult).then_inc(s_ssmn, 1)

            def edge(K, i):
                if K % 2:
                    nc.vector.tensor_copy(up[:, 0:TAPS - 1], tile(halo, i)).then_inc(s_edge, 1)
                else:
                    nc.vector.memset(up[:, 0:TAPS - 1], 0.0).then_inc(s_edge, 1)

            def conv(K, i, part, last=False):
                m = K * DT + i
                if part == 0:
                    dve.wait_ge(s_up, m + 2)
                    dve.wait_ge(s_edge, m + 1)
                    step.mark(ts_(acc[:, 1, :], up[:, 0:BANK], column(i, 0), None, ALU.mult))
                elif part < TAPS - 1:
                    step.wait()
                    step.mark(stt(acc[:, 1, :], up[:, part:part + BANK], column(i, part), acc[:, 1, :], ALU.mult, ALU.add))
                else:
                    if K % 2 == 0:
                        nc.vector.tensor_copy(tile(halo, i), up[:, BANK:BANK + TAPS - 1])
                    step.wait()
                    dve.wait_ge(s_u, m + 1)
                    stt(acc[:, 0, :], up[:, 3:3 + BANK], column(i, 3), acc[:, 1, :], ALU.mult, ALU.add).then_inc(s_conv, 1)
                    if not last:
                        edge(K, i + 1)

            def make_delta(K, j, par, part):
                m = K * DT + j
                if part == 0:
                    dve.wait_ge(s_spl, m + 1)
                    step.mark(ts_(delta[:, par, :], ps[:, DL, :], column(j, DT_B), 0.0, ALU.add, ALU.max))
                else:
                    step.wait()
                    tt_(delta[:, par, :], delta[:, par, :], spl[:], ALU.add).then_inc(s_delta, 1)

            def finish_y(K, j):
                m = K * DT + j
                dve.wait_ge(s_sum, m * 8 + 16)
                stt(tile(u, j), tile(u, j), column(j, D_P), ps[:, YB, :], ALU.mult, ALU.add).then_inc(s_yt, 1)

            def low(dst, src, high, sem_):
                tt_(dst, src, high.bitcast(FP), ALU.subtract).then_inc(sem_, 1)

            def low_ssm(K):
                dve.wait_ge(s_sh, K + 1)
                low(sl[:], ssm[:], sh[:], s_sl)

            def low_tiles(x0, ts=range(4)):
                for t in ts:
                    for h in range(2):
                        dve.wait_ge(s_xT, x0 + 2 * t + h + 1)
                        part = lambda x: x[:, 4 * h:4 * h + 4, P * t:P * t + P]
                        low(part(xl), ps[:, 2 * t + h, :].rearrange("p (k t) -> p k t", t=P), part(xh), s_xl)

            def low_weights(i, slot):
                dve.wait_ge(s_wh[slot], i + 1)
                low(wl[:, slot, :], ring[:, slot, :], wh[:, slot, :], s_wl[slot])

            project_norm(0, 0)
            low_weights(0, 0)
            low_weights(0, 1)
            low_tiles(0)
            edge(0, 0)
            at_, per = step.at, TAPS - 1
            with dve.Fori(0, DT - 1) as i:
                step.reg = i * per
                low_weights(i + 1, 0)
                for part in range(TAPS):
                    conv(0, i, part)
                low_weights(i + 1, 1)
            step.reg, step.at = None, at_ + per * (DT - 1)
            for part in range(TAPS):
                conv(0, DT - 1, part, last=True)
            project_norm(1, 4)
            normalise_dt_b_c(0)
            for K in range(UNITS):
                more = K + 1 < UNITS
                hf = K % 2
                if K == 0:
                    low_ssm(0)
                make_delta(K, 0, 0, 0)
                make_delta(K, 0, 0, 1)
                for n in range(1, 2 * NS, 2):
                    dve.wait_ge(s_bp, K * 2 * NS + n + 1)
                    if K and n == OVER_H + 1:
                        dve.wait_ge(s_out, K * 64)
                    nc.vector.tensor_copy(rep[:, n, :], ps[:, REP + n % 3, :]).then_inc(s_repd, 1)
                dve.wait_ge(s_repa, K * NS + NS)
                if more:
                    edge(K + 1, 0)

                def scan_tile(j, par, early, last, K=K, more=more, hf=hf):
                    m = K * DT + j

                    def scan(n):
                        dve.wait_ge(s_dA, m * NS + (n + 1))
                        if n % 4 == 0:
                            dve.wait_ge(s_dBu, m * 4 + (n // 4 + 1))
                        init = state[:, bass.ds(j, 1), n:n + 1].rearrange("p a n -> p (a n)") if hf else 0.0
                        nc.vector.tensor_tensor_scan(ps[:, HB + n % 4, :], ps[:, HB + n % 4, :],
                                                     dBu[:, (n // 4) % 2, n % 4, :], init, ALU.mult, ALU.add)\
                            .then_inc(s_scan, 1)

                    for p in range(8):
                        scan(2 * p)
                        scan(2 * p + 1)
                        if p == 1 and early >= 1:
                            finish_y(K, j - 1)
                        if p in CONV_AT and more and early >= 2:
                            conv(K + 1, j - 2, CONV_AT.index(p))
                        if p in DELTA_AT and not last:
                            make_delta(K, j + 1, 1 - par, DELTA_AT.index(p))
                        dve.wait_ge(s_sum, m * 8 + (ORDER_Y.index((p + 4) % 8) + 1 + (8 if p >= 4 else 0)))
                        dve.wait_ge(s_scan, m * NS + (2 * p + 2 + 8))
                        h2 = ps[:, HB + 2 * (p % 2):HB + 2 * (p % 2) + 2, :]
                        if hf == 0:
                            nc.vector.tensor_copy(state[:, bass.ds(j, 1), 2 * p:2 * p + 2],
                                                  h2[:, :, BANK - 1:BANK].rearrange("p n a -> p a n"))
                        tt_(g[:, p % 4, :, :], h2, rep[:, NS + 2 * p:NS + 2 * p + 2, :], ALU.mult).then_inc(s_g, 1)
                for j in range(4):
                    scan_tile(j, j % 2, j, False)
                at_, pairs = step.at, 5
                per = 2 * (1 + (TAPS - 1 if more else 0))
                with dve.Fori(0, pairs) as jj:
                    step.reg = jj * per
                    for par in range(2):
                        scan_tile(jj * 2 + (4 + par), par, 4, False)
                assert step.at == at_ + per, (step.at - at_, per)
                step.reg, step.at = None, at_ + per * pairs
                scan_tile(DT - 2, 0, 4, False)
                scan_tile(DT - 1, 1, 4, True)
                finish_y(K, DT - 1)
                if more:
                    for i in (DT - 2, DT - 1):
                        for part in range(TAPS):
                            conv(K + 1, i, part, last=(i == DT - 1))
                for j in range(DT):
                    if j >= 2:
                        dve.wait_ge(s_po, K * DT + j - 1)
                    dve.wait_ge(s_hi, K * DT + j + 1)
                    tt_(yl[:, j % 2, :], yr[:, j % 2, :], yh[:, j % 2, :].bitcast(FP), ALU.subtract)
                    low(wl[:, j % 2, :], wr[:, j % 4, :], wh[:, j % 2, :], s_lo)
                dve.wait_ge(s_po, K * DT + DT)
                dve.wait_ge(s_hl, K * 64 + 64)
                for t in (3, 0, 1, 2):
                    Ht = H[:, t, :].rearrange("p (h n) -> p h n", h=2)
                    tt_(Ht, ps[:, 2 * t:2 * t + 2, :], Ht, ALU.add).then_inc(s_h3, 1)
                v0 = norms_before(K)
                x0 = 2 * v0
                if K + 2 < UNITS:
                    project_norm(K + 2, v0, range(2))
                    v0, x0 = v0 + 2, x0 + 8
                dve.wait_ge(s_h3, K * 4 + 4)
                for t in range(4):
                    mean_var(4 + t, H[:, t, :])
                if more:
                    normalise_dt_b_c(K + 1)
                if K + 2 < UNITS:
                    project_norm(K + 2, v0 + 2, range(2, 4))
                for t in range(4):
                    if t >= 2:
                        low_tiles(x0, (t - 2,))
                        dve.wait_ge(s_xt, x0 + 2 * t - 2)
                    dve.wait_ge(s_rstd, v0 + t + 1)
                    ts_(ring[:, t % 2, :], H[:, t, :], mv[:, 4 + t, 0:1], rstd[:, 4 + t:5 + t], ALU.subtract, ALU.mult)\
                        .then_inc(s_x, 1)
                low_tiles(x0, (2, 3))
                for k in range(KT):
                    dve.wait_ge(s_tern[k % 2], K * 128 + (k // 2) * 32 + 32)
                    if k >= 2:
                        dve.wait_ge(s_fl, K * KT + k - 1)
                    tt_(ring[:, k % 2, :], tern[:, k % 2, :], srow[:, k % 2, :], ALU.mult).then_inc(s_wf, 1)
                    dve.wait_ge(s_fh, K * KT + k + 1)
                    if k >= 2:
                        dve.wait_ge(s_pf, K * KT + k - 1)
                    low(wl[:, k % 2, :], ring[:, k % 2, :], wh[:, k % 2, :], s_fl)
                if more:
                    low_ssm(K + 1)
                dve.wait_ge(s_pf, K * KT + KT)
                for t in OUT_ORDER:
                    Ht = H[:, t, :].rearrange("p (h n) -> p h n", h=2)
                    tt_(Ht, ps[:, 2 * t:2 * t + 2, :], Ht, ALU.add).then_inc(s_h4, 1)


def layouts(x, L0_tok_W, L0_tok_b, L0_attn_w_down, L0_attn_b_down, L0_attn_w_up, L0_attn_b_up, L0_attn_gate1,
            L0_attn_hy_in_w, L0_attn_hy_conv_w, L0_attn_hy_conv_b, L0_attn_hy_dt_bias, L0_attn_hy_D,
            L0_attn_hy_fcD_w, L0_attn_hy_norm_w, L0_attn_hy_out_w, L0_ffn_base_W, L0_ffn_router_W,
            L0_ffn_lora_A, L0_ffn_lora_B, **rest):
    import numpy as np

    P, DIN, DST, HD = 128, 256, 16, 64

    def k_tiles(w_t):
        return w_t.reshape(-1, P, w_t.shape[1]).transpose(1, 0, 2)

    def channels(v):
        return v.reshape((-1, P) + v.shape[1:]).swapaxes(0, 1)

    o = {}
    o["x"] = x
    o["tok_W"] = L0_tok_W.T
    o["tok_b"] = L0_tok_b
    o["up_b"] = L0_attn_b_up
    o["w_down"] = k_tiles(L0_attn_w_down.T)
    o["w_up"] = L0_attn_w_up.T
    o["w_base"] = k_tiles(L0_ffn_base_W.T)
    lora_a = L0_ffn_lora_A.transpose(1, 0, 2).reshape(1024, 128)
    o["w_lora"] = k_tiles(np.concatenate([lora_a, L0_ffn_router_W.T], axis=1))
    o["w_lora_b"] = L0_ffn_lora_B.reshape(128, 1024)
    w = L0_attn_hy_in_w
    o["in_z"] = w[0:DIN].T
    o["in_x"] = w[DIN:2 * DIN].T
    def apart(v):
        return np.concatenate([v[:DST], np.zeros_like(v[:DST]), v[DST:]])

    o["in_bc"] = apart(w[2 * DIN:2 * DIN + 2 * DST]).T
    dt = w[2 * DIN + 2 * DST:].reshape(2, 4, P)
    o["in_dt"] = np.repeat(dt, HD, axis=1).transpose(2, 0, 1)
    o["w_fc"] = k_tiles(np.repeat(L0_attn_hy_fcD_w, HD, axis=0).T)
    o["w_hout"] = k_tiles(L0_attn_hy_out_w.T)
    o["col"] = np.concatenate(
        [L0_attn_b_down.reshape(P, 1), np.full((P, 1), L0_attn_gate1),
         channels(np.repeat(L0_attn_hy_dt_bias, HD)), channels(np.repeat(L0_attn_hy_D, HD)),
         channels(L0_attn_hy_norm_w)], axis=1).astype(L0_attn_b_down.dtype)
    conv = np.concatenate([L0_attn_hy_conv_w[:, 0, :], L0_attn_hy_conv_b[:, None]], axis=1)
    o["conv_x"] = channels(conv[:DIN])
    o["conv_bc"] = apart(conv[DIN:])
    return o


def layouts1(L1_attn_W_in, L1_attn_conv_w, L1_attn_conv_b, L1_attn_Wx, L1_attn_dt_ln_w, L1_attn_b_ln_w,
             L1_attn_c_ln_w, L1_attn_Wdt, L1_attn_dt_bias, L1_attn_A, L1_attn_D_param, L1_attn_W_out,
             L1_ffn_ternary, L1_ffn_scales, **rest):
    import numpy as np

    P, DI, NS, RANK = 128, 2048, 16, 64
    f = L1_attn_W_in.dtype

    def channels(v):
        return v.reshape(-1, P, v.shape[1]).swapaxes(0, 1)

    def rows_padded(w):
        return np.concatenate([w[:RANK + NS], np.zeros((NS,) + w.shape[1:], f), w[RANK + NS:]], axis=0)

    o = {}
    o["w_in"] = L1_attn_W_in.reshape(2 * DI // P, P, 8, P).transpose(0, 3, 2, 1).reshape(2 * DI // P, P, 1024)
    o["w_x"] = rows_padded(L1_attn_Wx).T.reshape(DI // P, P, 112).swapaxes(0, 1)
    o["ln_w"] = rows_padded(np.concatenate([L1_attn_dt_ln_w, L1_attn_b_ln_w, L1_attn_c_ln_w])[:, None])
    o["w_dt"] = L1_attn_Wdt.reshape(DI // P, P, RANK).swapaxes(1, 2)
    o["cols"] = channels(np.concatenate([L1_attn_conv_w, L1_attn_conv_b[:, None], L1_attn_dt_bias[:, None],
                                         L1_attn_D_param[:, None], L1_attn_A], axis=1))
    o["w_out"] = L1_attn_W_out.T.reshape(DI // P, P, 1024)
    o["tern"] = np.ascontiguousarray(L1_ffn_ternary.T).view(np.int32).reshape(8, P, 256)
    o["scales"] = L1_ffn_scales.reshape(1024, 8).T
    return o


def tower(nc, a, out):
    h_dram = nc.dram_tensor("residual", (TOK, HID), FP).ap()
    layer0(nc, a, h_dram)
    y_dram = nc.dram_tensor("gated_y", (UNITS * DT, P, BANK), FP).ap()
    layer1(nc, a, h_dram, y_dram, out)


def kernel(**inputs):
    import numpy as np
    import concourse.bacc as bacc
    from concourse.bass_utils import run_bass_kernel_spmd

    inputs = {name: np.asarray(v) for name, v in inputs.items()}
    arrays = {name: np.ascontiguousarray(v) for name, v in {**layouts(**inputs), **layouts1(**inputs)}.items()}
    nc = bacc.Bacc("TRN2", target_bir_lowering=False, num_devices=1)
    a = {name: nc.dram_tensor(f"in_{name}", v.shape, mybir.dt.from_np(v.dtype), kind="ExternalInput").ap()
         for name, v in arrays.items()}
    out = nc.dram_tensor("out", (TOK, HID), FP, kind="ExternalOutput").ap()
    tower(nc, a, out)
    got = run_bass_kernel_spmd(nc, [{f"in_{name}": v for name, v in arrays.items()}], core_ids=[0])
    return got.results[0]["out"].reshape(2, ROW, HID)
```
